# Optimizing a Trainium2 kernel written in Bass

```python
import numpy as np
import jax
import jax.numpy as jnp

def _softmax(x, axis=-1):
    return jax.nn.softmax(x, axis=axis)

def _gelu(x):
    return jax.nn.gelu(x, approximate=True)

def _silu(x):
    return jax.nn.silu(x)

def _sigmoid(x):
    return jax.nn.sigmoid(x)

def _layernorm(x, axis=-1, eps=1e-05):
    m = jnp.mean(x, axis=axis, keepdims=True)
    v = jnp.var(x, axis=axis, keepdims=True)
    return (x - m) / jnp.sqrt(v + eps)

def _scatter_add(tgt, idx, src, axis=0):
    return tgt.at[idx].add(src)

def _segment_sum(src, seg, n):
    return jax.ops.segment_sum(src, seg, n)
kernel_name = 'mk_decoder_preln_d2_seqx_r8_8f3ab1'

def setup_inputs(seed: int=0):
    np.random.seed(seed)
    _w = jnp.asarray

    def _rec_inputs():
        import jax
        import jax.numpy as jnp
        _rk = jax.random.key(seed)
        x = 0.002226 + 0.9996 * jax.random.normal(jax.random.fold_in(_rk, 1), (32, 128, 128), jnp.float32)
        _lenS = 128 - jax.random.randint(jax.random.fold_in(_rk, 7), (32,), 0, max(1, 128 // 4) + 1, jnp.int32)
        _lenS2 = 77 - jax.random.randint(jax.random.fold_in(_rk, 8), (32,), 0, max(1, 77 // 4) + 1, jnp.int32)
        _ctx_1024P = jax.random.normal(jax.random.fold_in(_rk, 11), (32, 16, 128), jnp.float32)
        _ctx_1024c = jax.random.dirichlet(jax.random.fold_in(_rk, 511), 0.3 * jnp.ones((16,), jnp.float32), (32, 77))
        _ctx_1024t = jnp.einsum('bsk,bkd->bsd', _ctx_1024c, _ctx_1024P)
        _ctx_1024t = _ctx_1024t * jax.lax.rsqrt(jnp.mean(jnp.square(_ctx_1024t)) + 1e-12) * 0.953939
        ctx_1024 = -0.000125008 + 0.999885 * (_ctx_1024t + 0.3 * jax.random.normal(jax.random.fold_in(_rk, 611), (32, 77, 128), jnp.float32))
        return (x, ctx_1024)
    x, ctx_1024 = _rec_inputs()

    def _L0_attn_setup():
        import jax, jax.numpy as jnp
        import numpy as np
        N_HEADS = 16

        def _alibi_causal_mask(T, n_heads, dtype):
            slopes = (1.0 / jnp.power(2.0, jnp.arange(1, n_heads + 1, dtype=dtype)))[:, None, None]
            idx = jnp.arange(T)
            rel = (idx[None, :] - idx[:, None]).astype(dtype)
            alibi = jnp.tril(rel)
            causal = jnp.where(idx[None, :] > idx[:, None], -jnp.inf, 0.0).astype(dtype)
            return (alibi + causal)[None, :, :] * slopes
        key = jax.random.key(seed)
        ks = jax.random.split(key, 5)
        B, T, C = (2, 256, 128)
        scale = 0.02
        return {'x': jax.random.normal(ks[0], (B, T, C), dtype=jnp.float32), 'W_attn': jax.random.normal(ks[1], (C, 3 * C), dtype=jnp.float32) * scale, 'b_attn': jax.random.normal(ks[2], (3 * C,), dtype=jnp.float32) * scale, 'W_proj': jax.random.normal(ks[3], (C, C), dtype=jnp.float32) * scale, 'b_proj': jax.random.normal(ks[4], (C,), dtype=jnp.float32) * scale}
    _L0_attn_all = _L0_attn_setup()
    _L0_attn_in = {k: v for k, v in _L0_attn_all.items() if k in ('W_attn', 'b_attn', 'W_proj', 'b_proj')}
    del _L0_attn_all

    def _L0_xattn_setup():
        import jax, jax.numpy as jnp
        import numpy as np
        DIM = 128
        HEADS = 16
        DIM_HEAD = 64
        INNER = HEADS * DIM_HEAD
        EPS = 1e-05

        def _layernorm(t, w, b):
            mu = jnp.mean(t, axis=-1, keepdims=True)
            var = jnp.mean(jnp.square(t - mu), axis=-1, keepdims=True)
            return (t - mu) * jax.lax.rsqrt(var + EPS) * w + b
        key = jax.random.key(seed)
        ks = jax.random.split(key, 8)
        b, n, l = (8, 512, 64)
        x = jax.random.normal(ks[0], (b, n, DIM), dtype=jnp.float32)
        latents = jax.random.normal(ks[1], (b, l, DIM), dtype=jnp.float32)
        ln1_w = jnp.ones((DIM,), jnp.float32)
        ln1_b = jnp.zeros((DIM,), jnp.float32)
        ln2_w = jnp.ones((DIM,), jnp.float32)
        ln2_b = jnp.zeros((DIM,), jnp.float32)
        Wq = jax.random.normal(ks[2], (DIM, INNER), dtype=jnp.float32) / np.sqrt(DIM)
        Wkv = jax.random.normal(ks[3], (DIM, 2 * INNER), dtype=jnp.float32) / np.sqrt(DIM)
        Wo = jax.random.normal(ks[4], (INNER, DIM), dtype=jnp.float32) / np.sqrt(INNER)
        return {'x': x, 'latents': latents, 'ln1_w': ln1_w, 'ln1_b': ln1_b, 'ln2_w': ln2_w, 'ln2_b': ln2_b, 'Wq': Wq, 'Wkv': Wkv, 'Wo': Wo}
    _L0_xattn_all = _L0_xattn_setup()
    _L0_xattn_in = {k: v for k, v in _L0_xattn_all.items() if k in ('ln1_w', 'ln1_b', 'ln2_w', 'ln2_b', 'Wq', 'Wkv', 'Wo')}
    del _L0_xattn_all

    def _L0_ffn_setup():
        import jax, jax.numpy as jnp
        import numpy as np
        BLOCK = 32
        W_BITS = 4
        ACT_BITS = 16

        def act_qdq(x):
            qmax = 2.0 ** (ACT_BITS - 1) - 1.0
            scale = jnp.maximum(jnp.max(jnp.abs(x)) / qmax, 1e-12)
            return jnp.clip(jnp.round(x / scale), -qmax - 1.0, qmax) * scale

        def fixed_qdq_u16(x):
            scale = 1.0 / 65536.0
            return jnp.clip(jnp.round(x / scale), 0.0, 65535.0) * scale

        def lpbq_dequant(w):
            O, I = w.shape
            qmax = 2.0 ** (W_BITS - 1) - 1.0
            wb = w.reshape(O, I // BLOCK, BLOCK)
            s = jnp.maximum(jnp.max(jnp.abs(wb), axis=-1, keepdims=True) / qmax, 1e-12)
            wq = jnp.clip(jnp.round(wb / s), -qmax - 1.0, qmax) * s
            return wq.reshape(O, I)
        key = jax.random.key(seed)
        k1, k2, k3, k4 = jax.random.split(key, 4)
        B, S, H, I = (2, 512, 128, 384)
        x = jax.random.normal(k1, (B, S, H), jnp.float32)
        w_gate = jax.random.normal(k2, (I, H), jnp.float32) * 0.02
        w_up = jax.random.normal(k3, (I, H), jnp.float32) * 0.02
        w_down = jax.random.normal(k4, (H, I), jnp.float32) * 0.02
        return {'x': x, 'w_gate': w_gate, 'w_up': w_up, 'w_down': w_down}
    _L0_ffn_all = _L0_ffn_setup()
    _L0_ffn_in = {k: v for k, v in _L0_ffn_all.items() if k in ('w_gate', 'w_up', 'w_down')}
    del _L0_ffn_all

    def _L1_attn_setup():
        import jax, jax.numpy as jnp
        import numpy as np
        HEADS = 16
        WINDOW = 128
        key = jax.random.key(seed)
        k1, k2, k3, k4 = jax.random.split(key, 4)
        B, N, C = (2, 256, 128)
        x = jax.random.normal(k1, (B, N, C), dtype=jnp.float32)
        w_qkv = jax.random.normal(k2, (3 * C, C), dtype=jnp.float32) * C ** (-0.5)
        w_out = jax.random.normal(k3, (C, C), dtype=jnp.float32) * C ** (-0.5)
        b_out = jax.random.normal(k4, (C,), dtype=jnp.float32) * 0.01
        return {'x': x, 'w_qkv': w_qkv, 'w_out': w_out, 'b_out': b_out}
    _L1_attn_all = _L1_attn_setup()
    _L1_attn_in = {k: v for k, v in _L1_attn_all.items() if k in ('w_qkv', 'w_out', 'b_out')}
    del _L1_attn_all

    def _L1_xattn_setup():
        import jax, jax.numpy as jnp
        import numpy as np
        EMBED_DIM = 128
        NUM_HEAD = 16
        HEAD_DIM = EMBED_DIM // NUM_HEAD
        SCALE = HEAD_DIM ** (-0.5)
        key = jax.random.key(seed)
        ks = jax.random.split(key, 8)
        B, N, K, D = (2, 256, 256, EMBED_DIM)
        s = D ** (-0.5)
        return {'x': jax.random.normal(ks[0], (B, N, D), jnp.float32), 'ctx': jax.random.normal(ks[1], (B, K, D), jnp.float32), 'Wq': jax.random.normal(ks[2], (D, D), jnp.float32) * s, 'bq': jnp.zeros((D,), jnp.float32), 'Wkv': jax.random.normal(ks[3], (D, 2 * D), jnp.float32) * s, 'bkv': jnp.zeros((2 * D,), jnp.float32), 'Wproj': jax.random.normal(ks[4], (D, D), jnp.float32) * s, 'bproj': jnp.zeros((D,), jnp.float32)}
    _L1_xattn_all = _L1_xattn_setup()
    _L1_xattn_in = {k: v for k, v in _L1_xattn_all.items() if k in ('Wq', 'bq', 'Wkv', 'bkv', 'Wproj', 'bproj')}
    del _L1_xattn_all

    def _L1_ffn_setup():
        import jax, jax.numpy as jnp
        import numpy as np
        from jax import lax
        HIDDEN = 128
        INTER = 64
        E = 64
        K = 6
        G = 8
        TG = 4
        NSH = 2
        ISH = INTER * NSH

        def _moe_forward(hidden_states, gate_w, gate_bias, eg_w, eu_w, ed_w, sg_w, su_w, sd_w):
            B, S, H = hidden_states.shape
            x = hidden_states.reshape(-1, H)
            T = x.shape[0]
            shared = jax.nn.silu(x @ sg_w.T) * (x @ su_w.T) @ sd_w.T
            logits = x @ gate_w.T
            scores = jax.nn.sigmoid(logits) + gate_bias
            group_scores = scores.reshape(T, G, E // G).max(axis=-1)
            _, sel_groups = lax.top_k(group_scores, TG)
            group_mask = jnp.zeros((T, G), scores.dtype).at[jnp.arange(T)[:, None], sel_groups].set(1.0)
            mask = jnp.repeat(group_mask, E // G, axis=1)
            masked_scores = scores * mask
            topk_w, topk_i = lax.top_k(masked_scores, K)
            topk_w = topk_w / (topk_w.sum(axis=-1, keepdims=True) + 1e-08)
            comb = jnp.zeros((T, E), x.dtype).at[jnp.arange(T)[:, None], topk_i].add(topk_w)
            h = jax.nn.silu(jnp.einsum('th,eih->eti', x, eg_w)) * jnp.einsum('th,eih->eti', x, eu_w)
            routed = jnp.einsum('eti,ehi,te->th', h, ed_w, comb)
            return (shared + routed).reshape(B, S, H)
        key = jax.random.key(seed)
        ks = jax.random.split(key, 9)
        s = 0.02
        return {'hidden_states': jax.random.normal(ks[0], (1, 128, HIDDEN), jnp.float32), 'gate_w': jax.random.normal(ks[1], (E, HIDDEN), jnp.float32) * s, 'gate_bias': jnp.zeros((E,), jnp.float32), 'eg_w': jax.random.normal(ks[2], (E, INTER, HIDDEN), jnp.float32) * s, 'eu_w': jax.random.normal(ks[3], (E, INTER, HIDDEN), jnp.float32) * s, 'ed_w': jax.random.normal(ks[4], (E, HIDDEN, INTER), jnp.float32) * s, 'sg_w': jax.random.normal(ks[5], (ISH, HIDDEN), jnp.float32) * s, 'su_w': jax.random.normal(ks[6], (ISH, HIDDEN), jnp.float32) * s, 'sd_w': jax.random.normal(ks[7], (HIDDEN, ISH), jnp.float32) * s}
    _L1_ffn_all = _L1_ffn_setup()
    _L1_ffn_in = {k: v for k, v in _L1_ffn_all.items() if k in ('gate_w', 'gate_bias', 'eg_w', 'eu_w', 'ed_w', 'sg_w', 'su_w', 'sd_w')}
    del _L1_ffn_all
    return {'x': x, 'ctx_1024': ctx_1024, 'L0_attn_W_attn': _L0_attn_in['W_attn'], 'L0_attn_b_attn': _L0_attn_in['b_attn'], 'L0_attn_W_proj': _L0_attn_in['W_proj'], 'L0_attn_b_proj': _L0_attn_in['b_proj'], 'L0_xattn_ln1_w': _L0_xattn_in['ln1_w'], 'L0_xattn_ln1_b': _L0_xattn_in['ln1_b'], 'L0_xattn_ln2_w': _L0_xattn_in['ln2_w'], 'L0_xattn_ln2_b': _L0_xattn_in['ln2_b'], 'L0_xattn_Wq': _L0_xattn_in['Wq'], 'L0_xattn_Wkv': _L0_xattn_in['Wkv'], 'L0_xattn_Wo': _L0_xattn_in['Wo'], 'L0_ffn_w_gate': _L0_ffn_in['w_gate'], 'L0_ffn_w_up': _L0_ffn_in['w_up'], 'L0_ffn_w_down': _L0_ffn_in['w_down'], 'L1_attn_w_qkv': _L1_attn_in['w_qkv'], 'L1_attn_w_out': _L1_attn_in['w_out'], 'L1_attn_b_out': _L1_attn_in['b_out'], 'L1_xattn_Wq': _L1_xattn_in['Wq'], 'L1_xattn_bq': _L1_xattn_in['bq'], 'L1_xattn_Wkv': _L1_xattn_in['Wkv'], 'L1_xattn_bkv': _L1_xattn_in['bkv'], 'L1_xattn_Wproj': _L1_xattn_in['Wproj'], 'L1_xattn_bproj': _L1_xattn_in['bproj'], 'L1_ffn_gate_w': _L1_ffn_in['gate_w'], 'L1_ffn_gate_bias': _L1_ffn_in['gate_bias'], 'L1_ffn_eg_w': _L1_ffn_in['eg_w'], 'L1_ffn_eu_w': _L1_ffn_in['eu_w'], 'L1_ffn_ed_w': _L1_ffn_in['ed_w'], 'L1_ffn_sg_w': _L1_ffn_in['sg_w'], 'L1_ffn_su_w': _L1_ffn_in['su_w'], 'L1_ffn_sd_w': _L1_ffn_in['sd_w']}

def reference(x, ctx_1024, L0_attn_W_attn, L0_attn_b_attn, L0_attn_W_proj, L0_attn_b_proj, L0_xattn_ln1_w, L0_xattn_ln1_b, L0_xattn_ln2_w, L0_xattn_ln2_b, L0_xattn_Wq, L0_xattn_Wkv, L0_xattn_Wo, L0_ffn_w_gate, L0_ffn_w_up, L0_ffn_w_down, L1_attn_w_qkv, L1_attn_w_out, L1_attn_b_out, L1_xattn_Wq, L1_xattn_bq, L1_xattn_Wkv, L1_xattn_bkv, L1_xattn_Wproj, L1_xattn_bproj, L1_ffn_gate_w, L1_ffn_gate_bias, L1_ffn_eg_w, L1_ffn_eu_w, L1_ffn_ed_w, L1_ffn_sg_w, L1_ffn_su_w, L1_ffn_sd_w):
    import jax
    import jax.numpy as jnp

    def _L0_attn_ref(x, W_attn, b_attn, W_proj, b_proj):
        import jax, jax.numpy as jnp
        import numpy as np
        N_HEADS = 16

        def _alibi_causal_mask(T, n_heads, dtype):
            slopes = (1.0 / jnp.power(2.0, jnp.arange(1, n_heads + 1, dtype=dtype)))[:, None, None]
            idx = jnp.arange(T)
            rel = (idx[None, :] - idx[:, None]).astype(dtype)
            alibi = jnp.tril(rel)
            causal = jnp.where(idx[None, :] > idx[:, None], -jnp.inf, 0.0).astype(dtype)
            return (alibi + causal)[None, :, :] * slopes
        B, T, C = x.shape
        H = N_HEADS
        D = C // H
        qkv = x @ W_attn + b_attn
        q, k, v = jnp.split(qkv, 3, axis=-1)
        q = q.reshape(B, T, H, D).transpose(0, 2, 1, 3)
        k = k.reshape(B, T, H, D).transpose(0, 2, 1, 3)
        v = v.reshape(B, T, H, D).transpose(0, 2, 1, 3)
        att = jnp.einsum('bhtd,bhsd->bhts', q, k) / jnp.sqrt(jnp.asarray(D, x.dtype))
        att = att + _alibi_causal_mask(T, H, x.dtype)[None]
        att = jax.nn.softmax(att, axis=-1)
        y = jnp.einsum('bhts,bhsd->bhtd', att, v)
        y = y.transpose(0, 2, 1, 3).reshape(B, T, C)
        return y @ W_proj + b_proj

    def _L0_xattn_ref(x, latents, ln1_w, ln1_b, ln2_w, ln2_b, Wq, Wkv, Wo):
        import jax, jax.numpy as jnp
        import numpy as np
        DIM = 128
        HEADS = 16
        DIM_HEAD = 64
        INNER = HEADS * DIM_HEAD
        EPS = 1e-05

        def _layernorm(t, w, b):
            mu = jnp.mean(t, axis=-1, keepdims=True)
            var = jnp.mean(jnp.square(t - mu), axis=-1, keepdims=True)
            return (t - mu) * jax.lax.rsqrt(var + EPS) * w + b
        xn = _layernorm(x, ln1_w, ln1_b)
        latn = _layernorm(latents, ln2_w, ln2_b)
        b, l, _ = latn.shape
        q = latn @ Wq
        kv_input = jnp.concatenate([xn, latn], axis=1)
        kv = kv_input @ Wkv
        k, v = jnp.split(kv, 2, axis=-1)

        def heads(t):
            return t.reshape(t.shape[0], t.shape[1], HEADS, DIM_HEAD).transpose(0, 2, 1, 3)
        q, k, v = (heads(q), heads(k), heads(v))
        scale = 1.0 / np.sqrt(np.sqrt(DIM_HEAD))
        weight = jnp.einsum('bhld,bhnd->bhln', q * scale, k * scale)
        weight = jax.nn.softmax(weight.astype(jnp.float32), axis=-1).astype(weight.dtype)
        out = jnp.einsum('bhln,bhnd->bhld', weight, v)
        out = out.transpose(0, 2, 1, 3).reshape(b, l, INNER)
        return out @ Wo

    def _L0_ffn_ref(x, w_gate, w_up, w_down):
        import jax, jax.numpy as jnp
        import numpy as np
        BLOCK = 32
        W_BITS = 4
        ACT_BITS = 16

        def act_qdq(x):
            qmax = 2.0 ** (ACT_BITS - 1) - 1.0
            scale = jnp.maximum(jnp.max(jnp.abs(x)) / qmax, 1e-12)
            return jnp.clip(jnp.round(x / scale), -qmax - 1.0, qmax) * scale

        def fixed_qdq_u16(x):
            scale = 1.0 / 65536.0
            return jnp.clip(jnp.round(x / scale), 0.0, 65535.0) * scale

        def lpbq_dequant(w):
            O, I = w.shape
            qmax = 2.0 ** (W_BITS - 1) - 1.0
            wb = w.reshape(O, I // BLOCK, BLOCK)
            s = jnp.maximum(jnp.max(jnp.abs(wb), axis=-1, keepdims=True) / qmax, 1e-12)
            wq = jnp.clip(jnp.round(wb / s), -qmax - 1.0, qmax) * s
            return wq.reshape(O, I)
        x = act_qdq(x)
        up = act_qdq(x @ lpbq_dequant(w_up).T)
        gate = act_qdq(x @ lpbq_dequant(w_gate).T)
        sig = fixed_qdq_u16(jax.nn.sigmoid(gate))
        gate = act_qdq(gate * sig)
        o = act_qdq(gate * up)
        return o @ lpbq_dequant(w_down).T

    def _L1_attn_ref(x, w_qkv, w_out, b_out):
        import jax, jax.numpy as jnp
        import numpy as np
        HEADS = 16
        WINDOW = 128
        B, N, C = x.shape
        H, Dh = (HEADS, C // HEADS)
        scale = Dh ** (-0.5)
        qkv = (x @ w_qkv.T).reshape(B, N, 3, H, Dh)
        q = jnp.transpose(qkv[:, :, 0], (0, 2, 1, 3))
        k = jnp.transpose(qkv[:, :, 1], (0, 2, 1, 3))
        v = jnp.transpose(qkv[:, :, 2], (0, 2, 1, 3))
        scores = jnp.einsum('bhnd,bhmd->bhnm', q, k) * scale
        i = jnp.arange(N)[:, None]
        j = jnp.arange(N)[None, :]
        local_mask = (j <= i) & (jnp.abs(i - j) <= WINDOW)
        attn_local = jax.nn.softmax(jnp.where(local_mask[None, None], scores, -jnp.inf), axis=-1)
        out_local = jnp.einsum('bhnm,bhmd->bhnd', attn_local, v)
        stride = WINDOW
        k_g = k[:, :, ::stride]
        v_g = v[:, :, ::stride]
        scores_g = jnp.einsum('bhnd,bhmd->bhnm', q, k_g) * scale
        attn_g = jax.nn.softmax(scores_g, axis=-1)
        out_g = jnp.einsum('bhnm,bhmd->bhnd', attn_g, v_g)
        out = (out_local + out_g).transpose(0, 2, 1, 3).reshape(B, N, C)
        return out @ w_out.T + b_out

    def _L1_xattn_ref(x, ctx, Wq, bq, Wkv, bkv, Wproj, bproj):
        import jax, jax.numpy as jnp
        import numpy as np
        EMBED_DIM = 128
        NUM_HEAD = 16
        HEAD_DIM = EMBED_DIM // NUM_HEAD
        SCALE = HEAD_DIM ** (-0.5)
        B, N, D = x.shape
        K = ctx.shape[1]
        H, hd = (NUM_HEAD, HEAD_DIM)
        q = (x @ Wq + bq).reshape(B, N, H, hd).transpose(0, 2, 1, 3)
        kv = (ctx @ Wkv + bkv).reshape(B, K, 2, H, hd).transpose(2, 0, 3, 1, 4)
        k, v = (kv[0], kv[1])
        attn = jnp.einsum('bhnd,bhkd->bhnk', q * SCALE, k)
        attn = jax.nn.softmax(attn, axis=-1)
        out = jnp.einsum('bhnk,bhkd->bhnd', attn, v)
        out = out.transpose(0, 2, 1, 3).reshape(B, N, D)
        return out @ Wproj + bproj

    def _L1_ffn_ref(hidden_states, gate_w, gate_bias, eg_w, eu_w, ed_w, sg_w, su_w, sd_w):
        import jax, jax.numpy as jnp
        import numpy as np
        from jax import lax
        HIDDEN = 128
        INTER = 64
        E = 64
        K = 6
        G = 8
        TG = 4
        NSH = 2
        ISH = INTER * NSH

        def _moe_forward(hidden_states, gate_w, gate_bias, eg_w, eu_w, ed_w, sg_w, su_w, sd_w):
            B, S, H = hidden_states.shape
            x = hidden_states.reshape(-1, H)
            T = x.shape[0]
            shared = jax.nn.silu(x @ sg_w.T) * (x @ su_w.T) @ sd_w.T
            logits = x @ gate_w.T
            scores = jax.nn.sigmoid(logits) + gate_bias
            group_scores = scores.reshape(T, G, E // G).max(axis=-1)
            _, sel_groups = lax.top_k(group_scores, TG)
            group_mask = jnp.zeros((T, G), scores.dtype).at[jnp.arange(T)[:, None], sel_groups].set(1.0)
            mask = jnp.repeat(group_mask, E // G, axis=1)
            masked_scores = scores * mask
            topk_w, topk_i = lax.top_k(masked_scores, K)
            topk_w = topk_w / (topk_w.sum(axis=-1, keepdims=True) + 1e-08)
            comb = jnp.zeros((T, E), x.dtype).at[jnp.arange(T)[:, None], topk_i].add(topk_w)
            h = jax.nn.silu(jnp.einsum('th,eih->eti', x, eg_w)) * jnp.einsum('th,eih->eti', x, eu_w)
            routed = jnp.einsum('eti,ehi,te->th', h, ed_w, comb)
            return (shared + routed).reshape(B, S, H)
        return _moe_forward(hidden_states, gate_w, gate_bias, eg_w, eu_w, ed_w, sg_w, su_w, sd_w)
    x = x + _L0_attn_ref(_layernorm(x, axis=-1), L0_attn_W_attn, L0_attn_b_attn, L0_attn_W_proj, L0_attn_b_proj)
    x = x + _L0_xattn_ref(ctx_1024, _layernorm(x, axis=-1), L0_xattn_ln1_w, L0_xattn_ln1_b, L0_xattn_ln2_w, L0_xattn_ln2_b, L0_xattn_Wq, L0_xattn_Wkv, L0_xattn_Wo)
    x = x + _L0_ffn_ref(_layernorm(x, axis=-1), L0_ffn_w_gate, L0_ffn_w_up, L0_ffn_w_down)
    x = x + _L1_attn_ref(_layernorm(x, axis=-1), L1_attn_w_qkv, L1_attn_w_out, L1_attn_b_out)
    x = x + _L1_xattn_ref(_layernorm(x, axis=-1), ctx_1024, L1_xattn_Wq, L1_xattn_bq, L1_xattn_Wkv, L1_xattn_bkv, L1_xattn_Wproj, L1_xattn_bproj)
    x = x + _L1_ffn_ref(_layernorm(x, axis=-1), L1_ffn_gate_w, L1_ffn_gate_bias, L1_ffn_eg_w, L1_ffn_eu_w, L1_ffn_ed_w, L1_ffn_sg_w, L1_ffn_su_w, L1_ffn_sd_w)
    return x

_drawn_inputs = setup_inputs


def setup_inputs(seed=0):
    import zlib

    import numpy as np

    out = dict(_drawn_inputs(seed))
    spreads = {'L0_xattn_ln1_w': (1.0, 0.2),
     'L0_xattn_ln1_b': (0.0, 0.1),
     'L0_xattn_ln2_w': (1.0, 0.2),
     'L0_xattn_ln2_b': (0.0, 0.1),
     'L1_xattn_bq': (0.0, 0.55),
     'L1_xattn_bkv': (0.0, 0.1),
     'L1_xattn_bproj': (0.0, 0.1),
     'L1_ffn_gate_bias': (0.0, 0.8)}
    factors = {'L0_attn_b_attn': 8.0,
     'L0_ffn_w_gate': 5.927,
     'L0_ffn_w_up': 5.758,
     'L0_ffn_w_down': 5.855,
     'L1_attn_b_out': 8.0,
     'L1_ffn_gate_w': 8.0,
     'L1_ffn_eg_w': 8.0,
     'L1_ffn_eu_w': 8.0,
     'L1_ffn_ed_w': 8.0,
     'L1_ffn_sg_w': 8.0,
     'L1_ffn_su_w': 8.0,
     'L1_ffn_sd_w': 8.0}
    for name, (base, spread) in spreads.items():
        noise = np.random.default_rng([zlib.crc32(name.encode()), seed]).standard_normal(out[name].shape)
        drawn = base * np.exp(spread * noise) if base else spread * noise
        out[name] = jnp.asarray(drawn.astype(out[name].dtype))
    for name, factor in factors.items():
        out[name] = (out[name] * factor).astype(out[name].dtype)
    return out
```

```python
from contextlib import ExitStack

import concourse.bass as bass
import numpy as np
from concourse import mybir

F32 = mybir.dt.float32
BF16 = mybir.dt.bfloat16
F32R = mybir.dt.float32r
ALU = mybir.AluOpType
ACT = mybir.ActivationFunctionType
AX = mybir.AxisListType

B, T, C, L = 32, 128, 128, 77
H, D = 16, 8
HC, NC = 4, 4
XH, XD = 16, 64
XC = XH // 2
VSTEP = 128 + D
EPS = 1e-5
MASKED = -1e30


class Names:
    pass


def wait(engine, semaphore, value):
    if not isinstance(value, int) or value > 0:
        engine.wait_ge(semaphore, value)


def exists(b):
    return not isinstance(b, int) or 0 <= b < B


def over_sequences(engine, body):
    body(0, 0)
    body(1, 1)
    with engine.Fori(1, B // 2 - 1) as i:
        body(2 * i, 0)
        body(2 * i + 1, 1)
    body(B - 2, 0)
    body(B - 1, 1)


def tok(t, b):
    if isinstance(b, int):
        return t[:, b * 128:(b + 1) * 128]
    return t[:, bass.ds(b * 128, 128)]


def one(t, b, p=128):
    if isinstance(b, int):
        return t[0:p, b:b + 1]
    return t[0:p, bass.ds(b, 1)]


class Attention:
    def __init__(self, keys, cross, first_value, split_weights, mask, wq, wk, wv, wo, bq, bk, bv, base):
        self.keys, self.cross, self.first_value, self.split_weights = keys, cross, first_value, split_weights
        self.mask, self.wq, self.wk, self.wv, self.wo = mask, wq, wk, wv, wo
        self.bq, self.bk, self.bv, self.base = bq, bk, bv, base


class AttentionSemaphores:
    def __init__(self, sem, stage):
        self.normed = sem(f"{stage}_normed")
        self.based = sem(f"{stage}_based")
        self.transposed = sem(f"{stage}_transposed")
        self.inputs_t = sem(f"{stage}_inputs_t")
        self.projected = sem(f"{stage}_projected")
        self.keys = sem(f"{stage}_keys")
        self.values = sem(f"{stage}_values")
        self.scores = sem(f"{stage}_scores")
        self.maxed = sem(f"{stage}_maxed")
        self.exped = sem(f"{stage}_exped")
        self.probs_t = sem(f"{stage}_probs_t")
        self.probs_s = sem(f"{stage}_probs_s")
        self.weighted = sem(f"{stage}_weighted")
        self.recips = sem(f"{stage}_recips")
        self.recips_t = sem(f"{stage}_recips_t")
        self.recips_s = sem(f"{stage}_recips_s")
        self.heads_out = sem(f"{stage}_heads_out")
        self.projected_out = sem(f"{stage}_projected_out")
        self.updated = sem(f"{stage}_updated")
        self.own = sem(f"{stage}_own")
        self.measured = sem(f"{stage}_measured")




def attention_tensor(pe, nc, m, s, a):
    nk = a.keys

    def transpose_inputs(b, u):
        pe.wait_ge(s.normed, b + 1)
        wait(pe, s.keys, NC * b)
        last = nc.tensor.transpose(m.front[:, 0:128], m.xn[:, u, :], m.ident[:])
        if a.cross:
            pe.wait_ge(s.copied[u], 16 + 8 * (b - u))
            last = nc.tensor.transpose(m.front[:, 128:256], m.cs[:, u, :], m.ident[:])
        last.then_inc(s.transposed, 1)

    def project(b, u):
        pe.wait_ge(s.inputs_t, b + 1)
        x_t = m.xt[:, u, 0:128]
        kv_t = m.xt[:, u, 128:256] if a.cross else x_t
        nc.tensor.matmul(m.front[:, 128:256], a.wq, x_t, start=True, stop=True)
        nc.tensor.matmul(m.front[:, 256:384], a.wk, kv_t, start=True, stop=True)
        last = nc.tensor.matmul(m.front[:, 384:512], kv_t, a.wv, start=True, stop=True)
        if a.first_value:
            last = nc.tensor.matmul(m.front[:, 0:1], a.wv, m.xt[:, u, 0:1], start=True, stop=True)
        last.then_inc(s.projected, 1)

    def scores(b, u, c):
        j = NC * b + c
        pe.wait_ge(s.keys, j + 1)
        wait(pe, s.exped, j - 1)
        bank = m.score[c % 2][:, 0:HC * nk]
        if a.mask is not None:
            nc.tensor.matmul(bank, m.ident_b[:], a.mask(c), start=True, stop=False)
        kx = m.kx[:, u, HC * c:HC * c + HC, 0:nk]
        nc.tensor.matmul(bank, m.q[:, u, :], kx, start=a.mask is None, stop=True).then_inc(s.scores, 1)

    def transpose_probs(b, u, c):
        j = NC * b + c
        pe.wait_ge(s.exped, j + 1)
        wait(pe, s.probs_s, j - 1)
        for h in range(HC):
            last = nc.tensor.transpose(m.flip[c % 2][:, h * 128:h * 128 + 128], m.p[:, c % 2, h, :],
                                       m.ident[:])
        last.then_inc(s.probs_t, 1)

    def weigh(b, u, c):
        j = NC * b + c
        if c == 0:
            pe.wait_ge(s.values, b + 1)
            wait(pe, s.updated, b - 1)
        pe.wait_ge(s.probs_s, j + 1)
        for h in range(HC):
            g = HC * c + h
            last = nc.tensor.matmul(m.out[u][:, 0:128], m.vx[:, u, g * 128:g * 128 + 128],
                                    m.pt[:, c % 2, h, :], start=g == 0, stop=g == H - 1)
        last.then_inc(s.weighted, 1)

    def transpose_recips(b, u):
        pe.wait_ge(s.recips, b + 1)
        nc.tensor.transpose(m.out[u][:, 128:256], m.rx[:], m.ident[:]).then_inc(s.recips_t, 1)

    def project_out(b, u):
        pe.wait_ge(s.heads_out, b + 1)
        nc.tensor.matmul(m.out[u][:, 256:384], m.ot[:, u, :], a.wo, start=True, stop=True)\
            .then_inc(s.projected_out, 1)

    def body(b, u):
        for c in range(NC):
            transpose_probs(b, u, c)
            if c == 0 and exists(b + 1):
                project(b + 1, 1 - u)
            if c < 2:
                scores(b, u, c + 2)
            elif exists(b + 1):
                scores(b + 1, 1 - u, c - 2)
            if c > 0:
                weigh(b, u, c - 1)
            elif exists(b - 1):
                weigh(b - 1, 1 - u, NC - 1)
            if c == 3 and exists(b + 2):
                transpose_inputs(b + 2, u)
            if c == 0 and exists(b - 1):
                transpose_recips(b - 1, 1 - u)
            if c == 3 and exists(b - 1):
                project_out(b - 1, 1 - u)

    pe.wait_ge(m.s.weights, m.weights_in)
    transpose_inputs(0, 0)
    project(0, 0)
    scores(0, 0, 0)
    scores(0, 0, 1)
    transpose_inputs(1, 1)
    over_sequences(pe, body)
    weigh(B - 1, 1, NC - 1)
    transpose_recips(B - 1, 1)
    project_out(B - 1, 1)


def attention_scalar(act, nc, m, s, a):
    def copy_inputs(b, u):
        act.wait_ge(s.transposed, b + 1)
        w = 256 if a.cross else 128
        nc.scalar.copy(m.xt[:, u, 0:w], m.front[:, 0:w]).then_inc(s.inputs_t, 1)

    def exponentials(b, u, c):
        j = NC * b + c
        act.wait_ge(s.maxed, j + 1)
        wait(act, s.probs_t, j - 1)
        for h in range(HC):
            last = nc.scalar.activation(m.p[:, c % 2, h, 0:a.keys],
                                        m.score[c % 2][:, h * a.keys:(h + 1) * a.keys], ACT.Exp,
                                        bias=m.nmax[:, c % 2, h:h + 1],
                                        accum_out=m.sums[:, u, HC * c + h:HC * c + h + 1])
        last.then_inc(s.exped, 1)

    def copy_probs(b, u, c):
        j = NC * b + c
        act.wait_ge(s.probs_t, j + 1)
        wait(act, s.weighted, j - 1)
        nc.scalar.copy(m.pt[:, c % 2, :, :].rearrange("p h t -> p (h t)"), m.flip[c % 2][:])\
            .then_inc(s.probs_s, 1)

    def copy_recips(b, u):
        act.wait_ge(s.recips_t, b + 1)
        nc.scalar.copy(m.rs[:, u, :], m.out[u][:, 128:256]).then_inc(s.recips_s, 1)

    def body(b, u):
        for c in range(NC):
            if c < NC - 1:
                exponentials(b, u, c + 1)
            elif exists(b + 1):
                exponentials(b + 1, 1 - u, 0)
            copy_probs(b, u, c)
            if c == 3 and exists(b + 2):
                copy_inputs(b + 2, u)
            if c == 0 and exists(b - 1):
                copy_recips(b - 1, 1 - u)

    copy_inputs(0, 0)
    exponentials(0, 0, 0)
    copy_inputs(1, 1)
    over_sequences(act, body)
    copy_recips(B - 1, 1)


def attention_vector(dve, nc, m, s, a):
    def normalise(b, u):
        wait(dve, s.transposed, b - 1)
        nc.vector.tensor_scalar(m.xn[:, u, :], tok(m.x, b), one(m.rstd, b), one(m.shift, b),
                                ALU.mult, ALU.add).then_inc(s.normed, 1)

    def queries(b, u):
        dve.wait_ge(s.projected, b + 1)
        nc.vector.tensor_scalar(m.q[:, u, :], m.front[:, 128:256], a.bq, float(D) ** -0.5,
                                ALU.add, ALU.mult)

    def keys(b, u, c):
        rows = slice(32 * c, 32 * c + 32)
        k = m.front[rows, 256:256 + a.keys].unsqueeze(1).broadcast_to([32, HC, a.keys])
        own = m.own_rows[rows, :].unsqueeze(2).broadcast_to([32, HC, a.keys])
        nc.vector.scalar_tensor_tensor(m.kx[rows, u, HC * c:HC * c + HC, 0:a.keys], k, a.bk[rows, :],
                                       own, ALU.add, ALU.mult).then_inc(s.keys, 1)

    def values(b, u):
        wait(dve, s.weighted, NC * (b - 1))
        wide = m.vx[:, u, :].rearrange("p (h e) -> p h e", e=VSTEP)[:, :, 0:D]
        nc.vector.tensor_copy(wide, m.front[:, 384:512].rearrange("p (h d) -> p h d", d=D))\
            .then_inc(s.values, 1)

    def first_value(b, u):
        if a.first_value:
            wait(dve, s.heads_out, b - 1)
            nc.vector.tensor_copy(m.v0[:, u:u + 1], m.front[:, 0:1])

    def maxima(b, u, c):
        j = NC * b + c
        dve.wait_ge(s.scores, j + 1)
        nc.vector.tensor_reduce(m.nmax[:, c % 2, :],
                                m.score[c % 2][:, 0:HC * a.keys].rearrange("p (h k) -> p h k", h=HC),
                                AX.X, ALU.max, negate=True).then_inc(s.maxed, 1)

    def reciprocals(b, u):
        dve.wait_ge(s.exped, NC * b + NC)
        wait(dve, s.recips_t, b)
        nc.vector.reciprocal(m.rx[:].rearrange("p (h d) -> p h d", d=D),
                             m.sums[:, u, :].unsqueeze(2).broadcast_to([128, H, D]))\
            .then_inc(s.recips, 1)

    def heads_out(b, u):
        dve.wait_ge(s.recips_s, b + 1)
        dve.wait_ge(s.weighted, NC * b + NC)
        nc.vector.tensor_tensor(m.ot1[:], m.out[u][:, 0:128], m.rs[:, u, :], ALU.mult)\
            .then_inc(s.own, 1)
        dve.wait_ge(s.own, b + 1)
        extra = m.v0[:, u:u + 1] if a.first_value else a.bv
        nc.vector.tensor_scalar(m.ot[:, u, :], m.ot1[:], extra, None, ALU.add).then_inc(s.heads_out, 1)

    def update(b, u):
        dve.wait_ge(s.projected_out, b + 1)
        dve.wait_ge(s.based, b + 1)
        nc.vector.tensor_tensor(tok(m.x, b), m.out[u][:, 256:384], tok(m.x, b), ALU.add)\
            .then_inc(s.updated, 1)

    def statistics(b):
        dve.wait_ge(s.updated, b + 1)
        nc.vector.bn_stats(m.stats[:, b, :] if isinstance(b, int) else
                           m.stats[:, bass.ds(b, 1), :].rearrange("p a k -> p (a k)"), tok(m.x, b))\
            .then_inc(s.measured, 1)

    def body(b, u):
        for c in range(NC):
            if c == 0 and exists(b - 1):
                reciprocals(b - 1, 1 - u)
            if c < 2:
                maxima(b, u, c + 2)
            elif exists(b + 1):
                maxima(b + 1, 1 - u, c - 2)
            if c == 2 and exists(b - 1):
                heads_out(b - 1, 1 - u)
            if c == 2 and exists(b + 1):
                first_value(b + 1, 1 - u)
            if c == 0 and exists(b + 1):
                queries(b + 1, 1 - u)
            if c < 2 and exists(b + 1):
                keys(b + 1, 1 - u, c)
            if c in (1, 2) and exists(b + 1):
                keys(b + 1, 1 - u, c + 1)
            if c == 1 and exists(b + 1):
                values(b + 1, 1 - u)
            if c == 2 and exists(b + 2):
                normalise(b + 2, u)
            if c == 3 and exists(b - 1):
                update(b - 1, 1 - u)
                statistics(b - 1)

    normalise(0, 0)
    normalise(1, 1)
    queries(0, 0)
    first_value(0, 0)
    values(0, 0)
    for c in range(NC):
        keys(0, 0, c)
    maxima(0, 0, 0)
    maxima(0, 0, 1)
    over_sequences(dve, body)
    reciprocals(B - 1, 1)
    heads_out(B - 1, 1)
    update(B - 1, 1)
    statistics(B - 1)
    dve.wait_ge(s.measured, B)


def attention_pool(pool, nc, m, s, a):
    def body(b, u):
        pool.wait_ge(s.normed, b + 1)
        nc.gpsimd.tensor_tensor(tok(m.x, b), tok(m.x, b), a.base, ALU.add).then_inc(s.based, 1)
        if a.split_weights:
            split_experts(pool, nc, m, m.es, b, u)

    over_sequences(pool, body)


def split_experts(pool, nc, m, s, k, u):
    at = slice(k * 128, k * 128 + 128) if isinstance(k, int) else bass.ds(k * 128, 128)
    pool.wait_ge(s.raw[u], 16 + 8 * (k - u))
    nc.gpsimd.tensor_copy(m.w_hi[:, :, at], m.raw[:, u, 0:3, :]).then_inc(s.split_hi, 1)
    if not (isinstance(k, int) and k == B):
        nc.gpsimd.tensor_copy(m.pick[:, at], m.raw[:, u, 3, :])
    pool.wait_ge(s.split_hi, k + 1)
    nc.gpsimd.tensor_tensor(m.w_lo[:, :, at], m.raw[:, u, 0:3, :], m.w_hi[:, :, at].bitcast(F32),
                            ALU.subtract).then_inc(s.split, 1)


class WideSemaphores:
    def __init__(self, sem, stage):
        self.score_weights = sem(f"{stage}_score_weights")
        self.score_saved = sem(f"{stage}_score_saved")
        self.out_weights = sem(f"{stage}_out_weights")
        self.out_saved = sem(f"{stage}_out_saved")
        self.normed = sem(f"{stage}_normed")
        self.latents = sem(f"{stage}_latents")
        self.contexts = sem(f"{stage}_contexts")
        self.transposed = sem(f"{stage}_transposed")
        self.inputs_t = sem(f"{stage}_inputs_t")
        self.asked = sem(f"{stage}_asked")
        self.queries = sem(f"{stage}_queries")
        self.scores = sem(f"{stage}_scores")
        self.maxed = sem(f"{stage}_maxed")
        self.exped = sem(f"{stage}_exped")
        self.probs = sem(f"{stage}_probs")
        self.probs_t = sem(f"{stage}_probs_t")
        self.probs_s = sem(f"{stage}_probs_s")
        self.weighted = sem(f"{stage}_weighted")
        self.heads_s = sem(f"{stage}_heads_s")
        self.projected_out = sem(f"{stage}_projected_out")
        self.updated = sem(f"{stage}_updated")
        self.scaled = sem(f"{stage}_scaled")
        self.summed = sem(f"{stage}_summed")
        self.measured = sem(f"{stage}_measured")


KW = T + L


def wide_tensor(pe, nc, m, s):
    def weight_products(left, right, banks, made, saved):
        for g in range(4):
            wait(pe, saved, g - 1)
            for k in range(4):
                h = 4 * g + k
                last = nc.tensor.matmul(banks[g % 2][:, 128 * k:128 * k + 128], left[:, h, :],
                                        right[:, h, :], start=True, stop=True)
            last.then_inc(made, 1)

    def transpose_inputs(b, u):
        pe.wait_ge(s.latents, b + 1)
        pe.wait_ge(s.contexts, b + 1)
        wait(pe, s.inputs_t, b)
        nc.tensor.transpose(m.front[:, 0:128], m.kv[:, u, 0, :], m.ident[:])
        nc.tensor.transpose(m.front[:, 128:256], m.kv[:, u, 1, :], m.ident[:]).then_inc(s.transposed, 1)

    def ask(b, u, c):
        j = XC * b + c
        if c == 0:
            pe.wait_ge(s.inputs_t, b + 1)
        wait(pe, s.queries, j)
        for k in range(2):
            last = nc.tensor.matmul(m.ask[:, 128 * k:128 * k + 128], m.score_w[:, 2 * c + k, :],
                                    m.kvt[:, u, 0:T], start=True, stop=True)
        last.then_inc(s.asked, 1)

    def scores(b, u, c):
        j = XC * b + c
        pe.wait_ge(s.queries, j + 1)
        wait(pe, s.exped, j - 1)
        for k in range(2):
            last = nc.tensor.matmul(m.score[c % 2][:, KW * k:KW * k + KW],
                                    m.qs[:, c % 2, 128 * k:128 * k + 128], m.kvt[:, u, 0:KW],
                                    start=True, stop=True)
        last.then_inc(s.scores, 1)

    def transpose_probs(b, u, c):
        j = XC * b + c
        pe.wait_ge(s.probs, j + 1)
        wait(pe, s.probs_s, j)
        for part in range(2):
            for k in range(2):
                at = 256 * part + 128 * k
                last = nc.tensor.transpose(m.flip[0][:, at:at + 128],
                                           m.pw[:, c % 2, k, 128 * part:128 * part + 128], m.ident[:])
        last.then_inc(s.probs_t, 1)

    def weigh(b, u, c):
        j = XC * b + c
        pe.wait_ge(s.probs_s, j + 1)
        wait(pe, s.heads_s, j)
        for part in range(2):
            last = nc.tensor.matmul(m.mix[:, 0:256], m.kv[:, u, part, :],
                                    m.pwt[:, c % 2, 256 * part:256 * part + 256],
                                    start=part == 0, stop=part == 1)
        last.then_inc(s.weighted, 1)

    def project_out(b, u, c):
        j = XC * b + c
        if c == 0:
            wait(pe, s.updated, b - 1)
        pe.wait_ge(s.heads_s, j + 1)
        for k in range(2):
            last = nc.tensor.matmul(m.out[u][:, 0:128], m.us[:, c % 2, 128 * k:128 * k + 128],
                                    m.out_w[:, 2 * c + k, :], start=c == 0 and k == 0,
                                    stop=c == XC - 1 and k == 1)
        last.then_inc(s.projected_out, 1)

    def body(b, u):
        for c in range(XC):
            transpose_probs(b, u, c)
            if c < XC - 2:
                scores(b, u, c + 2)
            elif exists(b + 1):
                scores(b + 1, 1 - u, c + 2 - XC)
            if c > 0:
                weigh(b, u, c - 1)
            elif exists(b - 1):
                weigh(b - 1, 1 - u, XC - 1)
            if c == 2 and exists(b + 1):
                transpose_inputs(b + 1, 1 - u)
            if c < XC - 3:
                ask(b, u, c + 3)
            elif exists(b + 1):
                ask(b + 1, 1 - u, c + 3 - XC)
            if c > 1:
                project_out(b, u, c - 2)
            elif exists(b - 1):
                project_out(b - 1, 1 - u, XC - 2 + c)

    pe.wait_ge(m.s.wide_in, m.wide_loads)
    weight_products(m.wq_t, m.wk_t, m.score, s.score_weights, s.score_saved)
    weight_products(m.wv_t, m.wo_r, m.flip, s.out_weights, s.out_saved)
    transpose_inputs(0, 0)
    pe.wait_ge(s.score_saved, 4)
    pe.wait_ge(s.out_saved, 4)
    ask(0, 0, 0)
    ask(0, 0, 1)
    scores(0, 0, 0)
    ask(0, 0, 2)
    scores(0, 0, 1)
    over_sequences(pe, body)
    weigh(B - 1, 1, XC - 1)
    project_out(B - 1, 1, XC - 2)
    project_out(B - 1, 1, XC - 1)


def wide_scalar(act, nc, m, s):
    def copy_inputs(b, u):
        act.wait_ge(s.transposed, b + 1)
        nc.scalar.copy(m.kvt[:, u, :], m.front[:, 0:256]).then_inc(s.inputs_t, 1)

    def copy_queries(b, u, c):
        j = XC * b + c
        act.wait_ge(s.asked, j + 1)
        wait(act, s.scores, j - 1)
        nc.scalar.copy(m.qs[:, c % 2, :], m.ask[:, 0:256]).then_inc(s.queries, 1)

    def exponentials(b, u, c):
        j = XC * b + c
        act.wait_ge(s.maxed, j + 1)
        wait(act, s.probs, j - 1)
        for k in range(2):
            last = nc.scalar.activation(m.ew[:, c % 2, k, :], m.score[c % 2][:, KW * k:KW * k + KW],
                                        ACT.Exp, bias=m.nmax[:, c % 2, k:k + 1],
                                        accum_out=m.sums[:, c % 2, k:k + 1])
        last.then_inc(s.exped, 1)

    def copy_probs(b, u, c):
        j = XC * b + c
        act.wait_ge(s.probs_t, j + 1)
        wait(act, s.weighted, j - 1)
        nc.scalar.copy(m.pwt[:, c % 2, :], m.flip[0][:]).then_inc(s.probs_s, 1)

    def body(b, u):
        for c in range(XC):
            copy_probs(b, u, c)
            if c < XC - 1:
                exponentials(b, u, c + 1)
            elif exists(b + 1):
                exponentials(b + 1, 1 - u, 0)
            if c == 2 and exists(b + 1):
                copy_inputs(b + 1, 1 - u)
            if c < XC - 3:
                copy_queries(b, u, c + 3)
            elif exists(b + 1):
                copy_queries(b + 1, 1 - u, c + 3 - XC)

    for g in range(4):
        act.wait_ge(s.score_weights, g + 1)
        nc.scalar.mul(m.score_w[:, 4 * g:4 * g + 4, :].rearrange("p h c -> p (h c)"), m.score[g % 2][:],
                      float(XD) ** -0.5).then_inc(s.score_saved, 1)
    for g in range(4):
        act.wait_ge(s.out_weights, g + 1)
        nc.scalar.copy(m.out_w[:, 4 * g:4 * g + 4, :].rearrange("p h c -> p (h c)"), m.flip[g % 2][:])\
            .then_inc(s.out_saved, 1)
    copy_inputs(0, 0)
    copy_queries(0, 0, 0)
    copy_queries(0, 0, 1)
    copy_queries(0, 0, 2)
    exponentials(0, 0, 0)
    over_sequences(act, body)


def wide_vector(dve, nc, m, s):
    def normalise(b, u):
        wait(dve, s.latents, b - 1)
        wait(dve, s.contexts, b - 1)
        nc.vector.tensor_scalar(m.xn[:, u, :], tok(m.x, b), one(m.rstd, b), one(m.shift, b),
                                ALU.mult, ALU.add)
        nc.vector.tensor_scalar(m.cs[0:L, u, :], tok(m.ctx, b)[0:L], one(m.crstd, b, L),
                                one(m.cshift, b, L), ALU.mult, ALU.add).then_inc(s.normed, 1)

    def maxima(b, u, c):
        j = XC * b + c
        dve.wait_ge(s.scores, j + 1)
        nc.vector.tensor_reduce(m.nmax[:, c % 2, 0:2],
                                m.score[c % 2][:, 0:2 * KW].rearrange("p (h k) -> p h k", h=2),
                                AX.X, ALU.max, negate=True).then_inc(s.maxed, 1)

    def probabilities(b, u, c):
        j = XC * b + c
        dve.wait_ge(s.exped, j + 1)
        nc.vector.reciprocal(m.rw[:, c % 2, :], m.sums[:, c % 2, 0:2]).then_inc(s.summed, 1)
        dve.wait_ge(s.summed, j + 1)
        wait(dve, s.probs_t, j - 1)
        for k in range(2):
            last = nc.vector.tensor_scalar(m.pw[:, c % 2, k, 0:KW], m.ew[:, c % 2, k, :],
                                           m.rw[:, c % 2, k:k + 1], None, ALU.mult)
        last.then_inc(s.probs, 1)

    def copy_heads(b, u, c):
        j = XC * b + c
        dve.wait_ge(s.weighted, j + 1)
        wait(dve, s.projected_out, j - 1)
        nc.vector.tensor_copy(m.us[:, c % 2, :], m.mix[:, 0:256]).then_inc(s.heads_s, 1)

    def update(b, u):
        dve.wait_ge(s.projected_out, XC * (b + 1))
        nc.vector.tensor_tensor(tok(m.x, b), m.out[u][:, 0:128], tok(m.x, b), ALU.add)\
            .then_inc(s.updated, 1)

    def statistics(b):
        dve.wait_ge(s.updated, b + 1)
        nc.vector.bn_stats(m.stats[:, b, :] if isinstance(b, int) else
                           m.stats[:, bass.ds(b, 1), :].rearrange("p a k -> p (a k)"), tok(m.x, b))\
            .then_inc(s.measured, 1)

    def body(b, u):
        for c in range(XC):
            if c < XC - 1:
                probabilities(b, u, c + 1)
            elif exists(b + 1):
                probabilities(b + 1, 1 - u, 0)
            if c < XC - 2:
                maxima(b, u, c + 2)
            elif exists(b + 1):
                maxima(b + 1, 1 - u, c + 2 - XC)
            if c > 0:
                copy_heads(b, u, c - 1)
            elif exists(b - 1):
                copy_heads(b - 1, 1 - u, XC - 1)
            if c == 2 and exists(b - 1):
                update(b - 1, 1 - u)
            if c == 2 and exists(b + 2):
                normalise(b + 2, u)
            if c == 3 and exists(b - 1):
                statistics(b - 1)

    normalise(0, 0)
    normalise(1, 1)
    maxima(0, 0, 0)
    maxima(0, 0, 1)
    probabilities(0, 0, 0)
    over_sequences(dve, body)
    copy_heads(B - 1, 1, XC - 1)
    update(B - 1, 1)
    statistics(B - 1)
    dve.wait_ge(s.measured, B)


def wide_pool(pool, nc, m, s):
    def body(b, u):
        pool.wait_ge(s.normed, b + 1)
        wait(pool, s.weighted, XC * (b - 1))
        nc.gpsimd.tensor_tensor(m.xa[:], m.xn[:, u, :], m.affine[:, 0, :], ALU.mult).then_inc(s.scaled, 1)
        nc.gpsimd.tensor_tensor(m.ca[0:L], m.cs[0:L, u, :], m.affine[0:L, 2, :], ALU.mult)\
            .then_inc(s.scaled, 1)
        pool.wait_ge(s.scaled, 2 * b + 2)
        nc.gpsimd.tensor_tensor(m.kv[:, u, 0, :], m.xa[:], m.affine[:, 1, :], ALU.add).then_inc(s.latents, 1)
        nc.gpsimd.tensor_tensor(m.kv[0:L, u, 1, :], m.ca[0:L], m.affine[0:L, 3, :], ALU.add)\
            .then_inc(s.contexts, 1)
        pool.wait_ge(s.latents, b + 1)
        pool.wait_ge(s.contexts, b + 1)

    over_sequences(pool, body)


FI, FT = 384, 3
GB = 4
G = B // GB
QW = 1024
QMAX, WQMAX, QBLOCK = 32767.0, 7.0, 32
MAGIC = 1.5 * 2.0 ** 23
class FeedForwardSemaphores:
    def __init__(self, sem, stage):
        self.local_max = sem(f"{stage}_local_max")
        self.all_max = sem(f"{stage}_all_max")
        self.scaled = sem(f"{stage}_scaled")
        self.normed = sem(f"{stage}_normed")
        self.weights_q = sem(f"{stage}_weights_q")
        self.weights_t = sem(f"{stage}_weights_t")
        self.weights_s = sem(f"{stage}_weights_s")
        self.rounded = sem(f"{stage}_rounded")
        self.transposed = sem(f"{stage}_transposed")
        self.rounded_t = sem(f"{stage}_rounded_t")
        self.projected = sem(f"{stage}_projected")
        self.copied = sem(f"{stage}_copied")
        self.reduced = sem(f"{stage}_reduced")
        self.gates = sem(f"{stage}_gates")
        self.sigmoids = sem(f"{stage}_sigmoids")
        self.step = sem(f"{stage}_step")
        self.hidden = sem(f"{stage}_hidden")
        self.hidden_out = sem(f"{stage}_hidden_out")
        self.updated = sem(f"{stage}_updated")


(SX, IX, SU, FU, SG, FG, S2, F2, SO, FO) = range(10)


def quantised_weights(nc, m, link, w, sc, n_blocks):
    blocks = w.rearrange("p (n k) -> p n k", k=QBLOCK)
    s = sc[:, 0:n_blocks]
    r = sc[:, 24:24 + n_blocks]
    wide = [128, n_blocks, QBLOCK]
    link(nc.vector.tensor_reduce(s, blocks, AX.X, ALU.max, apply_absolute_value=True))
    link(nc.vector.tensor_scalar(s, s, 1.0 / WQMAX, 1e-12, ALU.mult, ALU.max))
    link(nc.vector.reciprocal(r, s))
    link(nc.vector.tensor_tensor(blocks, blocks, r.unsqueeze(2).broadcast_to(wide), ALU.mult))
    link(nc.vector.tensor_scalar(w, w, MAGIC, None, ALU.add))
    link(nc.vector.tensor_scalar(w, w, MAGIC, WQMAX, ALU.subtract, ALU.min))
    link(nc.vector.tensor_scalar(w, w, -WQMAX - 1.0, None, ALU.max))
    return nc.vector.tensor_tensor(blocks, blocks, s.unsqueeze(2).broadcast_to(wide), ALU.mult)


def ffn_vector(dve, nc, m, s, link):
    col = lambda k: m.scal[:, k:k + 1]

    def global_max(parts, n):
        nc.vector.tensor_reduce(m.lmax[:, n:n + 1], parts, AX.X, ALU.max).then_inc(s.local_max, 1)
        dve.wait_ge(s.all_max, n + 1)
        return m.gmax[:, n:n + 1]

    def scale_of(maximum, factors, k):
        link(nc.vector.tensor_scalar(m.tmp[:, 0:1], maximum, factors, None, ALU.mult))
        link(nc.vector.tensor_scalar(col(k), m.tmp[:, 0:1], 1.0 / QMAX, 1e-12, ALU.mult, ALU.max))
        link(nc.vector.reciprocal(m.tmp[:, 1:2], col(k)))
        link(nc.vector.tensor_scalar(col(k + 1), m.tmp[:, 1:2], factors, None, ALU.mult))

    with dve.Fori(0, B) as b:
        nc.vector.tensor_scalar(tok(m.xq, b), tok(m.x, b), one(m.rstd, b), one(m.shift, b),
                                ALU.mult, ALU.add).then_inc(s.normed, 1)
    dve.wait_ge(s.normed, B)
    link(nc.vector.tensor_reduce(m.amax[:, 0:8], m.xq[:].rearrange("p (n k) -> p n k", n=8), AX.X, ALU.max, apply_absolute_value=True))
    top = global_max(m.amax[:, 0:8], 0)
    scale_of(top, 1.0, SX)

    dve.wait_ge(m.s.wide_in, m.wide_loads)
    link(quantised_weights(nc, m, link, m.wug[:], m.wsc, 2 * FT * C // QBLOCK))
    quantised_weights(nc, m, link, m.wdn[:], m.wsc, FI // QBLOCK).then_inc(s.weights_q, 1)

    def round_inputs(g):
        wait(dve, s.transposed, g)
        cols = (m.xq[:, g * 512:(g + 1) * 512] if isinstance(g, int) else m.xq[:, bass.ds(g * 512, 512)])
        nc.vector.tensor_scalar(m.rq[:], cols, col(IX), MAGIC, ALU.mult, ALU.add).then_inc(s.step, 1)
        dve.wait_ge(s.step, g + 1)
        nc.vector.tensor_scalar(m.rq2[:], m.rq[:], MAGIC, None, ALU.subtract).then_inc(s.rounded, 1)

    def group_max(g):
        dve.wait_ge(s.copied, 2 * FT * (g + 1))
        for t, src in ((0, m.up), (1, m.gate)):
            view = src[:].rearrange("p (n k) -> p n k", n=FT)
            cols = view[:, :, g * 512:(g + 1) * 512] if isinstance(g, int) else view[:, :, bass.ds(g * 512, 512)]
            at = t * 32 + 3 * g
            dst = m.amax[:, at:at + FT] if isinstance(g, int) else m.amax[:, bass.ds(at, FT)]
            last = nc.vector.tensor_reduce(dst, cols, AX.X, ALU.max, apply_absolute_value=True)
        last.then_inc(s.reduced, 1)

    round_inputs(0)
    with dve.Fori(0, G - 1) as g:
        round_inputs(g + 1)
        group_max(g)
    group_max(G - 1)
    dve.wait_ge(s.reduced, G)
    top = global_max(m.amax[:, 0:FT * G], 1)
    scale_of(top, col(SX), SU)
    top = global_max(m.amax[:, 32:32 + FT * G], 2)
    scale_of(top, col(SX), SG)

    def block(t, i):
        view = t[:].rearrange("p (n k) -> p n k", n=FT)
        return view[:, :, bass.ds(i * QW, QW)]

    steps = B * C // QW
    with dve.Fori(0, steps) as i:
        n = 6 * i
        gate, up = block(m.gate, i), block(m.up, i)
        sig = m.sig[:].rearrange("p (n k) -> p n k", n=FT)
        nc.vector.tensor_scalar(gate, gate, col(FG), MAGIC, ALU.mult, ALU.add).then_inc(s.gates, 1)
        nc.vector.tensor_scalar(up, up, col(FU), MAGIC, ALU.mult, ALU.add).then_inc(s.gates, 1)
        dve.wait_ge(s.gates, n + 1)
        nc.vector.tensor_scalar(gate, gate, MAGIC, col(SG), ALU.subtract, ALU.mult).then_inc(s.gates, 1)
        dve.wait_ge(s.gates, n + 2)
        nc.vector.tensor_scalar(up, up, MAGIC, None, ALU.subtract).then_inc(s.gates, 1)
        dve.wait_ge(s.sigmoids, i + 1)
        nc.vector.tensor_scalar(sig, sig, 65536.0, MAGIC, ALU.mult, ALU.add).then_inc(s.gates, 1)
        dve.wait_ge(s.gates, n + 5)
        nc.vector.tensor_scalar(sig, sig, MAGIC, 65535.0, ALU.subtract, ALU.min).then_inc(s.gates, 1)
        dve.wait_ge(s.gates, n + 6)
        nc.vector.scalar_tensor_tensor(gate, sig, 1.0 / 65536.0, gate, ALU.mult, ALU.mult).then_inc(s.step, 1)
        dve.wait_ge(s.step, G + i + 1)
        nc.vector.tensor_reduce(m.amax[:, bass.ds(64 + i * FT, FT)], gate, AX.X, ALU.max, apply_absolute_value=True)\
            .then_inc(s.reduced, 1)
    dve.wait_ge(s.reduced, G + steps)
    top = global_max(m.amax[:, 64:64 + FT * steps], 3)
    scale_of(top, 1.0, S2)
    link(nc.vector.tensor_scalar(col(SO), col(S2), col(SU), None, ALU.mult))

    with dve.Fori(0, steps) as i:
        gate, up = block(m.gate, i), block(m.up, i)
        nc.vector.tensor_scalar(gate, gate, col(F2), MAGIC, ALU.mult, ALU.add).then_inc(s.gates, 1)
        dve.wait_ge(s.gates, 6 * steps + i + 1)
        nc.vector.scalar_tensor_tensor(gate, gate, MAGIC, up, ALU.subtract, ALU.mult).then_inc(s.step, 1)
        dve.wait_ge(s.step, G + steps + i + 1)
        nc.vector.tensor_reduce(m.amax[:, bass.ds(64 + i * FT, FT)], gate, AX.X, ALU.max, apply_absolute_value=True)\
            .then_inc(s.reduced, 1)
    dve.wait_ge(s.reduced, G + 2 * steps)
    top = global_max(m.amax[:, 64:64 + FT * steps], 4)
    link(nc.vector.tensor_copy(m.tmp[:, 4:5], col(SO)))
    scale_of(top, m.tmp[:, 4:5], SO)

    def round_hidden(i):
        gate = block(m.gate, i)
        nc.vector.tensor_scalar(gate, gate, col(FO), MAGIC, ALU.mult, ALU.add).then_inc(s.gates, 1)
        dve.wait_ge(s.gates, 7 * steps + i + 1)
        nc.vector.tensor_scalar(m.hq[:].rearrange("p (n k) -> p n k", n=FT), gate, MAGIC, None,
                                ALU.subtract).then_inc(s.hidden, 1)

    with dve.Fori(0, steps) as i:
        round_hidden(i)
        for q in range(QW // 128):
            dve.wait_ge(s.hidden_out, (QW // 128) * i + q + 1)
            x = tok(m.x, (QW // 128) * i + q)
            nc.vector.scalar_tensor_tensor(x, m.bank[q % 4][:, 0:128], col(SO), x, ALU.mult, ALU.add)\
                .then_inc(s.updated, 1)
    dve.wait_ge(s.updated, B)
    with dve.Fori(0, B) as b:
        nc.vector.bn_stats(m.stats[:, bass.ds(b, 1), :].rearrange("p a k -> p (a k)"),
                           tok(m.x, b)).then_inc(m.s.stats, 1)
    dve.wait_ge(m.s.stats, 3 * B)


def ffn_scalar(act, nc, m, s):
    act.wait_ge(s.weights_t, 1)
    nc.scalar.copy(m.wug_t[:, 0:512], m.bank[0][:])
    nc.scalar.copy(m.wug_t[:, 512:768], m.bank[1][:, 0:256])
    nc.scalar.copy(m.wdn_t[:], m.bank[2][:, 0:FI]).then_inc(s.weights_s, 1)
    with act.Fori(0, G) as g:
        act.wait_ge(s.transposed, g + 1)
        nc.scalar.copy(m.rqt[:], m.bank[6][:]).then_inc(s.rounded_t, 1)
        for t in range(2 * FT):
            act.wait_ge(s.projected, 2 * FT * g + t + 1)
            dst = (m.up if t < FT else m.gate)
            nc.scalar.copy(dst[:, bass.ds((t % FT) * B * C + g * 512, 512)], m.bank[t][:])\
                .then_inc(s.copied, 1)
    view = m.gate[:].rearrange("p (n k) -> p n k", n=FT)
    with act.Fori(0, B * C // QW) as i:
        act.wait_ge(s.gates, 6 * i + 3)
        nc.scalar.activation(m.sig[:].rearrange("p (n k) -> p n k", n=FT), view[:, :, bass.ds(i * QW, QW)],
                             ACT.Sigmoid).then_inc(s.sigmoids, 1)


def ffn_tensor(pe, nc, m, s):
    pe.wait_ge(s.weights_q, 1)
    for t in range(2 * FT):
        nc.tensor.transpose(m.bank[t // 4][:, (t % 4) * 128:(t % 4) * 128 + 128],
                            m.wug[:, t * 128:t * 128 + 128], m.ident[:])
    for t in range(FT):
        last = nc.tensor.transpose(m.bank[2][:, t * 128:t * 128 + 128], m.wdn[:, t * 128:t * 128 + 128],
                                   m.ident[:])
    last.then_inc(s.weights_t, 1)
    pe.wait_ge(s.weights_s, 1)

    def group(g):
        pe.wait_ge(s.rounded, g + 1)
        wait(pe, s.rounded_t, g)
        for q in range(GB):
            last = nc.tensor.transpose(m.bank[6][:, q * 128:q * 128 + 128], m.rq2[:, q * 128:q * 128 + 128],
                                       m.ident[:])
        last.then_inc(s.transposed, 1)
        pe.wait_ge(s.rounded_t, g + 1)
        for t in range(2 * FT):
            wait(pe, s.copied, 2 * FT * (g - 1) + t + 1)
            nc.tensor.matmul(m.bank[t][:], m.wug_t[:, t * 128:t * 128 + 128], m.rqt[:],
                             start=True, stop=True).then_inc(s.projected, 1)

    group(0)
    with pe.Fori(1, G) as g:
        group(g)
    pe.wait_ge(s.copied, 2 * FT * G)
    hq = m.hq[:].rearrange("p (n k) -> p n k", n=FT)
    per = QW // 128

    def step(i):
        pe.wait_ge(s.hidden, i + 1)
        for q in range(per):
            wait(pe, s.updated, per * i + q - 3)
            for t in range(FT):
                last = nc.tensor.matmul(m.bank[q % 4][:, 0:128], hq[:, t, q * 128:q * 128 + 128],
                                        m.wdn_t[:, t * 128:t * 128 + 128], start=t == 0, stop=t == FT - 1)
            last.then_inc(s.hidden_out, 1)

    step(0)
    with pe.Fori(1, B * C // QW) as i:
        step(i)


def ffn_pool(pool, nc, m, s):
    for n in range(5):
        pool.wait_ge(s.local_max, n + 1)
        nc.gpsimd.partition_all_reduce(m.gmax[:, n:n + 1], m.lmax[:, n:n + 1], 128,
                                       bass.bass_isa.ReduceOp.max).then_inc(s.all_max, 1)


E, EK, EG, EGK = 64, 6, 8, 4
NT = E // 2 + 1
LAG = 3
class ExpertSemaphores:
    def __init__(self, sem, stage):
        self.normed = sem(f"{stage}_normed")
        self.x_t = sem(f"{stage}_x_t")
        self.x_f = sem(f"{stage}_x_f")
        self.x_hi = sem(f"{stage}_x_hi")
        self.x_lo = sem(f"{stage}_x_lo")
        self.logits = sem(f"{stage}_logits")
        self.scores = sem(f"{stage}_scores")
        self.routed = sem(f"{stage}_routed")
        self.shares_t = sem(f"{stage}_shares_t")
        self.shares = sem(f"{stage}_shares")
        self.gated = sem(f"{stage}_gated")
        self.upped = sem(f"{stage}_upped")
        self.shared_out = sem(f"{stage}_shared_out")
        self.silus = sem(f"{stage}_silus")
        self.products = sem(f"{stage}_products")
        self.hiddens = sem(f"{stage}_hiddens")
        self.his = sem(f"{stage}_his")
        self.los = sem(f"{stage}_los")
        self.downed = sem(f"{stage}_downed")
        self.out_s = sem(f"{stage}_out_s")
        self.out_t = sem(f"{stage}_out_t")
        self.updated = sem(f"{stage}_updated")




def moe_tensor(pe, nc, m, s):
    def transpose_inputs(g):
        pe.wait_ge(s.normed, g + 1)
        for q in range(GB):
            last = nc.tensor.transpose(m.misc[:, q * 128:q * 128 + 128], m.xg[:, q, :], m.ident[:])
        last.then_inc(s.x_t, 1)

    def logits(g):
        pe.wait_ge(s.x_f, g + 1)
        for q in range(GB):
            last = nc.tensor.matmul(m.misc[:, q * E:q * E + E], m.xf[:, q * 128:q * 128 + 128],
                                    m.gate_w[:], start=True, stop=True)
        last.then_inc(s.logits, 1)

    def transpose_shares(g):
        pe.wait_ge(s.routed, g + 1)
        for q in range(GB):
            last = nc.tensor.transpose(m.misc[:, q * 128:q * 128 + 128], m.share[:, q, :].bitcast(F32),
                                       m.ident[:])
        last.then_inc(s.shares_t, 1)

    def three(bank, w_hi, w_lo, x_hi, x_lo, first=True, last=True):
        nc.tensor.matmul(bank, w_hi, x_hi, start=first, stop=False)
        nc.tensor.matmul(bank, w_hi, x_lo, start=False, stop=False)
        return nc.tensor.matmul(bank, w_lo, x_hi, start=False, stop=last)

    def project(g, u, k):
        n, tile = NT * g + k, slice(128 * k, 128 * k + 128)
        if k == 0:
            pe.wait_ge(s.x_hi, g + 1)
            pe.wait_ge(s.x_lo, g + 1)
            pe.wait_ge(s.shares, g + 1)
        wait(pe, s.silus, n - 1)
        x_hi, x_lo = m.x_hi[:, u, :], m.x_lo[:, u, :]
        three(m.gate_bank[(k + u) % 2][:], m.w_hi[:, 0, tile], m.w_lo[:, 0, tile], x_hi, x_lo)\
            .then_inc(s.gated, 1)
        wait(pe, s.products, n - 1)
        three(m.up_bank[(k + u) % 2][:], m.w_hi[:, 1, tile], m.w_lo[:, 1, tile], x_hi, x_lo)\
            .then_inc(s.upped, 1)
        if k < NT - 1:
            wait(pe, s.hiddens, n - 1)
            nc.tensor.matmul(m.share_bank[(k + u) % 2][:], m.pick[:, tile], m.share_t[:, u, :],
                             start=True, stop=True).then_inc(s.shared_out, 1)

    def project_down(g, k):
        n, tile = NT * g + k, slice(128 * k, 128 * k + 128)
        if k == 0:
            wait(pe, s.out_s, g)
        pe.wait_ge(s.los, n + 1)
        three(m.out_bank[:], m.w_hi[:, 2, tile], m.w_lo[:, 2, tile], m.h_hi[:, k % 3, :], m.h_lo[:, k % 3, :],
              first=k == 0, last=k == NT - 1).then_inc(s.downed, 1)

    def transpose_output(g):
        pe.wait_ge(s.out_s, g + 1)
        for q in range(GB):
            last = nc.tensor.transpose(m.misc[:, q * 128:q * 128 + 128], m.ys[:, q * 128:q * 128 + 128],
                                       m.ident[:])
        last.then_inc(s.out_t, 1)

    def body(g, u):
        before, after = group_exists(g - 1), group_exists(g + 1)
        for k in range(NT):
            project(g, u, k)
            if k >= LAG:
                project_down(g, k - LAG)
            elif before:
                project_down(g - 1, k - LAG + NT)
            if k == 5 and before:
                transpose_output(g - 1)
            if k == 7 and after:
                wait(pe, s.updated, GB * g)
                transpose_inputs(g + 1)
            if k == 9 and after:
                logits(g + 1)
            if k == 29 and after:
                transpose_shares(g + 1)

    transpose_inputs(0)
    logits(0)
    transpose_shares(0)
    over_groups(pe, body)
    for k in range(NT - LAG, NT):
        project_down(G - 1, k)
    transpose_output(G - 1)


def group_exists(g):
    return not isinstance(g, int) or 0 <= g < G


def over_groups(engine, body):
    body(0, 0)
    body(1, 1)
    with engine.Fori(1, G // 2 - 1) as i:
        body(2 * i, 0)
        body(2 * i + 1, 1)
    body(G - 2, 0)
    body(G - 1, 1)


def moe_scalar(act, nc, m, s):
    def copy_inputs(g):
        act.wait_ge(s.x_t, g + 1)
        wait(act, s.x_lo, g)
        nc.scalar.copy(m.xf[:], m.misc[:]).then_inc(s.x_f, 1)

    def routing_scores(g):
        act.wait_ge(s.logits, g + 1)
        nc.scalar.activation(m.sg[:], m.misc[:, 0:GB * E], ACT.Sigmoid).then_inc(s.scores, 1)

    def copy_shares(g, u):
        act.wait_ge(s.shares_t, g + 1)
        nc.scalar.copy(m.share_t[:, u, :], m.misc[:]).then_inc(s.shares, 1)

    def silu(g, u, k):
        n = NT * g + k
        act.wait_ge(s.gated, n + 1)
        wait(act, s.products, n - 1)
        nc.scalar.activation(m.sl[:, (k + u) % 2, :], m.gate_bank[(k + u) % 2][:], ACT.Silu)\
            .then_inc(s.silus, 1)

    def high_part(g, u, k):
        n = NT * g + k
        act.wait_ge(s.hiddens, n + 1)
        wait(act, s.downed, n - 2)
        nc.scalar.copy(m.h_hi[:, k % 3, :], m.h[:, (k + u) % 2, :]).then_inc(s.his, 1)

    def copy_output(g):
        act.wait_ge(s.downed, NT * (g + 1))
        nc.scalar.copy(m.ys[:], m.out_bank[:]).then_inc(s.out_s, 1)

    def body(g, u):
        before, after = group_exists(g - 1), group_exists(g + 1)
        for k in range(NT):
            if k == LAG and before:
                copy_output(g - 1)
            silu(g, u, k)
            if k > 1:
                high_part(g, u, k - 2)
            elif before:
                high_part(g - 1, 1 - u, NT - 2 + k)
            if k == 7 and after:
                copy_inputs(g + 1)
            if k == 9 and after:
                routing_scores(g + 1)
            if k == 29 and after:
                copy_shares(g + 1, 1 - u)

    copy_inputs(0)
    routing_scores(0)
    copy_shares(0, 0)
    over_groups(act, body)
    high_part(G - 1, 1, NT - 2)
    high_part(G - 1, 1, NT - 1)
    copy_output(G - 1)


ROUTE_STEPS = 16


def moe_vector(dve, nc, m, s):
    def normalise(g):
        wait(dve, s.x_t, g)
        for q in range(GB):
            b = GB * g + q
            last = nc.vector.tensor_scalar(m.xg[:, q, :], tok(m.x, b), one(m.rstd, b), one(m.shift, b),
                                           ALU.mult, ALU.add)
        last.then_inc(s.normed, 1)

    def split_inputs(g, u):
        dve.wait_ge(s.x_f, g + 1)
        nc.vector.tensor_copy(m.x_hi[:, u, :], m.xf[:]).then_inc(s.x_hi, 1)

    rows = lambda t, n: t[:].rearrange("p (q n) -> p q n", n=n)

    def wide(t, n):
        return t.unsqueeze(2).broadcast_to([128, GB, n])

    def route(g, n):
        at = ROUTE_STEPS * g + n
        wait(dve, m.s.route, at)
        if n == 0:
            dve.wait_ge(s.scores, g + 1)
            last = nc.vector.tensor_tensor(rows(m.sc, E), rows(m.sg, E),
                                           m.gate_b[:].unsqueeze(1).broadcast_to([128, GB, E]), ALU.add)
        elif n == 1:
            last = nc.vector.tensor_reduce(m.gs[:], m.sc[:].rearrange("p (n k) -> p n k", k=E // EG),
                                           AX.X, ALU.max)
        elif n == 2:
            nc.vector.memset(m.tmp[:, 7:8], 0.0)
            for q in range(GB):
                last = nc.vector.max(m.g8[:, q, :], m.gs[:, q * EG:q * EG + EG])
        elif n == 3:
            least = m.g8[:, :, EGK - 1:EGK].broadcast_to([128, GB, EG])
            nc.vector.tensor_tensor(rows(m.ga, EG), rows(m.gs, EG), least, ALU.is_gt)
            last = nc.vector.tensor_tensor(rows(m.ge, EG), rows(m.gs, EG), least, ALU.is_equal)
        elif n == 4:
            nc.vector.tensor_reduce(m.na[:], rows(m.ga, EG), AX.X, ALU.add)
            last = nc.vector.tensor_tensor_scan(m.gp[:], m.fresh_g[:], m.ge[:], 0.0, ALU.mult, ALU.add)
        elif n == 5:
            last = nc.vector.tensor_tensor(rows(m.gq, EG), rows(m.gp, EG), wide(m.na[:], EG), ALU.add)
        elif n == 6:
            last = nc.vector.scalar_tensor_tensor(m.gp[:], m.gq[:], float(EGK), m.ge[:], ALU.is_le,
                                                  ALU.mult)
        elif n == 7:
            last = nc.vector.tensor_tensor(m.gq[:], m.gp[:], m.ga[:], ALU.add)
        elif n == 8:
            spread = m.gq[:].unsqueeze(2).broadcast_to([128, GB * EG, E // EG])
            last = nc.vector.tensor_tensor(m.ms[:].rearrange("p (n k) -> p n k", k=E // EG),
                                           m.sc[:].rearrange("p (n k) -> p n k", k=E // EG), spread,
                                           ALU.mult)
        elif n == 9:
            nc.vector.memset(m.tmp[:, 7:8], 0.0)
            for q in range(GB):
                last = nc.vector.max(m.m8[:, q, :], m.ms[:, q * E:q * E + E])
        elif n == 10:
            least = m.m8[:, :, EK - 1:EK].broadcast_to([128, GB, E])
            nc.vector.tensor_tensor(rows(m.sa, E), rows(m.ms, E), least, ALU.is_gt)
            nc.vector.tensor_tensor(rows(m.se, E), rows(m.ms, E), least, ALU.is_equal)
            last = nc.vector.tensor_reduce(m.tw[:], m.m8[:, :, 0:EK], AX.X, ALU.add)
        elif n == 11:
            nc.vector.tensor_reduce(m.na[:], rows(m.sa, E), AX.X, ALU.add)
            nc.vector.tensor_scalar(m.tx[:], m.tw[:], 1e-8, None, ALU.add)
            last = nc.vector.tensor_tensor_scan(m.sp[:], m.fresh_e[:], m.se[:], 0.0, ALU.mult, ALU.add)
        elif n == 12:
            nc.vector.reciprocal(m.ty[:], m.tx[:])
            last = nc.vector.tensor_tensor(rows(m.sq, E), rows(m.sp, E), wide(m.na[:], E), ALU.add)
        elif n == 13:
            nc.vector.scalar_tensor_tensor(m.sp[:], m.sq[:], float(EK), m.se[:], ALU.is_le, ALU.mult)
            last = nc.vector.tensor_tensor(rows(m.sc, E), rows(m.ms, E), wide(m.ty[:], E), ALU.mult)
        elif n == 14:
            last = nc.vector.tensor_tensor(m.sq[:], m.sp[:], m.sa[:], ALU.add)
        elif n == 15:
            last = nc.vector.tensor_tensor(m.w[:], m.sc[:], m.sq[:], ALU.mult)
        last.then_inc(m.s.route, 1)

    def split_shares(g):
        dve.wait_ge(m.s.route, ROUTE_STEPS * (g + 1))
        wait(dve, s.shares_t, g)
        nc.vector.tensor_copy(m.share[:, :, 0:E], rows(m.w, E)).then_inc(m.s.halves, 1)
        dve.wait_ge(m.s.halves, g + 1)
        nc.vector.tensor_tensor(m.share[:, :, E:2 * E], rows(m.w, E), m.share[:, :, 0:E].bitcast(F32),
                                ALU.subtract).then_inc(s.routed, 1)

    def product(g, u, k):
        n = NT * g + k
        dve.wait_ge(s.upped, n + 1)
        dve.wait_ge(s.silus, n + 1)
        wait(dve, s.hiddens, n - 1)
        nc.vector.tensor_tensor(m.h1[:, (k + u) % 2, :], m.up_bank[(k + u) % 2][:],
                                m.sl[:, (k + u) % 2, :], ALU.mult).then_inc(s.products, 1)

    def hidden(g, u, k):
        n = NT * g + k
        dve.wait_ge(s.products, n + 1)
        wait(dve, s.los, n - 1)
        here = (k + u) % 2
        if k < NT - 1:
            dve.wait_ge(s.shared_out, (NT - 1) * g + k + 1)
            nc.vector.tensor_tensor(m.h[:, here, :], m.share_bank[here][:], m.h1[:, here, :], ALU.mult)\
                .then_inc(s.hiddens, 1)
        else:
            nc.vector.tensor_copy(m.h[:, here, :], m.h1[:, here, :]).then_inc(s.hiddens, 1)

    def update(g):
        dve.wait_ge(s.out_t, g + 1)
        for q in range(GB):
            x = tok(m.x, GB * g + q)
            nc.vector.tensor_tensor(x, m.misc[:, q * 128:q * 128 + 128], x, ALU.add)\
                .then_inc(s.updated, 1)

    def body(g, u):
        before, after = group_exists(g - 1), group_exists(g + 1)
        for k in range(NT):
            product(g, u, k)
            if k > 0:
                hidden(g, u, k - 1)
            elif before:
                hidden(g - 1, 1 - u, NT - 1)
            if k == 2 and after:
                normalise(g + 1)
            if k == 6 and before:
                update(g - 1)
            if k == 8 and after:
                split_inputs(g + 1, 1 - u)
            if 11 <= k < 11 + ROUTE_STEPS and after:
                route(g + 1, k - 11)
            if k == 27 and after:
                split_shares(g + 1)

    normalise(0)
    split_inputs(0, 0)
    for n in range(ROUTE_STEPS):
        route(0, n)
    split_shares(0)
    over_groups(dve, body)
    hidden(G - 1, 1, NT - 1)
    update(G - 1)


def moe_pool(pool, nc, m, s):
    def split_inputs(g, u):
        pool.wait_ge(s.x_hi, g + 1)
        wait(pool, s.logits, g + 1)
        nc.gpsimd.tensor_tensor(m.x_lo[:, u, :], m.xf[:], m.x_hi[:, u, :].bitcast(F32), ALU.subtract)\
            .then_inc(s.x_lo, 1)

    def low_part(g, u, k):
        n = NT * g + k
        pool.wait_ge(s.his, n + 1)
        nc.gpsimd.tensor_tensor(m.h_lo[:, k % 3, :], m.h[:, (k + u) % 2, :],
                                m.h_hi[:, k % 3, :].bitcast(F32), ALU.subtract).then_inc(s.los, 1)

    def body(g, u):
        for k in range(NT):
            if k > 0:
                low_part(g, u, k - 1)
            elif group_exists(g - 1):
                low_part(g - 1, 1 - u, NT - 1)
            if k == 10 and group_exists(g + 1):
                split_inputs(g + 1, 1 - u)

    split_inputs(0, 0)
    over_groups(pool, body)
    low_part(G - 1, 1, NT - 1)


class Chain:

    def __init__(self, dve, semaphore):
        self.dve, self.semaphore, self.count = dve, semaphore, 0

    def __call__(self, instruction):
        self.count += 1
        instruction.then_inc(self.semaphore, 1)
        self.dve.wait_ge(self.semaphore, self.count)


def inverse_root(nc, m, s, link, n, value, out, p):
    dve = link.dve
    dve.wait_ge(s.rooted, n)
    link(nc.vector.reciprocal(m.r0[0:p], m.root[0:p]))
    link(nc.vector.tensor_tensor(m.t0[0:p], m.r0[0:p], m.r0[0:p], ALU.mult))
    link(nc.vector.tensor_tensor(m.t0[0:p], m.t0[0:p], value, ALU.mult))
    link(nc.vector.tensor_scalar(m.t0[0:p], m.t0[0:p], -0.5, 1.5, ALU.mult, ALU.add))
    link(nc.vector.tensor_tensor(out, m.r0[0:p], m.t0[0:p], ALU.mult))


def norm_vector(nc, m, s, link, n, stats, rstd, shift, p=128):
    st = stats[0:p]
    link(nc.vector.tensor_tensor(m.t0[0:p], st[:, :, 1], st[:, :, 4], ALU.subtract))
    link(nc.vector.tensor_tensor(m.t0[0:p], m.t0[0:p], m.t0[0:p], ALU.mult))
    link(nc.vector.tensor_tensor(m.t1[0:p], st[:, :, 2], st[:, :, 5], ALU.add))
    link(nc.vector.tensor_scalar(m.t1[0:p], m.t1[0:p], 1.0 / C, None, ALU.mult))
    link(nc.vector.scalar_tensor_tensor(m.var[0:p], m.t0[0:p], 0.25, m.t1[0:p], ALU.mult, ALU.add))
    nc.vector.tensor_scalar(m.vare[0:p], m.var[0:p], EPS, None, ALU.add).then_inc(s.to_root, 1)
    inverse_root(nc, m, s, link, n, m.vare[0:p], rstd[0:p], p)
    link(nc.vector.tensor_tensor(m.t0[0:p], st[:, :, 1], st[:, :, 4], ALU.add))
    link(nc.vector.scalar_tensor_tensor(shift[0:p], m.t0[0:p], -0.5, rstd[0:p], ALU.mult, ALU.mult))


def renorm_vector(nc, m, s, link, n):
    link(nc.vector.tensor_tensor(m.t0[:], m.rstd[:], m.rstd[:], ALU.mult))
    link(nc.vector.tensor_tensor(m.t0[:], m.t0[:], m.var[:], ALU.mult))
    nc.vector.tensor_scalar(m.vare[:], m.t0[:], EPS, None, ALU.add).then_inc(s.to_root, 1)
    inverse_root(nc, m, s, link, n, m.vare[:], m.t1[:], 128)
    link(nc.vector.tensor_tensor(m.rstd[:], m.rstd[:], m.t1[:], ALU.mult))
    link(nc.vector.tensor_tensor(m.shift[:], m.shift[:], m.t1[:], ALU.mult))


def root_scalar(act, nc, m, s, n, p=128):
    act.wait_ge(s.to_root, n)
    nc.scalar.activation(m.root[0:p], m.vare[0:p], ACT.Sqrt).then_inc(s.rooted, 1)


def program(nc, io, out):
    arena = ExitStack()
    with arena:
        def sem(name):
            return arena.enter_context(nc.semaphore(name))

        def placer(stack):
            def sb(name, shape, dtype=F32):
                return stack.enter_context(nc.sbuf_tensor(name, shape, dtype))
            return sb

        m = Names()
        sb = placer(arena)

        m.x = sb("x", [128, B * C])
        m.stats = sb("stats", [128, B, 6])
        m.cstats = sb("cstats", [128, B, 6])
        m.rstd = sb("rstd", [128, B])
        m.shift = sb("shift", [128, B])
        m.crstd = sb("crstd", [128, B])
        m.cshift = sb("cshift", [128, B])
        m.var = sb("var", [128, B])
        m.vare = sb("vare", [128, B])
        m.root = sb("root", [128, B])
        m.r0 = sb("r0", [128, B])
        m.t0 = sb("t0", [128, B])
        m.t1 = sb("t1", [128, B])
        m.ident = sb("ident", [128, 128])
        m.ident_b = sb("ident_b", [128, 128], BF16)
        m.causal = sb("causal", [128, HC * T], BF16)
        m.own_rows = sb("own_rows", [128, HC])
        m.xn = sb("xn", [128, 2, C])
        m.cs = sb("cs", [128, 2, C])
        m.nmax = sb("nmax", [128, 2, HC])
        m.sums = sb("sums", [128, 2, H])
        m.w0 = sb("w0", [128, 3 * C])
        m.w0o = sb("w0o", [128, C])
        m.w3 = sb("w3", [128, 3 * C])
        m.w3o = sb("w3o", [128, C])
        m.w4q = sb("w4q", [128, C])
        m.w4kv = sb("w4kv", [128, 2 * C])
        m.w4o = sb("w4o", [128, C])
        m.bases = sb("bases", [128, 3, C])
        m.cols = sb("cols", [128, 7])
        m.scal = sb("scal", [128, 10])
        m.tmp = sb("tmp", [128, 8])
        m.lmax = sb("lmax", [128, 5])
        m.gmax = sb("gmax", [128, 5])
        m.amax = sb("amax", [128, 96])
        m.gate_w = sb("gate_w", [128, E])
        m.gate_b = sb("gate_b", [128, E])
        m.fresh_e = sb("fresh_e", [128, GB * E])
        m.fresh_g = sb("fresh_g", [128, GB * EG])
        with ExitStack() as part:
            over = placer(part)
            m.wq_t = over("wq_t", [XD, XH, C])
            m.wk_t = over("wk_t", [XD, XH, C])
            m.wv_t = over("wv_t", [XD, XH, C])
            m.wo_r = over("wo_r", [XD, XH, C])
            m.ctx = over("ctx", [128, B * C])
            m.affine = over("affine", [128, 4, C])
        with ExitStack() as part:
            over = placer(part)
            m.up = over("up", [128, FT * B * T])
            m.gate = over("gate", [128, FT * B * T])
        m.w_hi = sb("w_hi", [128, 3, NT * 128], F32R)
        m.w_lo = sb("w_lo", [128, 3, NT * 128], F32R)
        with ExitStack() as part:
            over = placer(part)
            m.xq = over("xq", [128, B * C])
        with ExitStack() as part:
            over = placer(part)
            m.pick = over("pick", [128, (NT - 1) * 128], F32R)
        m.score_w = sb("score_w", [128, XH, C])
        m.out_w = sb("out_w", [128, XH, C])
        with ExitStack() as part:
            over = placer(part)
            m.raw = over("raw", [128, 2, 4, 128])
        m.wug = sb("wug", [128, 2 * FT * C])
        m.wdn = sb("wdn", [128, FI])
        with ExitStack() as part:
            over = placer(part)
            m.sa = over("sa", [128, GB * E])
            m.se = over("se", [128, GB * E])
            m.sp = over("sp", [128, GB * E])
            m.sq = over("sq", [128, GB * E])
        m.alibi = sb("alibi", [128, H * T], BF16)
        with ExitStack() as part:
            over = placer(part)
            m.kv = over("kv", [128, 2, 2, C])
            m.kvt = over("kvt", [128, 2, 256])
            m.qs = over("qs", [128, 2, 256])
            m.ew = over("ew", [128, 2, 2, KW])
            m.rw = over("rw", [128, 2, 2])
            m.pw = over("pw", [128, 2, 2, 256])
            m.pwt = over("pwt", [128, 2, 512])
            m.us = over("us", [128, 2, 256])
            m.xa = over("xa", [128, C])
            m.ca = over("ca", [128, C])
        with ExitStack() as part:
            over = placer(part)
            m.sig = over("sig", [128, FT * QW])
            m.rq = over("rq", [128, 512])
            m.rq2 = over("rq2", [128, 512])
            m.rqt = over("rqt", [128, 512])
            m.wug_t = over("wug_t", [128, 2 * FT * C])
            m.wdn_t = over("wdn_t", [128, FI])
            m.wsc = over("wsc", [128, 48])
        with ExitStack() as part:
            over = placer(part)
            m.xg = over("xg", [128, GB, C])
            m.xf = over("xf", [128, 512])
            m.x_hi = over("x_hi", [128, 2, 512], F32R)
            m.x_lo = over("x_lo", [128, 2, 512], F32R)
            m.share_t = over("share_t", [128, 2, 512], F32R)
            m.share = over("share", [128, GB, 2 * E], F32R)
            m.sl = over("sl", [128, 2, 512])
            m.h1 = over("h1", [128, 2, 512])
            m.h = over("h", [128, 2, 512])
            m.h_hi = over("h_hi", [128, 3, 512], F32R)
            m.h_lo = over("h_lo", [128, 3, 512], F32R)
            m.ys = over("ys", [128, 512])
            m.sg = over("sg", [128, GB * E])
            m.sc = over("sc", [128, GB * E])
            m.ms = over("ms", [128, GB * E])
            m.w = over("w", [128, GB * E])
            m.gs = over("gs", [128, GB * EG])
            m.ga = over("ga", [128, GB * EG])
            m.ge = over("ge", [128, GB * EG])
            m.gp = over("gp", [128, GB * EG])
            m.gq = over("gq", [128, GB * EG])
            m.g8 = over("g8", [128, GB, 8])
            m.m8 = over("m8", [128, GB, 8])
            m.na = over("na", [128, GB])
            m.tw = over("tw", [128, GB])
            m.tx = over("tx", [128, GB])
            m.ty = over("ty", [128, GB])
        m.kx = sb("kx", [128, 2, H, 128])
        m.vx = sb("vx", [128, 2, H * VSTEP])
        m.xt = sb("xt", [128, 2, 256])
        m.q = sb("q", [128, 2, T])
        m.p = sb("p", [128, 2, HC, 128])
        m.pt = sb("pt", [128, 2, HC, 128])
        m.rx = sb("rx", [128, C])
        m.rs = sb("rs", [128, 2, T])
        m.ot1 = sb("ot1", [128, T])
        m.ot = sb("ot", [128, 2, T])
        m.v0 = sb("v0", [128, 2])
        m.hq = m.sig

        m.bank = bank = [arena.enter_context(nc.psum_tensor(f"bank{i}", [128, 512], F32)) for i in range(8)]
        m.score, m.flip, m.out, m.front = bank[0:2], bank[2:4], bank[4:6], bank[6]
        m.ask, m.mix = bank[3], bank[7]
        m.gate_bank, m.up_bank, m.share_bank, m.out_bank, m.misc = bank[0:2], bank[2:4], bank[4:6], bank[6], bank[7]

        m.s, m.es = Names(), Names()
        m.s.loaded = sem("all_loaded")
        m.s.weights = sem("all_weights")
        m.s.wide_in = sem("all_wide_in")
        m.s.ctx_in = sem("all_ctx_in")
        m.s.stats = sem("all_stats")
        m.s.to_root = sem("all_to_root")
        m.s.rooted = sem("all_rooted")
        m.s.chain = sem("all_chain")
        m.s.zeros = sem("all_zeros")
        m.s.route = sem("all_route")
        m.s.halves = sem("all_halves")
        m.s.stored = sem("all_stored")
        m.es.split_hi, m.es.split = sem("experts_split_hi"), sem("experts_split")
        m.es.raw = [sem("experts_raw0"), sem("experts_raw1")]
        s0, s3, s4 = (AttentionSemaphores(sem, n) for n in ("attn0", "attn1", "cross"))
        s1, s2, s5 = WideSemaphores(sem, "wide"), FeedForwardSemaphores(sem, "ffn"), ExpertSemaphores(sem, "moe")
        s4.copied = [sem("cross_copied0"), sem("cross_copied1")]

        col = lambda k: m.cols[:, k:k + 1]
        attn0 = Attention(
            keys=T, cross=False, first_value=False, split_weights=False,
            mask=lambda c: m.alibi[:, 512 * c:512 * c + 512],
            wq=m.w0[:, 0:128], wk=m.w0[:, 128:256], wv=m.w0[:, 256:384], wo=m.w0o[:],
            bq=col(0), bk=col(1), bv=col(2), base=m.bases[:, 0, :])
        attn1 = Attention(
            keys=T, cross=False, first_value=True, split_weights=True, mask=lambda c: m.causal[:],
            wq=m.w3[:, 0:128], wk=m.w3[:, 128:256], wv=m.w3[:, 256:384], wo=m.w3o[:],
            bq=col(6), bk=col(6), bv=None, base=m.bases[:, 1, :])
        cross = Attention(
            keys=L, cross=True, first_value=False, split_weights=False, mask=None,
            wq=m.w4q[:], wk=m.w4kv[:, 0:128], wv=m.w4kv[:, 128:256], wo=m.w4o[:],
            bq=col(3), bk=col(4), bv=col(5), base=m.bases[:, 2, :])

        def row(name, p=128):
            return io[name].rearrange("(a c) -> a c", a=1).broadcast_to([p, io[name].shape[0]])

        tiles = lambda a: a.rearrange("(n p) c -> p n c", p=128)
        heads = lambda a: a.rearrange("(n p) c -> p n c", p=XD)
        first_loads = [
            (m.w0[:], io["L0_attn_W_attn"]), (m.w0o[:], io["L0_attn_W_proj"]), (m.ident[:], io["identity"]),
            (m.ident_b[:], io["identity_b"]), (m.alibi[:], io["alibi"]), (m.own_rows[:], io["own_rows"]),
            (m.cols[:, 0:6], io["bias_columns"]), (m.bases[:, 0, :], row("L0_attn_b_proj"))]
        m.weights_in = 16 * len(first_loads)
        later_loads = [
            (m.wq_t[:], heads(io["wide_wq_t"])), (m.wk_t[:], heads(io["wide_wkv_t"][0:XH * XD])),
            (m.wv_t[:], heads(io["wide_wkv_t"][XH * XD:2 * XH * XD])), (m.wo_r[:], heads(io["L0_xattn_Wo"])),
            (m.affine[:, 0, :], row("L0_xattn_ln2_w")), (m.affine[:, 1, :], row("L0_xattn_ln2_b")),
            (m.affine[:, 2, :], row("L0_xattn_ln1_w")), (m.affine[:, 3, :], row("L0_xattn_ln1_b")),
            (m.wug[:, 0:FI].rearrange("p (n c) -> p n c", c=C), tiles(io["L0_ffn_w_up"])),
            (m.wug[:, FI:2 * FI].rearrange("p (n c) -> p n c", c=C), tiles(io["L0_ffn_w_gate"])),
            (m.wdn[:], io["L0_ffn_w_down"]), (m.causal[:], io["causal"]), (m.w3[:], io["attn1_wqkv_t"]),
            (m.w3o[:], io["attn1_wout_t"]), (m.bases[:, 1, :], row("L1_attn_b_out")),
            (m.w4q[:], io["L1_xattn_Wq"]), (m.w4kv[:], io["L1_xattn_Wkv"]), (m.w4o[:], io["L1_xattn_Wproj"]),
            (m.bases[:, 2, :], row("L1_xattn_bproj")), (m.gate_w[:], io["moe_gate_t"]),
            (m.gate_b[:], row("L1_ffn_gate_bias")), (m.fresh_e[:], io["fresh_experts"]),
            (m.fresh_g[:], io["fresh_groups"])]
        m.wide_loads = 16 * len(later_loads)
        x_parts = 4
        per = B // x_parts

        with nc.Block() as block:
            @block.sync
            def _(sp):
                x_view = m.x[:].rearrange("t (b c) -> t b c", c=C)
                for k in range(x_parts):
                    sp.dma_start(x_view[:, k * per:(k + 1) * per, :],
                                 io["x"][k * per:(k + 1) * per].rearrange("b t c -> t b c"))\
                        .then_inc(m.s.loaded, 16)
                    for dst, src in first_loads[k::x_parts]:
                        sp.dma_start(dst, src).then_inc(m.s.weights, 16)
                sp.dma_start(m.ctx[0:L, :].rearrange("t (b c) -> t b c", c=C),
                             io["ctx_1024"].rearrange("b t c -> t b c")).then_inc(m.s.ctx_in, 16)
                for dst, src in later_loads:
                    sp.dma_start(dst, src).then_inc(m.s.wide_in, 16)

                def load_experts(k, u):
                    wait(sp, m.es.split, k - 1)
                    src = io["experts"][k] if isinstance(k, int) else io["experts"][bass.ds(k, 1)].rearrange("a p n c -> p (a n) c")
                    sp.dma_start(m.raw[:, u, :, :], src).then_inc(m.es.raw[u], 16)

                sp.wait_ge(s2.weights_t, 1)
                over_sequences(sp, load_experts)
                load_experts(B, 0)

                def load_context(b, u):
                    wait(sp, s4.transposed, b - 1)
                    src = io["ctx_1024"][b] if isinstance(b, int) else io["ctx_1024"][bass.ds(b, 1)].rearrange("a t c -> t (a c)")
                    sp.dma_start(m.cs[0:L, u, :], src).then_inc(s4.copied[u], 16)

                sp.wait_ge(s3.updated, B)
                over_sequences(sp, load_context)
                with sp.Fori(0, G) as g:
                    sp.wait_ge(s5.updated, GB * g + GB)
                    sp.dma_start(out[bass.ds(g * GB, GB)].rearrange("b t c -> t b c"),
                                 x_view[:, bass.ds(g * GB, GB), :]).then_inc(m.s.stored, 16)
                sp.wait_ge(m.s.stored, 16 * G)

            @block.gpsimd
            def _(pool):
                for t in (m.kx, m.vx, m.p, m.cs):
                    nc.gpsimd.memset(t[:], 0.0).then_inc(m.s.zeros, 1)
                pool.wait_ge(m.s.weights, m.weights_in)
                pool.wait_ge(m.s.loaded, 16 * x_parts)
                attention_pool(pool, nc, m, s0, attn0)
                pool.wait_ge(s0.updated, B)
                for t in (m.kv, m.pw):
                    nc.gpsimd.memset(t[:], 0.0).then_inc(m.s.zeros, 1)
                pool.wait_ge(m.s.zeros, 6)
                pool.wait_ge(m.s.wide_in, m.wide_loads)
                wide_pool(pool, nc, m, s1)
                ffn_pool(pool, nc, m, s2)
                pool.wait_ge(s2.updated, B)
                for t in (m.kx, m.vx):
                    nc.gpsimd.memset(t[:], 0.0).then_inc(m.s.zeros, 1)
                attention_pool(pool, nc, m, s3, attn1)
                split_experts(pool, nc, m, m.es, B, 0)
                pool.wait_ge(s3.updated, B)
                nc.gpsimd.memset(m.p[:], 0.0).then_inc(m.s.zeros, 1)
                attention_pool(pool, nc, m, s4, cross)
                moe_pool(pool, nc, m, s5)

            @block.scalar
            def _(act):
                root_scalar(act, nc, m, m.s, 1)
                root_scalar(act, nc, m, m.s, 2, L)
                act.wait_ge(m.s.zeros, 4)
                attention_scalar(act, nc, m, s0, attn0)
                root_scalar(act, nc, m, m.s, 3)
                root_scalar(act, nc, m, m.s, 4)
                wide_scalar(act, nc, m, s1)
                root_scalar(act, nc, m, m.s, 5)
                ffn_scalar(act, nc, m, s2)
                root_scalar(act, nc, m, m.s, 6)
                attention_scalar(act, nc, m, s3, attn1)
                root_scalar(act, nc, m, m.s, 7)
                act.wait_ge(m.s.zeros, 9)
                attention_scalar(act, nc, m, s4, cross)
                root_scalar(act, nc, m, m.s, 8)
                moe_scalar(act, nc, m, s5)

            @block.vector
            def _(dve):
                link = Chain(dve, m.s.chain)
                dve.wait_ge(m.s.loaded, 16 * x_parts)
                with dve.Fori(0, B) as b:
                    nc.vector.bn_stats(m.stats[:, bass.ds(b, 1), :].rearrange("p a k -> p (a k)"),
                                       tok(m.x, b)).then_inc(m.s.stats, 1)
                dve.wait_ge(m.s.ctx_in, 16)
                with dve.Fori(0, B) as b:
                    nc.vector.bn_stats(m.cstats[0:L, bass.ds(b, 1), :].rearrange("p a k -> p (a k)"),
                                       tok(m.ctx, b)[0:L]).then_inc(m.s.stats, 1)
                dve.wait_ge(m.s.stats, 2 * B)
                norm_vector(nc, m, m.s, link, 1, m.stats, m.rstd, m.shift)
                norm_vector(nc, m, m.s, link, 2, m.cstats, m.crstd, m.cshift, L)
                nc.vector.memset(m.cols[:, 6:7], 0.0)
                dve.wait_ge(m.s.weights, m.weights_in)
                dve.wait_ge(m.s.zeros, 4)
                attention_vector(dve, nc, m, s0, attn0)
                norm_vector(nc, m, m.s, link, 3, m.stats, m.rstd, m.shift)
                renorm_vector(nc, m, m.s, link, 4)
                dve.wait_ge(m.s.zeros, 6)
                wide_vector(dve, nc, m, s1)
                norm_vector(nc, m, m.s, link, 5, m.stats, m.rstd, m.shift)
                ffn_vector(dve, nc, m, s2, link)
                norm_vector(nc, m, m.s, link, 6, m.stats, m.rstd, m.shift)
                dve.wait_ge(m.s.zeros, 8)
                attention_vector(dve, nc, m, s3, attn1)
                norm_vector(nc, m, m.s, link, 7, m.stats, m.rstd, m.shift)
                attention_vector(dve, nc, m, s4, cross)
                norm_vector(nc, m, m.s, link, 8, m.stats, m.rstd, m.shift)
                moe_vector(dve, nc, m, s5)

            @block.tensor
            def _(pe):
                pe.wait_ge(m.s.weights, m.weights_in)
                pe.wait_ge(m.s.zeros, 4)
                attention_tensor(pe, nc, m, s0, attn0)
                pe.wait_ge(m.s.wide_in, m.wide_loads)
                wide_tensor(pe, nc, m, s1)
                ffn_tensor(pe, nc, m, s2)
                attention_tensor(pe, nc, m, s3, attn1)
                attention_tensor(pe, nc, m, s4, cross)
                pe.wait_ge(m.es.split, B + 1)
                moe_tensor(pe, nc, m, s5)


def constants():
    eye = np.eye(128, dtype=np.float32)
    at = np.arange(T)
    rel = (at[None, :] - at[:, None]).astype(np.float32)
    slope = 2.0 ** -np.arange(1, H + 1, dtype=np.float32)
    future = rel > 0
    alibi = np.where(future[:, None, :], np.float32(MASKED), rel[:, None, :] * slope[None, :, None])
    causal = np.repeat(np.where(future, np.float32(MASKED), np.float32(0))[:, None, :], HC, 1)
    own = (np.arange(128)[:, None] % 32 // D == np.arange(HC)[None, :]).astype(np.float32)

    def fresh(n):
        return np.tile((np.arange(GB * n) % n != 0).astype(np.float32), (128, 1))

    bf = mybir.dt.np(BF16)
    return {"identity": eye, "identity_b": eye.astype(bf), "alibi": alibi.reshape(T, -1).astype(bf),
            "causal": causal.reshape(T, -1).astype(bf), "own_rows": own,
            "fresh_experts": fresh(E), "fresh_groups": fresh(EG)}


def layouts(w):
    def columns(name):
        return w[name].reshape(-1, 128).T

    def up(a, shared):
        return np.concatenate([a.reshape(E // 2, 128, C), shared[None]]).transpose(0, 2, 1)

    down = np.concatenate([w["L1_ffn_ed_w"].reshape(E // 2, 2, C, 64).transpose(0, 1, 3, 2).reshape(E // 2, 128, C),
                           w["L1_ffn_sd_w"].T[None]])
    expert = 2 * np.arange(NT)[:, None] + np.arange(128)[None, :] // 64
    pick = (np.arange(128)[None, :, None] % E == expert[:, None, :]).astype(np.float32)
    experts = np.stack([up(w["L1_ffn_eg_w"], w["L1_ffn_sg_w"]), up(w["L1_ffn_eu_w"], w["L1_ffn_su_w"]),
                        down, pick], 2)
    out = {"bias_columns": np.concatenate([columns("L0_attn_b_attn"), columns("L1_xattn_bq"),
                                           columns("L1_xattn_bkv")], 1),
           "wide_wq_t": w["L0_xattn_Wq"].T, "wide_wkv_t": w["L0_xattn_Wkv"].T,
           "attn1_wqkv_t": w["L1_attn_w_qkv"].T, "attn1_wout_t": w["L1_attn_w_out"].T,
           "moe_gate_t": w["L1_ffn_gate_w"].T, "experts": experts}
    return {n: np.ascontiguousarray(a) for n, a in out.items()}


USED_AS_GIVEN = ("x", "ctx_1024", "L0_attn_W_attn", "L0_attn_W_proj", "L0_attn_b_proj", "L0_xattn_Wo",
                 "L0_xattn_ln1_w", "L0_xattn_ln1_b", "L0_xattn_ln2_w", "L0_xattn_ln2_b", "L0_ffn_w_up",
                 "L0_ffn_w_gate", "L0_ffn_w_down", "L1_attn_b_out", "L1_xattn_Wq", "L1_xattn_Wkv",
                 "L1_xattn_Wproj", "L1_xattn_bproj", "L1_ffn_gate_bias")


def kernel(**inputs):
    import concourse.bacc as bacc
    from concourse.bass_utils import run_bass_kernel_spmd

    nc = bacc.Bacc("TRN2", target_bir_lowering=False, num_devices=1)
    given = {n: np.ascontiguousarray(a) for n, a in inputs.items()}
    arrays = {n: given[n] for n in USED_AS_GIVEN}
    arrays.update(layouts(given))
    arrays.update(constants())
    arrays = {f"in_{n}": a for n, a in arrays.items()}
    io = {n[3:]: nc.dram_tensor(n, a.shape, mybir.dt.from_np(a.dtype), kind="ExternalInput").ap()
          for n, a in arrays.items()}
    out = nc.dram_tensor("out_dram", (B, T, C), F32, kind="ExternalOutput").ap()
    program(nc, io, out)
    return run_bass_kernel_spmd(nc, [arrays], core_ids=[0]).results[0]["out_dram"]
```

```python
from contextlib import ExitStack

import concourse.bass as bass
import numpy as np
from concourse import mybir

F32 = mybir.dt.float32
BF16 = mybir.dt.bfloat16
F32R = mybir.dt.float32r
ALU = mybir.AluOpType
ACT = mybir.ActivationFunctionType
AX = mybir.AxisListType

B, T, C, L = 32, 128, 128, 77
H, D = 16, 8
HC, NC = 4, 4
XH, XD = 16, 64
XC = XH // 2
POOL_STEPS = 7
VSTEP = 128 + D
EPS = 1e-5
MASKED = -1e30


class Names:
    pass


def wait(engine, semaphore, value):
    if not isinstance(value, int) or value > 0:
        engine.wait_ge(semaphore, value)


def exists(b):
    return not isinstance(b, int) or 0 <= b < B


def over_sequences(engine, body):
    body(0, 0)
    body(1, 1)
    with engine.Fori(1, B // 2 - 1) as i:
        body(2 * i, 0)
        body(2 * i + 1, 1)
    body(B - 2, 0)
    body(B - 1, 1)


def tok(t, b):
    if isinstance(b, int):
        return t[:, b * 128:(b + 1) * 128]
    return t[:, bass.ds(b * 128, 128)]


def one(t, b, p=128):
    if isinstance(b, int):
        return t[0:p, b:b + 1]
    return t[0:p, bass.ds(b, 1)]


class Attention:
    def __init__(self, keys, cross, first_value, split_weights, measures_context, mask, wq, wk, wv, wo, bq, bk, bv, base):
        self.keys, self.cross, self.first_value, self.split_weights = keys, cross, first_value, split_weights
        self.measures_context = measures_context
        self.columns = keys + keys % 2
        self.mask, self.wq, self.wk, self.wv, self.wo = mask, wq, wk, wv, wo
        self.bq, self.bk, self.bv, self.base = bq, bk, bv, base


class AttentionSemaphores:
    def __init__(self, sem, stage):
        self.normed = sem(f"{stage}_normed")
        self.based = sem(f"{stage}_based")
        self.transposed = sem(f"{stage}_transposed")
        self.inputs_t = sem(f"{stage}_inputs_t")
        self.projected = sem(f"{stage}_projected")
        self.keys = sem(f"{stage}_keys")
        self.values = sem(f"{stage}_values")
        self.scores = sem(f"{stage}_scores")
        self.maxed = sem(f"{stage}_maxed")
        self.exped = sem(f"{stage}_exped")
        self.probs_t = sem(f"{stage}_probs_t")
        self.probs_s = sem(f"{stage}_probs_s")
        self.weighted = sem(f"{stage}_weighted")
        self.recips = sem(f"{stage}_recips")
        self.recips_t = sem(f"{stage}_recips_t")
        self.recips_s = sem(f"{stage}_recips_s")
        self.heads_out = sem(f"{stage}_heads_out")
        self.projected_out = sem(f"{stage}_projected_out")
        self.updated = sem(f"{stage}_updated")
        self.own = sem(f"{stage}_own")
        self.keys_s = sem(f"{stage}_keys_s")




def attention_tensor(pe, nc, m, s, a):
    def transpose_inputs(b, u):
        pe.wait_ge(s.normed, b + 1)
        wait(pe, s.keys, NC * b)
        last = nc.tensor.transpose(m.front[:, 0:128], m.xn[:, u, :], m.ident[:])
        if a.cross:
            pe.wait_ge(s.copied[u], 16 + 8 * (b - u))
            last = nc.tensor.transpose(m.front[:, 128:256], m.cs[:, u, :], m.ident[:])
        last.then_inc(s.transposed, 1)

    def project(b, u):
        pe.wait_ge(s.inputs_t, b + 1)
        x_t = m.xt[:, u, 0:128]
        kv_t = m.xt[:, u, 128:256] if a.cross else x_t
        nc.tensor.matmul(m.front[:, 128:256], a.wq, x_t, start=True, stop=True)
        nc.tensor.matmul(m.front[:, 256:384], a.wk, kv_t, start=True, stop=True)
        last = nc.tensor.matmul(m.front[:, 384:512], kv_t, a.wv, start=True, stop=True)
        if a.first_value:
            last = nc.tensor.matmul(m.front[:, 0:1], a.wv, m.xt[:, u, 0:1], start=True, stop=True)
        last.then_inc(s.projected, 1)

    def scores(b, u, c):
        j = NC * b + c
        pe.wait_ge(s.keys, j + 1)
        pe.wait_ge(s.based, POOL_STEPS * b + 3 + c)
        wait(pe, s.exped, j - 1)
        bank = m.score[c % 2][:, 0:HC * a.columns]
        if a.mask is not None:
            nc.tensor.matmul(bank, m.ident_b[:], a.mask(c), start=True, stop=False)
        heads = slice(HC * c, HC * c + HC)
        k_hi, k_lo = m.kx[:, heads, 0:a.columns], m.kx_lo[:, heads, 0:a.columns]
        nc.tensor.matmul(bank, m.q_hi[:, u, :], k_hi, start=a.mask is None, stop=False)
        nc.tensor.matmul(bank, m.q_lo[:, u, :], k_hi, start=False, stop=False)
        nc.tensor.matmul(bank, m.q_hi[:, u, :], k_lo, start=False, stop=True).then_inc(s.scores, 1)

    def transpose_probs(b, u, c):
        j = NC * b + c
        pe.wait_ge(s.exped, j + 1)
        wait(pe, s.probs_s, j - 1)
        for h in range(HC):
            last = nc.tensor.transpose(m.flip[c % 2][:, h * 128:h * 128 + 128], m.p[:, c % 2, h, :],
                                       m.ident[:])
        last.then_inc(s.probs_t, 1)

    def weigh(b, u, c):
        j = NC * b + c
        if c == 0:
            pe.wait_ge(s.values, b + 1)
            wait(pe, s.updated, b - 1)
        pe.wait_ge(s.probs_s, j + 1)
        for h in range(HC):
            g = HC * c + h
            last = nc.tensor.matmul(m.out[u][:, 0:128], m.vx[:, u, g * 128:g * 128 + 128],
                                    m.pt[:, c % 2, h, :], start=g == 0, stop=g == H - 1)
        last.then_inc(s.weighted, 1)

    def transpose_recips(b, u):
        pe.wait_ge(s.recips, b + 1)
        nc.tensor.transpose(m.out[u][:, 128:256], m.rx[:], m.ident[:]).then_inc(s.recips_t, 1)

    def project_out(b, u):
        pe.wait_ge(s.heads_out, b + 1)
        nc.tensor.matmul(m.out[u][:, 256:384], m.ot[:, u, :], a.wo, start=True, stop=True)\
            .then_inc(s.projected_out, 1)

    def body(b, u):
        for c in range(NC):
            transpose_probs(b, u, c)
            if c == 0 and exists(b + 1):
                project(b + 1, 1 - u)
            if c < 2:
                scores(b, u, c + 2)
            elif exists(b + 1):
                scores(b + 1, 1 - u, c - 2)
            if c > 0:
                weigh(b, u, c - 1)
            elif exists(b - 1):
                weigh(b - 1, 1 - u, NC - 1)
            if c == 3 and exists(b + 2):
                transpose_inputs(b + 2, u)
            if c == 0 and exists(b - 1):
                transpose_recips(b - 1, 1 - u)
            if c == 3 and exists(b - 1):
                project_out(b - 1, 1 - u)

    pe.wait_ge(m.s.weights, m.weights_in)
    transpose_inputs(0, 0)
    project(0, 0)
    scores(0, 0, 0)
    scores(0, 0, 1)
    transpose_inputs(1, 1)
    over_sequences(pe, body)
    weigh(B - 1, 1, NC - 1)
    transpose_recips(B - 1, 1)
    project_out(B - 1, 1)


def attention_scalar(act, nc, m, s, a):
    def copy_inputs(b, u):
        act.wait_ge(s.transposed, b + 1)
        w = 256 if a.cross else 128
        nc.scalar.copy(m.xt[:, u, 0:w], m.front[:, 0:w]).then_inc(s.inputs_t, 1)

    def exponentials(b, u, c):
        j = NC * b + c
        act.wait_ge(s.maxed, j + 1)
        wait(act, s.probs_t, j - 1)
        for h in range(HC):
            last = nc.scalar.activation(m.p[:, c % 2, h, 0:a.keys],
                                        m.score[c % 2][:, h * a.columns:h * a.columns + a.keys], ACT.Exp,
                                        bias=m.nmax[:, c % 2, h:h + 1],
                                        accum_out=m.sums[:, u, HC * c + h:HC * c + h + 1])
        last.then_inc(s.exped, 1)

    def copy_probs(b, u, c):
        j = NC * b + c
        act.wait_ge(s.probs_t, j + 1)
        wait(act, s.weighted, j - 1)
        nc.scalar.copy(m.pt[:, c % 2, :, :].rearrange("p h t -> p (h t)"), m.flip[c % 2][:])\
            .then_inc(s.probs_s, 1)

    def copy_recips(b, u):
        act.wait_ge(s.recips_t, b + 1)
        nc.scalar.copy(m.rs[:, u, :], m.out[u][:, 128:256]).then_inc(s.recips_s, 1)

    def body(b, u):
        for c in range(NC):
            if c < NC - 1:
                exponentials(b, u, c + 1)
            elif exists(b + 1):
                exponentials(b + 1, 1 - u, 0)
            copy_probs(b, u, c)
            if c == 3 and exists(b + 2):
                copy_inputs(b + 2, u)
            if c == 1 and exists(b - 1):
                copy_recips(b - 1, 1 - u)

    copy_inputs(0, 0)
    exponentials(0, 0, 0)
    copy_inputs(1, 1)
    over_sequences(act, body)
    copy_recips(B - 1, 1)


def widened(m, out, keys, a, c):
    rows = slice(32 * c, 32 * c + 32)
    return (out[rows, HC * c:HC * c + HC, 0:a.keys],
            keys[rows, 0:a.keys].unsqueeze(1).broadcast_to([32, HC, a.keys]),
            m.own_rows[rows, :].unsqueeze(2).broadcast_to([32, HC, a.keys]))


def attention_vector(dve, nc, m, s, a):
    def normalise(b, u):
        wait(dve, s.transposed, b - 1)
        nc.vector.tensor_scalar(m.xn[:, u, :], tok(m.x, b), one(m.rstd, b), one(m.shift, b),
                                ALU.mult, ALU.add).then_inc(s.normed, 1)

    def queries(b, u):
        dve.wait_ge(s.projected, b + 1)
        wait(dve, s.based, POOL_STEPS * (b - 1) + 2)
        for dst in (m.q[:], m.q_hi[:, u, :]):
            nc.vector.tensor_scalar(dst, m.front[:, 128:256], a.bq, float(D) ** -0.5, ALU.add, ALU.mult)
        nc.vector.tensor_scalar(m.ks[:, u, 0:a.keys], m.front[:, 256:256 + a.keys], a.bk, None, ALU.add)\
            .then_inc(s.keys_s, 1)
        dve.wait_ge(s.keys_s, b + 1)
        nc.vector.tensor_tensor(m.q_lo[:, u, :], m.q[:], m.q_hi[:, u, :].bitcast(F32), ALU.subtract)

    def keys(b, u, c):
        wait(dve, s.scores, NC * (b - 1) + c + 1)
        nc.vector.tensor_tensor(*widened(m, m.kx, m.ks[:, u, :], a, c), ALU.mult).then_inc(s.keys, 1)

    def values(b, u):
        wait(dve, s.weighted, NC * (b - 1))
        wide = m.vx[:, u, :].rearrange("p (h e) -> p h e", e=VSTEP)[:, :, 0:D]
        nc.vector.tensor_copy(wide, m.front[:, 384:512].rearrange("p (h d) -> p h d", d=D))\
            .then_inc(s.values, 1)

    def first_value(b, u):
        if a.first_value:
            wait(dve, s.heads_out, b - 1)
            nc.vector.tensor_copy(m.v0[:, u:u + 1], m.front[:, 0:1])

    def maxima(b, u, c):
        j = NC * b + c
        dve.wait_ge(s.scores, j + 1)
        nc.vector.tensor_reduce(m.nmax[:, c % 2, :],
                                m.score[c % 2][:, 0:HC * a.columns].rearrange("p (h k) -> p h k", h=HC)[:, :, 0:a.keys],
                                AX.X, ALU.max, negate=True).then_inc(s.maxed, 1)

    def reciprocals(b, u):
        dve.wait_ge(s.exped, NC * b + NC)
        wait(dve, s.recips_t, b)
        nc.vector.reciprocal(m.rx[:].rearrange("p (h d) -> p h d", d=D),
                             m.sums[:, u, :].unsqueeze(2).broadcast_to([128, H, D]))\
            .then_inc(s.recips, 1)

    def heads_out(b, u):
        dve.wait_ge(s.recips_s, b + 1)
        dve.wait_ge(s.weighted, NC * b + NC)
        nc.vector.tensor_tensor(m.ot1[:], m.out[u][:, 0:128], m.rs[:, u, :], ALU.mult)\
            .then_inc(s.own, 1)
        dve.wait_ge(s.own, 2 * b + 1)
        extra = m.v0[:, u:u + 1] if a.first_value else a.bv
        nc.vector.tensor_scalar(m.ot[:, u, :], m.ot1[:], extra, None, ALU.add).then_inc(s.heads_out, 1)

    def update(b, u):
        dve.wait_ge(s.projected_out, b + 1)
        dve.wait_ge(s.based, POOL_STEPS * (b + 1))
        nc.vector.tensor_tensor(tok(m.x, b), m.out[u][:, 256:384], tok(m.x, b), ALU.add)\
            .then_inc(s.updated, 1)

    def statistics(b):
        dve.wait_ge(s.updated, b + 1)
        nc.vector.bn_stats(m.stats[:, b, :] if isinstance(b, int) else
                           m.stats[:, bass.ds(b, 1), :].rearrange("p a k -> p (a k)"), tok(m.x, b))\
            .then_inc(s.own, 1)

    def context_statistics(b):
        if isinstance(b, int) and b == 0:
            dve.wait_ge(m.s.ctx_in, 16)
        nc.vector.bn_stats(m.cstats[0:L, b, :] if isinstance(b, int) else
                           m.cstats[0:L, bass.ds(b, 1), :].rearrange("p a k -> p (a k)"),
                           tok(m.ctx, b)[0:L]).then_inc(m.s.stats, 1)

    def body(b, u):
        for c in range(NC):
            if c == 0 and exists(b - 1):
                reciprocals(b - 1, 1 - u)
            if c < 2:
                maxima(b, u, c + 2)
            elif exists(b + 1):
                maxima(b + 1, 1 - u, c - 2)
            if c == 2 and exists(b - 1):
                heads_out(b - 1, 1 - u)
            if c == 2 and exists(b + 1):
                first_value(b + 1, 1 - u)
            if c == 0 and exists(b + 1):
                queries(b + 1, 1 - u)
            if c < 2 and exists(b + 1):
                keys(b + 1, 1 - u, c)
            if c in (1, 2) and exists(b + 1):
                keys(b + 1, 1 - u, c + 1)
            if c == 1 and exists(b + 1):
                values(b + 1, 1 - u)
            if c == 2 and exists(b + 2):
                normalise(b + 2, u)
            if c == 3 and exists(b - 1):
                update(b - 1, 1 - u)
                statistics(b - 1)
            if c == 3 and a.measures_context:
                context_statistics(b)

    normalise(0, 0)
    normalise(1, 1)
    queries(0, 0)
    first_value(0, 0)
    values(0, 0)
    for c in range(NC):
        keys(0, 0, c)
    maxima(0, 0, 0)
    maxima(0, 0, 1)
    over_sequences(dve, body)
    reciprocals(B - 1, 1)
    heads_out(B - 1, 1)
    update(B - 1, 1)
    statistics(B - 1)
    dve.wait_ge(s.own, 2 * B)


def attention_pool(pool, nc, m, s, a):
    def low_keys(b, u):
        before = POOL_STEPS * b
        pool.wait_ge(s.keys_s, b + 1)
        nc.gpsimd.tensor_tensor(m.k_hi[:, 0:a.keys], m.ks[:, u, 0:a.keys],
                                m.cols[:, 6:7].broadcast_to([128, a.keys]), ALU.add)\
            .then_inc(s.based, 1)
        pool.wait_ge(s.based, before + 1)
        nc.gpsimd.tensor_tensor(m.k_lo[:, 0:a.keys], m.ks[:, u, 0:a.keys],
                                m.k_hi[:, 0:a.keys].bitcast(F32), ALU.subtract).then_inc(s.based, 1)
        pool.wait_ge(s.based, before + 2)
        for c in range(NC):
            wait(pool, s.scores, NC * (b - 1) + c + 1)
            nc.gpsimd.tensor_tensor(*widened(m, m.kx_lo, m.k_lo, a, c), ALU.mult).then_inc(s.based, 1)

    def body(b, u):
        pool.wait_ge(s.normed, b + 1)
        pool.wait_ge(s.based, POOL_STEPS * b + 6)
        nc.gpsimd.tensor_tensor(tok(m.x, b), tok(m.x, b), a.base, ALU.add).then_inc(s.based, 1)
        if exists(b + 1):
            low_keys(b + 1, 1 - u)
            pool.wait_ge(s.based, POOL_STEPS * (b + 1) + 6)
        if a.split_weights:
            split_experts(pool, nc, m, m.es, b, u)

    low_keys(0, 0)
    over_sequences(pool, body)


def split_experts(pool, nc, m, s, k, u):
    at = slice(k * 128, k * 128 + 128) if isinstance(k, int) else bass.ds(k * 128, 128)
    pool.wait_ge(s.raw[u], 16 + 8 * (k - u))
    nc.gpsimd.tensor_copy(m.w_hi[:, :, at], m.raw[:, u, 0:3, :]).then_inc(s.split_hi, 1)
    if not (isinstance(k, int) and k == B):
        nc.gpsimd.tensor_copy(m.pick[:, at], m.raw[:, u, 3, :])
    pool.wait_ge(s.split_hi, k + 1)
    nc.gpsimd.tensor_tensor(m.w_lo[:, :, at], m.raw[:, u, 0:3, :], m.w_hi[:, :, at].bitcast(F32),
                            ALU.subtract).then_inc(s.split, 1)


class WideSemaphores:
    def __init__(self, sem, stage):
        self.weight_products = sem(f"{stage}_weight_products")
        self.weights_saved = sem(f"{stage}_weights_saved")
        self.normed = sem(f"{stage}_normed")
        self.latents = sem(f"{stage}_latents")
        self.contexts = sem(f"{stage}_contexts")
        self.transposed = sem(f"{stage}_transposed")
        self.inputs_t = sem(f"{stage}_inputs_t")
        self.asked = sem(f"{stage}_asked")
        self.queries = sem(f"{stage}_queries")
        self.scores = sem(f"{stage}_scores")
        self.maxed = sem(f"{stage}_maxed")
        self.exped = sem(f"{stage}_exped")
        self.probs = sem(f"{stage}_probs")
        self.probs_t = sem(f"{stage}_probs_t")
        self.probs_s = sem(f"{stage}_probs_s")
        self.weighted = sem(f"{stage}_weighted")
        self.heads_s = sem(f"{stage}_heads_s")
        self.projected_out = sem(f"{stage}_projected_out")
        self.updated = sem(f"{stage}_updated")
        self.scaled = sem(f"{stage}_scaled")
        self.summed = sem(f"{stage}_summed")
        self.measured = sem(f"{stage}_measured")
        self.inputs_lo = sem(f"{stage}_inputs_lo")
        self.query_lows = sem(f"{stage}_query_lows")
        self.prob_lows = sem(f"{stage}_prob_lows")


KW = T + L
KP = KW + KW % 2


def wide_tensor(pe, nc, m, s):
    def weight_products(left, right, banks, before):
        for g in range(4):
            wait(pe, s.weights_saved, before + g - 1)
            for k in range(4):
                h = 4 * g + k
                last = nc.tensor.matmul(banks[g % 2][:, 128 * k:128 * k + 128], left[:, h, :],
                                        right[:, h, :], start=True, stop=True)
            last.then_inc(s.weight_products, 1)

    def transpose_inputs(b, u):
        pe.wait_ge(s.latents, 2 * b + 1)
        pe.wait_ge(s.contexts, 2 * b + 1)
        wait(pe, s.inputs_t, b)
        nc.tensor.transpose(m.front[:, 0:128], m.kv[:, u, 0, :], m.ident[:])
        nc.tensor.transpose(m.front[:, 128:256], m.kv[:, u, 1, :], m.ident[:]).then_inc(s.transposed, 1)

    def ask(b, u, c):
        j = XC * b + c
        if c == 0:
            pe.wait_ge(s.inputs_t, b + 1)
        wait(pe, s.query_lows, j)
        for k in range(2):
            last = nc.tensor.matmul(m.ask[:, 128 * k:128 * k + 128], m.score_w[:, 2 * c + k, :],
                                    m.kvt[:, u, 0:T], start=True, stop=True)
        last.then_inc(s.asked, 1)

    def in_parts(out, left_hi, left_lo, right_hi, right_lo, first=True, last=True):
        nc.tensor.matmul(out, left_hi, right_hi, start=first, stop=False)
        nc.tensor.matmul(out, left_hi, right_lo, start=False, stop=False)
        return nc.tensor.matmul(out, left_lo, right_hi, start=False, stop=last)

    def scores(b, u, c):
        j = XC * b + c
        if c == 0:
            pe.wait_ge(s.inputs_lo, b + 1)
        pe.wait_ge(s.query_lows, j + 1)
        wait(pe, s.exped, j - 1)
        for k in range(2):
            head = slice(128 * k, 128 * k + 128)
            last = in_parts(m.score[c % 2][:, KP * k:KP * k + KP], m.qs_hi[:, c % 4, head],
                            m.qs_lo[:, c % 4, head], m.kvt_hi[:, u, 0:KP], m.kvt_lo[:, u, 0:KP])
        last.then_inc(s.scores, 1)

    def transpose_probs(b, u, c):
        j = XC * b + c
        pe.wait_ge(s.probs, j + 1)
        wait(pe, s.prob_lows, j)
        for part in range(2):
            for k in range(2):
                at = 256 * part + 128 * k
                last = nc.tensor.transpose(m.flip[0][:, at:at + 128],
                                           m.pw[:, c % 2, k, 128 * part:128 * part + 128], m.ident[:])
        last.then_inc(s.probs_t, 1)

    def weigh(b, u, c):
        j = XC * b + c
        if c == 0:
            pe.wait_ge(s.contexts, 2 * b + 2)
        pe.wait_ge(s.prob_lows, j + 1)
        wait(pe, s.heads_s, j)
        for part in range(2):
            keys = slice(256 * part, 256 * part + 256)
            last = in_parts(m.mix[:, 0:256], m.kv_hi[:, u, part, :], m.kv_lo[:, u, part, :],
                            m.pwt_hi[:, c % 2, keys], m.pwt_lo[:, c % 2, keys], part == 0, part == 1)
        last.then_inc(s.weighted, 1)

    def project_out(b, u, c):
        j = XC * b + c
        if c == 0:
            wait(pe, s.updated, b - 1)
        pe.wait_ge(s.heads_s, j + 1)
        for k in range(2):
            last = nc.tensor.matmul(m.out[u][:, 0:128], m.us[:, c % 2, 128 * k:128 * k + 128],
                                    m.out_w[:, 2 * c + k, :], start=c == 0 and k == 0,
                                    stop=c == XC - 1 and k == 1)
        last.then_inc(s.projected_out, 1)

    def body(b, u):
        for c in range(XC):
            transpose_probs(b, u, c)
            if c < XC - 2:
                scores(b, u, c + 2)
            elif exists(b + 1):
                scores(b + 1, 1 - u, c + 2 - XC)
            if c > 0:
                weigh(b, u, c - 1)
            elif exists(b - 1):
                weigh(b - 1, 1 - u, XC - 1)
            if c == 2 and exists(b + 1):
                transpose_inputs(b + 1, 1 - u)
            if c < XC - 4:
                ask(b, u, c + 4)
            elif exists(b + 1):
                ask(b + 1, 1 - u, c + 4 - XC)
            if c > 1:
                project_out(b, u, c - 2)
            elif exists(b - 1):
                project_out(b - 1, 1 - u, XC - 2 + c)

    pe.wait_ge(m.s.wide_in, m.wide_loads)
    weight_products(m.wq_t, m.wk_t, m.score, 0)
    weight_products(m.wv_t, m.wo_r, m.flip, 4)
    transpose_inputs(0, 0)
    pe.wait_ge(s.weights_saved, 8)
    ask(0, 0, 0)
    ask(0, 0, 1)
    scores(0, 0, 0)
    ask(0, 0, 2)
    scores(0, 0, 1)
    ask(0, 0, 3)
    over_sequences(pe, body)
    weigh(B - 1, 1, XC - 1)
    project_out(B - 1, 1, XC - 2)
    project_out(B - 1, 1, XC - 1)


def wide_scalar(act, nc, m, s):
    def copy_inputs(b, u):
        act.wait_ge(s.transposed, b + 1)
        wait(act, s.scores, XC * (b - 1))
        nc.scalar.copy(m.kvt[:, u, :], m.front[:, 0:256])
        nc.scalar.copy(m.kvt_hi[:, u, :], m.front[:, 0:256]).then_inc(s.inputs_t, 1)

    def copy_queries(b, u, c):
        j = XC * b + c
        act.wait_ge(s.asked, j + 1)
        wait(act, s.scores, j - 3)
        nc.scalar.copy(m.qs_hi[:, c % 4, :], m.ask[:, 0:256]).then_inc(s.queries, 1)

    def exponentials(b, u, c):
        j = XC * b + c
        act.wait_ge(s.maxed, j + 1)
        wait(act, s.probs, j - 1)
        for k in range(2):
            last = nc.scalar.activation(m.ew[:, c % 2, k, :], m.score[c % 2][:, KP * k:KP * k + KW],
                                        ACT.Exp, bias=m.nmax[:, c % 2, k:k + 1],
                                        accum_out=m.sums[:, c % 2, k:k + 1])
        last.then_inc(s.exped, 1)

    def copy_probs(b, u, c):
        j = XC * b + c
        act.wait_ge(s.probs_t, j + 1)
        wait(act, s.weighted, j - 1)
        nc.scalar.copy(m.pwt_hi[:, c % 2, :], m.flip[0][:]).then_inc(s.probs_s, 1)

    def copy_heads(b, u, c):
        j = XC * b + c
        act.wait_ge(s.weighted, j + 1)
        wait(act, s.projected_out, j - 1)
        nc.scalar.copy(m.us[:, c % 2, :], m.mix[:, 0:256]).then_inc(s.heads_s, 1)

    def body(b, u):
        for c in range(XC):
            if c < XC - 3:
                copy_queries(b, u, c + 3)
            elif exists(b + 1):
                copy_queries(b + 1, 1 - u, c + 3 - XC)
            if c < XC - 1:
                exponentials(b, u, c + 1)
            elif exists(b + 1):
                exponentials(b + 1, 1 - u, 0)
            copy_probs(b, u, c)
            if c == 3 and exists(b + 1):
                copy_inputs(b + 1, 1 - u)
            if c > 0:
                copy_heads(b, u, c - 1)
            elif exists(b - 1):
                copy_heads(b - 1, 1 - u, XC - 1)

    root_scalar(act, nc, m, m.s, 2, L)
    for g in range(4):
        act.wait_ge(s.weight_products, g + 1)
        nc.scalar.mul(m.score_w[:, 4 * g:4 * g + 4, :].rearrange("p h c -> p (h c)"), m.score[g % 2][:],
                      float(XD) ** -0.5).then_inc(s.weights_saved, 1)
    root_scalar(act, nc, m, m.s, 3)
    for g in range(4):
        act.wait_ge(s.weight_products, g + 5)
        nc.scalar.copy(m.out_w[:, 4 * g:4 * g + 4, :].rearrange("p h c -> p (h c)"), m.flip[g % 2][:])\
            .then_inc(s.weights_saved, 1)
        if g == 1:
            root_scalar(act, nc, m, m.s, 4)
    copy_inputs(0, 0)
    copy_queries(0, 0, 0)
    copy_queries(0, 0, 1)
    copy_queries(0, 0, 2)
    exponentials(0, 0, 0)
    over_sequences(act, body)
    copy_heads(B - 1, 1, XC - 1)


def wide_vector(dve, nc, m, s):
    def normalise(b, u):
        wait(dve, s.latents, 2 * (b - 1))
        wait(dve, s.contexts, 2 * (b - 1))
        nc.vector.tensor_scalar(m.xn[:, u, :], tok(m.x, b), one(m.rstd, b), one(m.shift, b),
                                ALU.mult, ALU.add)
        nc.vector.tensor_scalar(m.cs[0:L, u, :], tok(m.ctx, b)[0:L], one(m.crstd, b, L),
                                one(m.cshift, b, L), ALU.mult, ALU.add).then_inc(s.normed, 1)

    def maxima(b, u, c):
        j = XC * b + c
        dve.wait_ge(s.scores, j + 1)
        nc.vector.tensor_reduce(m.nmax[:, c % 2, 0:2],
                                m.score[c % 2][:, 0:2 * KP].rearrange("p (h k) -> p h k", h=2)[:, :, 0:KW],
                                AX.X, ALU.max, negate=True).then_inc(s.maxed, 1)

    def reciprocals(b, u, c):
        j = XC * b + c
        dve.wait_ge(s.exped, j + 1)
        wait(dve, s.probs, j - 1)
        nc.vector.reciprocal(m.rw[:, c % 2, :], m.sums[:, c % 2, 0:2]).then_inc(s.summed, 1)

    def prob_lows(b, u, c):
        dve.wait_ge(s.probs_s, XC * b + c + 1)
        nc.vector.tensor_tensor(m.pwt_lo[:, c % 2, :], m.flip[0][:], m.pwt_hi[:, c % 2, :].bitcast(F32),
                                ALU.subtract).then_inc(s.prob_lows, 1)

    def query_lows(b, u, c):
        dve.wait_ge(s.queries, XC * b + c + 1)
        nc.vector.tensor_tensor(m.qs_lo[:, c % 4, :], m.ask[:, 0:256], m.qs_hi[:, c % 4, :].bitcast(F32),
                                ALU.subtract).then_inc(s.query_lows, 1)

    def update(b, u):
        dve.wait_ge(s.projected_out, XC * (b + 1))
        nc.vector.tensor_tensor(tok(m.x, b), m.out[u][:, 0:128], tok(m.x, b), ALU.add)\
            .then_inc(s.updated, 1)

    def statistics(b):
        dve.wait_ge(s.updated, b + 1)
        nc.vector.bn_stats(m.stats[:, b, :] if isinstance(b, int) else
                           m.stats[:, bass.ds(b, 1), :].rearrange("p a k -> p (a k)"), tok(m.x, b))\
            .then_inc(s.measured, 1)

    def extremes(b):
        for k, op in ((0, ALU.max), (1, ALU.min)):
            dst = m.ext[:, k, b:b + 1] if isinstance(b, int) else m.ext[:, k, bass.ds(b, 1)]
            last = nc.vector.tensor_reduce(dst, tok(m.x, b), AX.X, op)
        last.then_inc(s.measured, 1)

    def body(b, u):
        for c in range(XC):
            if c < XC - 3:
                query_lows(b, u, c + 3)
            elif exists(b + 1):
                query_lows(b + 1, 1 - u, c + 3 - XC)
            if c < XC - 1:
                reciprocals(b, u, c + 1)
            elif exists(b + 1):
                reciprocals(b + 1, 1 - u, 0)
            prob_lows(b, u, c)
            if c < XC - 2:
                maxima(b, u, c + 2)
            elif exists(b + 1):
                maxima(b + 1, 1 - u, c + 2 - XC)
            if c == 2 and exists(b - 1):
                update(b - 1, 1 - u)
            if c == 2 and exists(b + 2):
                normalise(b + 2, u)
            if c == 3 and exists(b - 1):
                statistics(b - 1)
            if c == 4 and exists(b - 1):
                extremes(b - 1)
            if isinstance(b, int) and XC * b + c < QUANTISE_STEPS:
                quantise_weights(dve, nc, m, XC * b + c)

    normalise(0, 0)
    normalise(1, 1)
    query_lows(0, 0, 0)
    query_lows(0, 0, 1)
    maxima(0, 0, 0)
    query_lows(0, 0, 2)
    maxima(0, 0, 1)
    reciprocals(0, 0, 0)
    over_sequences(dve, body)
    update(B - 1, 1)
    statistics(B - 1)
    extremes(B - 1)
    dve.wait_ge(s.measured, 2 * B)


def wide_pool(pool, nc, m, s):
    def probabilities(b, u, c):
        j = XC * b + c
        pool.wait_ge(s.summed, j + 1)
        wait(pool, s.probs_t, j - 1)
        nc.gpsimd.tensor_tensor(m.pw[:, c % 2, :, 0:KW], m.ew[:, c % 2, :, :],
                                m.rw[:, c % 2, :].unsqueeze(2).broadcast_to([128, 2, KW]), ALU.mult)\
            .then_inc(s.probs, 1)

    def inputs(b, u, step):
        both = m.kv[:, u, :, :]
        if step == 0:
            pool.wait_ge(s.normed, b + 1)
            nc.gpsimd.tensor_tensor(m.xa[:], m.xn[:, u, :], m.affine[:, 0, :], ALU.mult).then_inc(s.scaled, 1)
            nc.gpsimd.tensor_tensor(m.ca[0:L], m.cs[0:L, u, :], m.affine[0:L, 2, :], ALU.mult)\
                .then_inc(s.scaled, 1)
        elif step == 1:
            pool.wait_ge(s.scaled, 2 * b + 2)
            wait(pool, s.weighted, XC * (b - 1))
            nc.gpsimd.tensor_tensor(m.kv[:, u, 0, :], m.xa[:], m.affine[:, 1, :], ALU.add)\
                .then_inc(s.latents, 1)
            nc.gpsimd.tensor_tensor(m.kv[0:L, u, 1, :], m.ca[0:L], m.affine[0:L, 3, :], ALU.add)\
                .then_inc(s.contexts, 1)
        elif step == 2:
            pool.wait_ge(s.latents, 2 * b + 1)
            pool.wait_ge(s.contexts, 2 * b + 1)
            nc.gpsimd.tensor_tensor(m.kv_hi[:, u, :, :], both,
                                    m.cols[:, 6:7].unsqueeze(2).broadcast_to([128, 2, C]), ALU.add)\
                .then_inc(s.latents, 1)
        elif step == 3:
            pool.wait_ge(s.latents, 2 * b + 2)
            nc.gpsimd.tensor_tensor(m.kv_lo[:, u, :, :], both, m.kv_hi[:, u, :, :].bitcast(F32),
                                    ALU.subtract).then_inc(s.contexts, 1)
        else:
            pool.wait_ge(s.inputs_t, b + 1)
            nc.gpsimd.tensor_tensor(m.kvt_lo[:, u, :], m.kvt[:, u, :], m.kvt_hi[:, u, :].bitcast(F32),
                                    ALU.subtract).then_inc(s.inputs_lo, 1)

    def body(b, u):
        for c in range(XC):
            if c < XC - 1:
                probabilities(b, u, c + 1)
            elif exists(b + 1):
                probabilities(b + 1, 1 - u, 0)
            if c < 5 and exists(b + 1):
                inputs(b + 1, 1 - u, c)

    for step in range(5):
        inputs(0, 0, step)
    probabilities(0, 0, 0)
    over_sequences(pool, body)


FI, FT = 384, 3
GB = 4
G = B // GB
QW, QN = GB * T, G
QMAX, WQMAX, QBLOCK = 32767.0, 7.0, 32
MAGIC = 1.5 * 2.0 ** 23
class FeedForwardSemaphores:
    def __init__(self, sem, stage):
        self.local_max = sem(f"{stage}_local_max")
        self.all_max = sem(f"{stage}_all_max")
        self.scaled = sem(f"{stage}_scaled")
        self.normed = sem(f"{stage}_normed")
        self.input_sums = sem(f"{stage}_input_sums")
        self.weights_t = sem(f"{stage}_weights_t")
        self.weights_s = sem(f"{stage}_weights_s")
        self.rounded = sem(f"{stage}_rounded")
        self.transposed = sem(f"{stage}_transposed")
        self.rounded_t = sem(f"{stage}_rounded_t")
        self.projected = sem(f"{stage}_projected")
        self.copied = sem(f"{stage}_copied")
        self.reduced = sem(f"{stage}_reduced")
        self.sums = sem(f"{stage}_sums")
        self.gates = sem(f"{stage}_gates")
        self.sigmoids = sem(f"{stage}_sigmoids")
        self.sigmoid_sums = sem(f"{stage}_sigmoid_sums")
        self.rounded_sigmoids = sem(f"{stage}_rounded_sigmoids")
        self.up_sums = sem(f"{stage}_up_sums")
        self.ups = sem(f"{stage}_ups")
        self.products = sem(f"{stage}_products")
        self.hidden = sem(f"{stage}_hidden")
        self.hidden_out = sem(f"{stage}_hidden_out")
        self.updated = sem(f"{stage}_updated")
        self.measured = sem(f"{stage}_measured")


(SX, IX, SU, FU, SG, FG, S2, F2, SO, FO) = range(10)


QUANTISE_STEPS = 16


def quantise_weights(dve, nc, m, n):
    w, at, count = (m.wug, 0, 2 * FT * C // QBLOCK) if n < 8 else (m.wdn, 24, FI // QBLOCK)
    flat, blocks = w[:], w[:].rearrange("p (n k) -> p n k", k=QBLOCK)
    s, r = m.wscale[:, at:at + count], m.wrecip[:, at:at + count]
    wide = [128, count, QBLOCK]
    if n == 0:
        dve.wait_ge(m.s.wide_in, m.wide_loads)
    wait(dve, m.s.quantised, n)
    if n % 8 == 0:
        last = nc.vector.tensor_reduce(s, blocks, AX.X, ALU.max, apply_absolute_value=True)
    elif n % 8 == 1:
        last = nc.vector.tensor_scalar(s, s, 1.0 / WQMAX, 1e-12, ALU.mult, ALU.max)
    elif n % 8 == 2:
        last = nc.vector.reciprocal(r, s)
    elif n % 8 == 3:
        last = nc.vector.tensor_tensor(blocks, blocks, r.unsqueeze(2).broadcast_to(wide), ALU.mult)
    elif n % 8 == 4:
        last = nc.vector.tensor_scalar(flat, flat, MAGIC, None, ALU.add)
    elif n % 8 == 5:
        last = nc.vector.tensor_scalar(flat, flat, MAGIC, WQMAX, ALU.subtract, ALU.min)
    elif n % 8 == 6:
        last = nc.vector.tensor_scalar(flat, flat, -WQMAX - 1.0, None, ALU.max)
    else:
        last = nc.vector.tensor_tensor(blocks, blocks, s.unsqueeze(2).broadcast_to(wide), ALU.mult)
    last.then_inc(m.s.quantised, 1)


def over_blocks(engine, body):
    body(0, 0)
    body(1, 1)
    with engine.Fori(1, QN // 2 - 1) as i:
        body(2 * i, 0)
        body(2 * i + 1, 1)
    body(QN - 2, 0)
    body(QN - 1, 1)


def block(t, n):
    view = t[:].rearrange("p (n k) -> p n k", n=FT)
    return view[:, :, n * QW:(n + 1) * QW] if isinstance(n, int) else view[:, :, bass.ds(n * QW, QW)]


def half(t, u):
    return t[:, u, :].rearrange("p (n k) -> p n k", n=FT)


def ffn_vector(dve, nc, m, s, link):
    col = lambda k: m.scal[:, k:k + 1]

    def global_max(parts, n):
        nc.vector.tensor_reduce(m.lmax[:, n:n + 1], parts, AX.X, ALU.max, apply_absolute_value=True)\
            .then_inc(s.local_max, 1)
        dve.wait_ge(s.all_max, n + 1)
        return m.gmax[:, n:n + 1]

    def scale_of(maximum, factors, k):
        link(nc.vector.tensor_scalar(m.tmp[:, 0:1], maximum, factors, None, ALU.mult))
        link(nc.vector.tensor_scalar(col(k), m.tmp[:, 0:1], 1.0 / QMAX, 1e-12, ALU.mult, ALU.max))
        link(nc.vector.reciprocal(m.tmp[:, 1:2], col(k)))
        link(nc.vector.tensor_scalar(col(k + 1), m.tmp[:, 1:2], factors, None, ALU.mult))

    link(nc.vector.tensor_tensor(m.ext[:], m.ext[:], m.rstd[:].unsqueeze(1).broadcast_to([128, 2, B]), ALU.mult))
    link(nc.vector.tensor_tensor(m.ext[:], m.ext[:], m.shift[:].unsqueeze(1).broadcast_to([128, 2, B]), ALU.add))
    scale_of(global_max(m.ext[:].rearrange("p a b -> p (a b)"), 0), 1.0, SX)

    def round_inputs(g):
        for q in range(GB):
            b = GB * g + q
            last = nc.vector.tensor_scalar(m.xw[:, q * C:(q + 1) * C], tok(m.x, b), one(m.rstd, b),
                                           one(m.shift, b), ALU.mult, ALU.add)
        last.then_inc(s.normed, 1)
        dve.wait_ge(s.normed, g + 1)
        nc.vector.tensor_scalar(m.rq[:], m.xw[:], col(IX), MAGIC, ALU.mult, ALU.add).then_inc(s.input_sums, 1)
        dve.wait_ge(s.input_sums, g + 1)
        wait(dve, s.transposed, g)
        nc.vector.tensor_scalar(m.rq2[:], m.rq[:], MAGIC, None, ALU.subtract).then_inc(s.rounded, 1)
        dve.wait_ge(s.rounded, g + 1)

    def group_max(g):
        dve.wait_ge(s.copied, 2 * FT * (g + 1))
        for t, src in ((0, m.up), (1, m.gate)):
            at = t * 32 + FT * g
            dst = m.amax[:, at:at + FT] if isinstance(g, int) else m.amax[:, bass.ds(at, FT)]
            last = nc.vector.tensor_reduce(dst, block(src, g), AX.X, ALU.max, apply_absolute_value=True)
        last.then_inc(s.reduced, 1)

    round_inputs(0)
    round_inputs(1)
    with dve.Fori(0, G - 2) as g:
        round_inputs(g + 2)
        group_max(g)
    group_max(G - 2)
    group_max(G - 1)
    dve.wait_ge(s.reduced, G)
    scale_of(global_max(m.amax[:, 32:32 + FT * G], 1), col(SX), SG)
    scale_of(global_max(m.amax[:, 0:FT * G], 2), col(SX), SU)
    nc.vector.memset(m.tmp[:, 7:8], 0.0).then_inc(s.scaled, 1)

    def gates(n, u):
        dve.wait_ge(s.sums, n + 1)
        nc.vector.tensor_scalar(block(m.gate, n), block(m.gate, n), MAGIC, col(SG), ALU.subtract, ALU.mult)\
            .then_inc(s.gates, 1)

    def gated(n, u):
        dve.wait_ge(s.sigmoid_sums, n + 1)
        nc.vector.tensor_scalar(half(m.sig, u), half(m.sig, u), MAGIC, 65535.0, ALU.subtract, ALU.min)\
            .then_inc(s.rounded_sigmoids, 1)
        dve.wait_ge(s.rounded_sigmoids, n + 1)
        nc.vector.scalar_tensor_tensor(block(m.gate, n), half(m.sig, u), 1.0 / 65536.0, block(m.gate, n),
                                       ALU.mult, ALU.mult).then_inc(s.products, 1)

    def product_max(n, before):
        dve.wait_ge(s.products, n + before + 1)
        at = 64 + FT * n
        dst = m.amax[:, at:at + FT] if isinstance(n, int) else m.amax[:, bass.ds(at, FT)]
        nc.vector.tensor_reduce(dst, block(m.gate, n), AX.X, ALU.max, apply_absolute_value=True)\
            .then_inc(s.reduced, 1)

    def gate_body(n, u):
        if not isinstance(n, int) or n + 1 < QN:
            gates(n + 1, 1 - u)
        gated(n, u)
        product_max(n, 0)

    gates(0, 0)
    over_blocks(dve, gate_body)
    dve.wait_ge(s.reduced, G + QN)
    scale_of(global_max(m.amax[:, 64:64 + FT * QN], 3), 1.0, S2)
    nc.vector.tensor_scalar(col(SO), col(S2), col(SU), None, ALU.mult).then_inc(s.scaled, 1)

    def hidden_body(n, u):
        dve.wait_ge(s.sums, QN + n + 1)
        dve.wait_ge(s.ups, n + 1)
        nc.vector.scalar_tensor_tensor(block(m.gate, n), block(m.gate, n), MAGIC, block(m.up, n),
                                       ALU.subtract, ALU.mult).then_inc(s.products, 1)
        product_max(n, QN)

    over_blocks(dve, hidden_body)
    dve.wait_ge(s.reduced, G + 2 * QN)
    top = global_max(m.amax[:, 64:64 + FT * QN], 4)
    link(nc.vector.tensor_copy(m.tmp[:, 4:5], col(SO)))
    scale_of(top, m.tmp[:, 4:5], SO)
    nc.vector.memset(m.tmp[:, 7:8], 0.0).then_inc(s.scaled, 1)

    def round_hidden(n, u):
        dve.wait_ge(s.sums, 2 * QN + n + 1)
        wait(dve, s.hidden_out, GB * (n - 1))
        nc.vector.tensor_scalar(half(m.sig, u), block(m.gate, n), MAGIC, None, ALU.subtract)\
            .then_inc(s.hidden, 1)

    def statistics(b):
        nc.vector.bn_stats(m.stats[:, b, :] if isinstance(b, int) else
                           m.stats[:, bass.ds(b, 1), :].rearrange("p a k -> p (a k)"), tok(m.x, b))\
            .then_inc(s.measured, 1)

    def down_body(n, u):
        if not isinstance(n, int) or n + 1 < QN:
            round_hidden(n + 1, 1 - u)
        for q in range(GB):
            dve.wait_ge(s.hidden_out, GB * n + q + 1)
            x = tok(m.x, GB * n + q)
            nc.vector.scalar_tensor_tensor(x, m.bank[q % 4][:, 0:128], col(SO), x, ALU.mult, ALU.add)\
                .then_inc(s.updated, 1)
        for q in range(GB):
            dve.wait_ge(s.updated, GB * n + q + 1)
            statistics(GB * n + q)

    round_hidden(0, 0)
    over_blocks(dve, down_body)
    dve.wait_ge(s.measured, B)


def ffn_scalar(act, nc, m, s):
    def copy_inputs(g, u):
        act.wait_ge(s.transposed, g + 1)
        wait(act, s.projected, 2 * FT * (g - 1))
        nc.scalar.copy(m.rqt[:, u, :], m.bank[6][:]).then_inc(s.rounded_t, 1)

    def copies(g, u):
        for t in range(2 * FT):
            act.wait_ge(s.projected, 2 * FT * g + t + 1)
            dst = m.up if t < FT else m.gate
            at = (t % FT) * B * T + g * 512
            nc.scalar.copy(dst[:, at:at + 512] if isinstance(g, int) else dst[:, bass.ds(at, 512)], m.bank[t][:])\
                .then_inc(s.copied, 1)
            if t == 2 and (not isinstance(g, int) or g + 1 < G):
                copy_inputs(g + 1, 1 - u)

    def rounding_sum(dst, src, scale, done):
        nc.scalar.activation(dst, src, ACT.Identity, bias=m.magic[:], scale=scale).then_inc(done, 1)

    def gate_sums(n):
        rounding_sum(block(m.gate, n), block(m.gate, n), m.scal[:, FG:FG + 1], s.sums)

    def gate_body(n, u):
        if n + 1 < QN:
            gate_sums(n + 1)
        act.wait_ge(s.gates, n + 1)
        wait(act, s.products, n - 1)
        nc.scalar.activation(half(m.sig, u), block(m.gate, n), ACT.Sigmoid).then_inc(s.sigmoids, 1)
        act.wait_ge(s.sigmoids, n + 1)
        rounding_sum(half(m.sig, u), half(m.sig, u), 65536.0, s.sigmoid_sums)

    act.wait_ge(s.weights_t, 1)
    nc.scalar.copy(m.wug_t[:, 0:512], m.bank[0][:])
    nc.scalar.copy(m.wug_t[:, 512:768], m.bank[1][:, 0:256])
    nc.scalar.copy(m.wdn_t[:], m.bank[2][:, 0:FI]).then_inc(s.weights_s, 1)
    copy_inputs(0, 0)
    over_blocks(act, copies)
    act.wait_ge(s.scaled, 1)
    gate_sums(0)
    for n in range(QN):
        gate_body(n, n % 2)
    act.wait_ge(s.scaled, 2)
    for n in range(QN):
        rounding_sum(block(m.gate, n), block(m.gate, n), m.scal[:, F2:F2 + 1], s.sums)
    act.wait_ge(s.scaled, 3)
    for n in range(QN):
        rounding_sum(block(m.gate, n), block(m.gate, n), m.scal[:, FO:FO + 1], s.sums)


def ffn_tensor(pe, nc, m, s):
    pe.wait_ge(m.s.quantised, QUANTISE_STEPS)
    for t in range(2 * FT):
        nc.tensor.transpose(m.bank[t // 4][:, (t % 4) * 128:(t % 4) * 128 + 128],
                            m.wug[:, t * 128:t * 128 + 128], m.ident[:])
    for t in range(FT):
        last = nc.tensor.transpose(m.bank[2][:, t * 128:t * 128 + 128], m.wdn[:, t * 128:t * 128 + 128],
                                   m.ident[:])
    last.then_inc(s.weights_t, 1)

    def transpose_inputs(g):
        pe.wait_ge(s.rounded, g + 1)
        wait(pe, s.rounded_t, g)
        for q in range(GB):
            last = nc.tensor.transpose(m.bank[6][:, q * 128:q * 128 + 128], m.rq2[:, q * 128:q * 128 + 128],
                                       m.ident[:])
        last.then_inc(s.transposed, 1)

    def group(g, u):
        pe.wait_ge(s.rounded_t, g + 1)
        for t in range(2 * FT):
            wait(pe, s.copied, 2 * FT * (g - 1) + t + 1)
            nc.tensor.matmul(m.bank[t][:], m.wug_t[:, t * 128:t * 128 + 128], m.rqt[:, u, :],
                             start=True, stop=True).then_inc(s.projected, 1)
            if t == 2 and (not isinstance(g, int) or g + 1 < G):
                transpose_inputs(g + 1)

    transpose_inputs(0)
    pe.wait_ge(s.weights_s, 1)
    over_blocks(pe, group)
    pe.wait_ge(s.copied, 2 * FT * G)

    def down_body(n, u):
        pe.wait_ge(s.hidden, n + 1)
        for q in range(GB):
            wait(pe, s.updated, GB * n + q - 3)
            for t in range(FT):
                last = nc.tensor.matmul(m.bank[q % 4][:, 0:128], half(m.sig, u)[:, t, q * 128:q * 128 + 128],
                                        m.wdn_t[:, t * 128:t * 128 + 128], start=t == 0, stop=t == FT - 1)
            last.then_inc(s.hidden_out, 1)

    over_blocks(pe, down_body)


def ffn_pool(pool, nc, m, s):
    def all_max(n):
        pool.wait_ge(s.local_max, n + 1)
        nc.gpsimd.partition_all_reduce(m.gmax[:, n:n + 1], m.lmax[:, n:n + 1], 128,
                                       bass.bass_isa.ReduceOp.max).then_inc(s.all_max, 1)

    def round_up(n):
        nc.gpsimd.tensor_scalar(block(m.up, n), block(m.up, n), m.scal[:, FU:FU + 1], MAGIC, ALU.mult, ALU.add)\
            .then_inc(s.up_sums, 1)
        pool.wait_ge(s.up_sums, n + 1)
        nc.gpsimd.tensor_scalar(block(m.up, n), block(m.up, n), MAGIC, None, ALU.subtract).then_inc(s.ups, 1)

    for n in range(3):
        all_max(n)
    pool.wait_ge(s.scaled, 1)
    for n in range(QN - 3):
        round_up(n)
    all_max(3)
    for n in range(QN - 3, QN):
        round_up(n)
    all_max(4)


E, EK, EG, EGK = 64, 6, 8, 4
NT = E // 2 + 1
LAG = 3
class ExpertSemaphores:
    def __init__(self, sem, stage):
        self.normed = sem(f"{stage}_normed")
        self.x_t = sem(f"{stage}_x_t")
        self.x_f = sem(f"{stage}_x_f")
        self.x_hi = sem(f"{stage}_x_hi")
        self.x_lo = sem(f"{stage}_x_lo")
        self.logits = sem(f"{stage}_logits")
        self.scores = sem(f"{stage}_scores")
        self.routed = sem(f"{stage}_routed")
        self.shares_t = sem(f"{stage}_shares_t")
        self.shares = sem(f"{stage}_shares")
        self.gated = sem(f"{stage}_gated")
        self.upped = sem(f"{stage}_upped")
        self.shared_out = sem(f"{stage}_shared_out")
        self.silus = sem(f"{stage}_silus")
        self.products = sem(f"{stage}_products")
        self.hiddens = sem(f"{stage}_hiddens")
        self.his = sem(f"{stage}_his")
        self.los = sem(f"{stage}_los")
        self.downed = sem(f"{stage}_downed")
        self.out_s = sem(f"{stage}_out_s")
        self.out_t = sem(f"{stage}_out_t")
        self.updated = sem(f"{stage}_updated")




def moe_tensor(pe, nc, m, s):
    def transpose_inputs(g):
        pe.wait_ge(s.normed, g + 1)
        for q in range(GB):
            last = nc.tensor.transpose(m.misc[:, q * 128:q * 128 + 128], m.xg[:, q, :], m.ident[:])
        last.then_inc(s.x_t, 1)

    def logits(g):
        pe.wait_ge(s.x_f, g + 1)
        for q in range(GB):
            last = nc.tensor.matmul(m.misc[:, q * E:q * E + E], m.xf[:, q * 128:q * 128 + 128],
                                    m.gate_w[:], start=True, stop=True)
        last.then_inc(s.logits, 1)

    def transpose_shares(g):
        pe.wait_ge(s.routed, g + 1)
        for q in range(GB):
            last = nc.tensor.transpose(m.misc[:, q * 128:q * 128 + 128], m.share[:, q, :].bitcast(F32),
                                       m.ident[:])
        last.then_inc(s.shares_t, 1)

    def three(bank, w_hi, w_lo, x_hi, x_lo, first=True, last=True):
        nc.tensor.matmul(bank, w_hi, x_hi, start=first, stop=False)
        nc.tensor.matmul(bank, w_hi, x_lo, start=False, stop=False)
        return nc.tensor.matmul(bank, w_lo, x_hi, start=False, stop=last)

    def project(g, u, k):
        n, tile = NT * g + k, slice(128 * k, 128 * k + 128)
        if k == 0:
            pe.wait_ge(s.x_hi, g + 1)
            pe.wait_ge(s.x_lo, g + 1)
        wait(pe, s.silus, n - 1)
        x_hi, x_lo = m.x_hi[:, u, :], m.x_lo[:, u, :]
        three(m.gate_bank[(k + u) % 2][:], m.w_hi[:, 0, tile], m.w_lo[:, 0, tile], x_hi, x_lo)\
            .then_inc(s.gated, 1)
        wait(pe, s.products, n - 1)
        three(m.up_bank[(k + u) % 2][:], m.w_hi[:, 1, tile], m.w_lo[:, 1, tile], x_hi, x_lo)\
            .then_inc(s.upped, 1)
        if k < NT - 1:
            wait(pe, s.hiddens, n - 1)
            if k == 0:
                pe.wait_ge(s.shares, g + 1)
            nc.tensor.matmul(m.share_bank[(k + u) % 2][:], m.pick[:, tile], m.share_t[:, u, :],
                             start=True, stop=True).then_inc(s.shared_out, 1)

    def project_down(g, k):
        n, tile = NT * g + k, slice(128 * k, 128 * k + 128)
        if k == 0:
            wait(pe, s.out_s, g)
        pe.wait_ge(s.los, n + 1)
        three(m.out_bank[:], m.w_hi[:, 2, tile], m.w_lo[:, 2, tile], m.h_hi[:, k % 3, :], m.h_lo[:, k % 3, :],
              first=k == 0, last=k == NT - 1).then_inc(s.downed, 1)

    def transpose_output(g):
        pe.wait_ge(s.out_s, g + 1)
        for q in range(GB):
            last = nc.tensor.transpose(m.misc[:, q * 128:q * 128 + 128], m.ys[:, q * 128:q * 128 + 128],
                                       m.ident[:])
        last.then_inc(s.out_t, 1)

    def body(g, u):
        before, after = group_exists(g - 1), group_exists(g + 1)
        for k in range(NT):
            project(g, u, k)
            if k >= LAG:
                project_down(g, k - LAG)
            elif before:
                project_down(g - 1, k - LAG + NT)
            if k == 5 and before:
                transpose_output(g - 1)
            if k == 7 and after:
                wait(pe, s.updated, GB * g)
                transpose_inputs(g + 1)
            if k == 9 and after:
                logits(g + 1)
            if k == 29 and after:
                transpose_shares(g + 1)

    transpose_inputs(0)
    logits(0)
    transpose_shares(0)
    over_groups(pe, body)
    for k in range(NT - LAG, NT):
        project_down(G - 1, k)
    transpose_output(G - 1)


def group_exists(g):
    return not isinstance(g, int) or 0 <= g < G


def over_groups(engine, body):
    body(0, 0)
    body(1, 1)
    with engine.Fori(1, G // 2 - 1) as i:
        body(2 * i, 0)
        body(2 * i + 1, 1)
    body(G - 2, 0)
    body(G - 1, 1)


def moe_scalar(act, nc, m, s):
    def copy_inputs(g):
        act.wait_ge(s.x_t, g + 1)
        wait(act, s.x_lo, g)
        nc.scalar.copy(m.xf[:], m.misc[:]).then_inc(s.x_f, 1)

    def routing_scores(g):
        act.wait_ge(s.logits, g + 1)
        nc.scalar.activation(m.sg[:], m.misc[:, 0:GB * E], ACT.Sigmoid).then_inc(s.scores, 1)

    def copy_shares(g, u):
        act.wait_ge(s.shares_t, g + 1)
        nc.scalar.copy(m.share_t[:, u, :], m.misc[:]).then_inc(s.shares, 1)

    def silu(g, u, k):
        n = NT * g + k
        act.wait_ge(s.gated, n + 1)
        wait(act, s.products, n - 1)
        nc.scalar.activation(m.sl[:, (k + u) % 2, :], m.gate_bank[(k + u) % 2][:], ACT.Silu)\
            .then_inc(s.silus, 1)

    def high_part(g, u, k):
        n = NT * g + k
        act.wait_ge(s.hiddens, n + 1)
        wait(act, s.downed, n - 2)
        nc.scalar.copy(m.h_hi[:, k % 3, :], m.h[:, (k + u) % 2, :]).then_inc(s.his, 1)

    def copy_output(g):
        act.wait_ge(s.downed, NT * (g + 1))
        nc.scalar.copy(m.ys[:], m.out_bank[:]).then_inc(s.out_s, 1)

    def body(g, u):
        before, after = group_exists(g - 1), group_exists(g + 1)
        for k in range(NT):
            if k == LAG and before:
                copy_output(g - 1)
            silu(g, u, k)
            if k > 1:
                high_part(g, u, k - 2)
            elif before:
                high_part(g - 1, 1 - u, NT - 2 + k)
            if k == 7 and after:
                copy_inputs(g + 1)
            if k == 9 and after:
                routing_scores(g + 1)
            if k == 29 and after:
                copy_shares(g + 1, 1 - u)

    copy_inputs(0)
    routing_scores(0)
    copy_shares(0, 0)
    over_groups(act, body)
    high_part(G - 1, 1, NT - 2)
    high_part(G - 1, 1, NT - 1)
    copy_output(G - 1)


ROUTE_STEPS = 16


def moe_vector(dve, nc, m, s):
    def normalise(g):
        wait(dve, s.x_t, g)
        for q in range(GB):
            b = GB * g + q
            last = nc.vector.tensor_scalar(m.xg[:, q, :], tok(m.x, b), one(m.rstd, b), one(m.shift, b),
                                           ALU.mult, ALU.add)
        last.then_inc(s.normed, 1)

    def split_inputs(g, u):
        dve.wait_ge(s.x_f, g + 1)
        nc.vector.tensor_copy(m.x_hi[:, u, :], m.xf[:]).then_inc(s.x_hi, 1)

    rows = lambda t, n: t[:].rearrange("p (q n) -> p q n", n=n)

    def wide(t, n):
        return t.unsqueeze(2).broadcast_to([128, GB, n])

    def route(g, n):
        at = ROUTE_STEPS * g + n
        wait(dve, m.s.route, at)
        if n == 0:
            dve.wait_ge(s.scores, g + 1)
            last = nc.vector.tensor_tensor(rows(m.sc, E), rows(m.sg, E),
                                           m.gate_b[:].unsqueeze(1).broadcast_to([128, GB, E]), ALU.add)
        elif n == 1:
            last = nc.vector.tensor_reduce(m.gs[:], m.sc[:].rearrange("p (n k) -> p n k", k=E // EG),
                                           AX.X, ALU.max)
        elif n == 2:
            nc.vector.memset(m.tmp[:, 7:8], 0.0)
            for q in range(GB):
                last = nc.vector.max(m.g8[:, q, :], m.gs[:, q * EG:q * EG + EG])
        elif n == 3:
            least = m.g8[:, :, EGK - 1:EGK].broadcast_to([128, GB, EG])
            nc.vector.tensor_tensor(rows(m.ga, EG), rows(m.gs, EG), least, ALU.is_gt)
            last = nc.vector.tensor_tensor(rows(m.ge, EG), rows(m.gs, EG), least, ALU.is_equal)
        elif n == 4:
            nc.vector.tensor_reduce(m.na[:], rows(m.ga, EG), AX.X, ALU.add)
            last = nc.vector.tensor_tensor_scan(m.gp[:], m.fresh_g[:], m.ge[:], 0.0, ALU.mult, ALU.add)
        elif n == 5:
            last = nc.vector.tensor_tensor(rows(m.gq, EG), rows(m.gp, EG), wide(m.na[:], EG), ALU.add)
        elif n == 6:
            last = nc.vector.scalar_tensor_tensor(m.gp[:], m.gq[:], float(EGK), m.ge[:], ALU.is_le,
                                                  ALU.mult)
        elif n == 7:
            last = nc.vector.tensor_tensor(m.gq[:], m.gp[:], m.ga[:], ALU.add)
        elif n == 8:
            spread = m.gq[:].unsqueeze(2).broadcast_to([128, GB * EG, E // EG])
            last = nc.vector.tensor_tensor(m.ms[:].rearrange("p (n k) -> p n k", k=E // EG),
                                           m.sc[:].rearrange("p (n k) -> p n k", k=E // EG), spread,
                                           ALU.mult)
        elif n == 9:
            nc.vector.memset(m.tmp[:, 7:8], 0.0)
            for q in range(GB):
                last = nc.vector.max(m.m8[:, q, :], m.ms[:, q * E:q * E + E])
        elif n == 10:
            least = m.m8[:, :, EK - 1:EK].broadcast_to([128, GB, E])
            nc.vector.tensor_tensor(rows(m.sa, E), rows(m.ms, E), least, ALU.is_gt)
            nc.vector.tensor_tensor(rows(m.se, E), rows(m.ms, E), least, ALU.is_equal)
            last = nc.vector.tensor_reduce(m.tw[:], m.m8[:, :, 0:EK], AX.X, ALU.add)
        elif n == 11:
            nc.vector.tensor_reduce(m.na[:], rows(m.sa, E), AX.X, ALU.add)
            nc.vector.tensor_scalar(m.tx[:], m.tw[:], 1e-8, None, ALU.add)
            last = nc.vector.tensor_tensor_scan(m.sp[:], m.fresh_e[:], m.se[:], 0.0, ALU.mult, ALU.add)
        elif n == 12:
            nc.vector.reciprocal(m.ty[:], m.tx[:])
            last = nc.vector.tensor_tensor(rows(m.sq, E), rows(m.sp, E), wide(m.na[:], E), ALU.add)
        elif n == 13:
            nc.vector.scalar_tensor_tensor(m.sp[:], m.sq[:], float(EK), m.se[:], ALU.is_le, ALU.mult)
            last = nc.vector.tensor_tensor(rows(m.sc, E), rows(m.ms, E), wide(m.ty[:], E), ALU.mult)
        elif n == 14:
            last = nc.vector.tensor_tensor(m.sq[:], m.sp[:], m.sa[:], ALU.add)
        elif n == 15:
            last = nc.vector.tensor_tensor(m.w[:], m.sc[:], m.sq[:], ALU.mult)
        last.then_inc(m.s.route, 1)

    def split_shares(g):
        dve.wait_ge(m.s.route, ROUTE_STEPS * (g + 1))
        wait(dve, s.shares_t, g)
        nc.vector.tensor_copy(m.share[:, :, 0:E], rows(m.w, E)).then_inc(m.s.halves, 1)
        dve.wait_ge(m.s.halves, g + 1)
        nc.vector.tensor_tensor(m.share[:, :, E:2 * E], rows(m.w, E), m.share[:, :, 0:E].bitcast(F32),
                                ALU.subtract).then_inc(s.routed, 1)

    def product(g, u, k):
        n = NT * g + k
        dve.wait_ge(s.upped, n + 1)
        dve.wait_ge(s.silus, n + 1)
        wait(dve, s.hiddens, n - 1)
        nc.vector.tensor_tensor(m.h1[:, (k + u) % 2, :], m.up_bank[(k + u) % 2][:],
                                m.sl[:, (k + u) % 2, :], ALU.mult).then_inc(s.products, 1)

    def hidden(g, u, k):
        n = NT * g + k
        dve.wait_ge(s.products, n + 1)
        wait(dve, s.los, n - 1)
        here = (k + u) % 2
        if k < NT - 1:
            dve.wait_ge(s.shared_out, (NT - 1) * g + k + 1)
            nc.vector.tensor_tensor(m.h[:, here, :], m.share_bank[here][:], m.h1[:, here, :], ALU.mult)\
                .then_inc(s.hiddens, 1)
        else:
            nc.vector.tensor_copy(m.h[:, here, :], m.h1[:, here, :]).then_inc(s.hiddens, 1)

    def update(g):
        dve.wait_ge(s.out_t, g + 1)
        for q in range(GB):
            x = tok(m.x, GB * g + q)
            nc.vector.tensor_tensor(x, m.misc[:, q * 128:q * 128 + 128], x, ALU.add)\
                .then_inc(s.updated, 1)

    def body(g, u):
        before, after = group_exists(g - 1), group_exists(g + 1)
        for k in range(NT):
            product(g, u, k)
            if k > 0:
                hidden(g, u, k - 1)
            elif before:
                hidden(g - 1, 1 - u, NT - 1)
            if k == 2 and after:
                normalise(g + 1)
            if k == 6 and before:
                update(g - 1)
            if k == 8 and after:
                split_inputs(g + 1, 1 - u)
            if 11 <= k < 11 + ROUTE_STEPS and after:
                route(g + 1, k - 11)
            if k == 27 and after:
                split_shares(g + 1)

    normalise(0)
    split_inputs(0, 0)
    for n in range(ROUTE_STEPS):
        route(0, n)
    split_shares(0)
    over_groups(dve, body)
    hidden(G - 1, 1, NT - 1)
    update(G - 1)


def moe_pool(pool, nc, m, s):
    def split_inputs(g, u):
        pool.wait_ge(s.x_hi, g + 1)
        wait(pool, s.logits, g + 1)
        nc.gpsimd.tensor_tensor(m.x_lo[:, u, :], m.xf[:], m.x_hi[:, u, :].bitcast(F32), ALU.subtract)\
            .then_inc(s.x_lo, 1)

    def low_part(g, u, k):
        n = NT * g + k
        pool.wait_ge(s.his, n + 1)
        nc.gpsimd.tensor_tensor(m.h_lo[:, k % 3, :], m.h[:, (k + u) % 2, :],
                                m.h_hi[:, k % 3, :].bitcast(F32), ALU.subtract).then_inc(s.los, 1)

    def body(g, u):
        for k in range(NT):
            if k > 0:
                low_part(g, u, k - 1)
            elif group_exists(g - 1):
                low_part(g - 1, 1 - u, NT - 1)
            if k == 10 and group_exists(g + 1):
                split_inputs(g + 1, 1 - u)

    split_inputs(0, 0)
    over_groups(pool, body)
    low_part(G - 1, 1, NT - 1)


class Chain:

    def __init__(self, dve, semaphore):
        self.dve, self.semaphore, self.count = dve, semaphore, 0

    def __call__(self, instruction):
        self.count += 1
        instruction.then_inc(self.semaphore, 1)
        self.dve.wait_ge(self.semaphore, self.count)


def inverse_root(nc, m, s, link, n, value, out, p):
    dve = link.dve
    dve.wait_ge(s.rooted, n)
    link(nc.vector.reciprocal(m.r0[0:p], m.root[0:p]))
    link(nc.vector.tensor_tensor(m.t0[0:p], m.r0[0:p], m.r0[0:p], ALU.mult))
    link(nc.vector.tensor_tensor(m.t0[0:p], m.t0[0:p], value, ALU.mult))
    link(nc.vector.tensor_scalar(m.t0[0:p], m.t0[0:p], -0.5, 1.5, ALU.mult, ALU.add))
    link(nc.vector.tensor_tensor(out, m.r0[0:p], m.t0[0:p], ALU.mult))


def norm_vector(nc, m, s, link, n, stats, rstd, shift, p=128):
    st = stats[0:p]
    link(nc.vector.tensor_tensor(m.t0[0:p], st[:, :, 1], st[:, :, 4], ALU.subtract))
    link(nc.vector.tensor_tensor(m.t0[0:p], m.t0[0:p], m.t0[0:p], ALU.mult))
    link(nc.vector.tensor_tensor(m.t1[0:p], st[:, :, 2], st[:, :, 5], ALU.add))
    link(nc.vector.tensor_scalar(m.t1[0:p], m.t1[0:p], 1.0 / C, None, ALU.mult))
    link(nc.vector.scalar_tensor_tensor(m.var[0:p], m.t0[0:p], 0.25, m.t1[0:p], ALU.mult, ALU.add))
    nc.vector.tensor_scalar(m.vare[0:p], m.var[0:p], EPS, None, ALU.add).then_inc(s.to_root, 1)
    inverse_root(nc, m, s, link, n, m.vare[0:p], rstd[0:p], p)
    link(nc.vector.tensor_tensor(m.t0[0:p], st[:, :, 1], st[:, :, 4], ALU.add))
    link(nc.vector.scalar_tensor_tensor(shift[0:p], m.t0[0:p], -0.5, rstd[0:p], ALU.mult, ALU.mult))


def renorm_vector(nc, m, s, link, n):
    link(nc.vector.tensor_tensor(m.t0[:], m.rstd[:], m.rstd[:], ALU.mult))
    link(nc.vector.tensor_tensor(m.t0[:], m.t0[:], m.var[:], ALU.mult))
    nc.vector.tensor_scalar(m.vare[:], m.t0[:], EPS, None, ALU.add).then_inc(s.to_root, 1)
    inverse_root(nc, m, s, link, n, m.vare[:], m.t1[:], 128)
    link(nc.vector.tensor_tensor(m.rstd[:], m.rstd[:], m.t1[:], ALU.mult))
    link(nc.vector.tensor_tensor(m.shift[:], m.shift[:], m.t1[:], ALU.mult))


def root_scalar(act, nc, m, s, n, p=128):
    act.wait_ge(s.to_root, n)
    nc.scalar.activation(m.root[0:p], m.vare[0:p], ACT.Sqrt).then_inc(s.rooted, 1)


def program(nc, io, out):
    arena = ExitStack()
    with arena:
        def sem(name):
            return arena.enter_context(nc.semaphore(name))

        def placer(stack):
            def sb(name, shape, dtype=F32):
                return stack.enter_context(nc.sbuf_tensor(name, shape, dtype))
            return sb

        x_parts = 4
        per = B // x_parts
        m = Names()
        sb = placer(arena)

        m.x = sb("x", [128, B * C])
        m.stats = sb("stats", [128, B, 6])
        m.cstats = sb("cstats", [128, B, 6])
        m.rstd = sb("rstd", [128, B])
        m.shift = sb("shift", [128, B])
        m.crstd = sb("crstd", [128, B])
        m.cshift = sb("cshift", [128, B])
        m.var = sb("var", [128, B])
        m.vare = sb("vare", [128, B])
        m.root = sb("root", [128, B])
        m.r0 = sb("r0", [128, B])
        m.t0 = sb("t0", [128, B])
        m.t1 = sb("t1", [128, B])
        m.ident = sb("ident", [128, 128])
        m.ident_b = sb("ident_b", [128, 128], BF16)
        m.causal = sb("causal", [128, HC * T], BF16)
        m.own_rows = sb("own_rows", [128, HC])
        m.xn = sb("xn", [128, 2, C])
        m.cs = sb("cs", [128, 2, C])
        m.nmax = sb("nmax", [128, 2, HC])
        m.sums = sb("sums", [128, 2, H])
        m.w0 = sb("w0", [128, 3 * C])
        m.w0o = sb("w0o", [128, C])
        m.w3 = sb("w3", [128, 3 * C])
        m.w3o = sb("w3o", [128, C])
        m.w4q = sb("w4q", [128, C])
        m.w4kv = sb("w4kv", [128, 2 * C])
        m.w4o = sb("w4o", [128, C])
        m.bases = sb("bases", [128, 3, C])
        m.cols = sb("cols", [128, 7])
        m.scal = sb("scal", [128, 10])
        m.tmp = sb("tmp", [128, 8])
        m.lmax = sb("lmax", [128, 5])
        m.gmax = sb("gmax", [128, 5])
        m.amax = sb("amax", [128, 96])
        m.magic = sb("magic", [128, 1])
        m.ext = sb("ext", [128, 2, B])
        m.wscale = sb("wscale", [128, 36])
        m.wrecip = sb("wrecip", [128, 36])
        m.gate_w = sb("gate_w", [128, E])
        m.gate_b = sb("gate_b", [128, E])
        m.fresh_e = sb("fresh_e", [128, GB * E])
        m.fresh_g = sb("fresh_g", [128, GB * EG])
        with ExitStack() as part:
            over = placer(part)
            m.wq_t = over("wq_t", [XD, XH, C])
            m.wk_t = over("wk_t", [XD, XH, C])
            m.wv_t = over("wv_t", [XD, XH, C])
            m.wo_r = over("wo_r", [XD, XH, C])
            m.ctx = over("ctx", [128, B * C])
            m.affine = over("affine", [128, 4, C])
        with ExitStack() as part:
            over = placer(part)
            m.up = over("up", [128, FT * B * T])
            m.gate = over("gate", [128, FT * B * T])
        m.w_hi = sb("w_hi", [128, 3, NT * 128], F32R)
        m.w_lo = sb("w_lo", [128, 3, NT * 128], F32R)
        with ExitStack() as part:
            over = placer(part)
            m.unused = over("unused", [128, 2])
        with ExitStack() as part:
            over = placer(part)
            m.pick = over("pick", [128, (NT - 1) * 128], F32R)
        m.score_w = sb("score_w", [128, XH, C])
        m.out_w = sb("out_w", [128, XH, C])
        with ExitStack() as part:
            over = placer(part)
            m.raw = over("raw", [128, 2, 4, 128])
        m.wug = sb("wug", [128, 2 * FT * C])
        m.wdn = sb("wdn", [128, FI])
        with ExitStack() as part:
            over = placer(part)
            m.sa = over("sa", [128, GB * E])
            m.se = over("se", [128, GB * E])
            m.sp = over("sp", [128, GB * E])
            m.sq = over("sq", [128, GB * E])
        m.alibi = sb("alibi", [128, H * T], BF16)
        with ExitStack() as part:
            over = placer(part)
            m.kv = over("kv", [128, 2, 2, C])
            m.kvt = over("kvt", [128, 2, 256])
            m.qs_hi = over("qs_hi", [128, 4, 256], F32R)
            m.qs_lo = over("qs_lo", [128, 4, 256], F32R)
            m.kvt_hi = over("kvt_hi", [128, 2, 256], F32R)
            m.kvt_lo = over("kvt_lo", [128, 2, 256], F32R)
            m.kv_hi = over("kv_hi", [128, 2, 2, C], F32R)
            m.kv_lo = over("kv_lo", [128, 2, 2, C], F32R)
            m.ew = over("ew", [128, 2, 2, KW])
            m.rw = over("rw", [128, 2, 2])
            m.pw = over("pw", [128, 2, 2, 256])
            m.pwt_hi = over("pwt_hi", [128, 2, 512], F32R)
            m.pwt_lo = over("pwt_lo", [128, 2, 512], F32R)
            m.us = over("us", [128, 2, 256])
            m.xa = over("xa", [128, C])
            m.ca = over("ca", [128, C])
        with ExitStack() as part:
            over = placer(part)
            m.sig = over("sig", [128, 2, FT * QW])
            m.xw = over("xw", [128, 512])
            m.rq = over("rq", [128, 512])
            m.rq2 = over("rq2", [128, 512])
            m.rqt = over("rqt", [128, 2, 512])
            m.wug_t = over("wug_t", [128, 2 * FT * C])
            m.wdn_t = over("wdn_t", [128, FI])
        with ExitStack() as part:
            over = placer(part)
            m.xg = over("xg", [128, GB, C])
            m.xf = over("xf", [128, 512])
            m.x_hi = over("x_hi", [128, 2, 512], F32R)
            m.x_lo = over("x_lo", [128, 2, 512], F32R)
            m.share_t = over("share_t", [128, 2, 512], F32R)
            m.share = over("share", [128, GB, 2 * E], F32R)
            m.sl = over("sl", [128, 2, 512])
            m.h1 = over("h1", [128, 2, 512])
            m.h = over("h", [128, 2, 512])
            m.h_hi = over("h_hi", [128, 3, 512], F32R)
            m.h_lo = over("h_lo", [128, 3, 512], F32R)
            m.ys = over("ys", [128, 512])
            m.sg = over("sg", [128, GB * E])
            m.sc = over("sc", [128, GB * E])
            m.ms = over("ms", [128, GB * E])
            m.w = over("w", [128, GB * E])
            m.gs = over("gs", [128, GB * EG])
            m.ga = over("ga", [128, GB * EG])
            m.ge = over("ge", [128, GB * EG])
            m.gp = over("gp", [128, GB * EG])
            m.gq = over("gq", [128, GB * EG])
            m.g8 = over("g8", [128, GB, 8])
            m.m8 = over("m8", [128, GB, 8])
            m.na = over("na", [128, GB])
            m.tw = over("tw", [128, GB])
            m.tx = over("tx", [128, GB])
            m.ty = over("ty", [128, GB])
        m.kx = sb("kx", [128, H, 128], F32R)
        m.kx_lo = sb("kx_lo", [128, H, 128], F32R)
        m.ks = sb("ks", [128, 2, 128])
        m.k_hi = sb("k_hi", [128, 128], F32R)
        m.k_lo = sb("k_lo", [128, 128])
        m.q_hi = sb("q_hi", [128, 2, T], F32R)
        m.q_lo = sb("q_lo", [128, 2, T], F32R)
        m.vx = sb("vx", [128, 2, H * VSTEP])
        m.xt = sb("xt", [128, 2, 256])
        m.q = sb("q", [128, T])
        m.p = sb("p", [128, 2, HC, 128])
        m.pt = sb("pt", [128, 2, HC, 128])
        m.rx = sb("rx", [128, C])
        m.rs = sb("rs", [128, 2, T])
        m.ot1 = sb("ot1", [128, T])
        m.ot = sb("ot", [128, 2, T])
        m.v0 = sb("v0", [128, 2])

        m.bank = bank = [arena.enter_context(nc.psum_tensor(f"bank{i}", [128, 512], F32)) for i in range(8)]
        m.score, m.flip, m.out, m.front = bank[0:2], bank[2:4], bank[4:6], bank[6]
        m.ask, m.mix = bank[3], bank[7]
        m.gate_bank, m.up_bank, m.share_bank, m.out_bank, m.misc = bank[0:2], bank[2:4], bank[4:6], bank[6], bank[7]

        m.s, m.es = Names(), Names()
        m.s.loaded = [sem(f"all_loaded{k}") for k in range(x_parts)]
        m.s.weights = sem("all_weights")
        m.s.wide_in = sem("all_wide_in")
        m.s.ctx_in = sem("all_ctx_in")
        m.s.stats = sem("all_stats")
        m.s.quantised = sem("all_quantised")
        m.s.to_root = sem("all_to_root")
        m.s.rooted = sem("all_rooted")
        m.s.chain = sem("all_chain")
        m.s.zeros = sem("all_zeros")
        m.s.route = sem("all_route")
        m.s.halves = sem("all_halves")
        m.s.stored = sem("all_stored")
        m.es.split_hi, m.es.split = sem("experts_split_hi"), sem("experts_split")
        m.es.raw = [sem("experts_raw0"), sem("experts_raw1")]
        s0, s3, s4 = (AttentionSemaphores(sem, n) for n in ("attn0", "attn1", "cross"))
        s1, s2, s5 = WideSemaphores(sem, "wide"), FeedForwardSemaphores(sem, "ffn"), ExpertSemaphores(sem, "moe")
        s4.copied = [sem("cross_copied0"), sem("cross_copied1")]

        col = lambda k: m.cols[:, k:k + 1]
        attn0 = Attention(
            keys=T, cross=False, first_value=False, split_weights=False, measures_context=True,
            mask=lambda c: m.alibi[:, 512 * c:512 * c + 512],
            wq=m.w0[:, 0:128], wk=m.w0[:, 128:256], wv=m.w0[:, 256:384], wo=m.w0o[:],
            bq=col(0), bk=col(1), bv=col(2), base=m.bases[:, 0, :])
        attn1 = Attention(
            keys=T, cross=False, first_value=True, split_weights=True, measures_context=False, mask=lambda c: m.causal[:],
            wq=m.w3[:, 0:128], wk=m.w3[:, 128:256], wv=m.w3[:, 256:384], wo=m.w3o[:],
            bq=col(6), bk=col(6), bv=None, base=m.bases[:, 1, :])
        cross = Attention(
            keys=L, cross=True, first_value=False, split_weights=False, measures_context=False, mask=None,
            wq=m.w4q[:], wk=m.w4kv[:, 0:128], wv=m.w4kv[:, 128:256], wo=m.w4o[:],
            bq=col(3), bk=col(4), bv=col(5), base=m.bases[:, 2, :])

        def row(name, p=128):
            return io[name].rearrange("(a c) -> a c", a=1).broadcast_to([p, io[name].shape[0]])

        tiles = lambda a: a.rearrange("(n p) c -> p n c", p=128)
        heads = lambda a: a.rearrange("(n p) c -> p n c", p=XD)
        first_loads = [
            (m.w0[:], io["L0_attn_W_attn"]), (m.w0o[:], io["L0_attn_W_proj"]), (m.ident[:], io["identity"]),
            (m.ident_b[:], io["identity_b"]), (m.alibi[:], io["alibi"]), (m.own_rows[:], io["own_rows"]),
            (m.cols[:, 0:6], io["bias_columns"]), (m.bases[:, 0, :], row("L0_attn_b_proj"))]
        m.weights_in = 16 * len(first_loads)
        later_loads = [
            (m.wq_t[:], heads(io["wide_wq_t"])), (m.wk_t[:], heads(io["wide_wkv_t"][0:XH * XD])),
            (m.wv_t[:], heads(io["wide_wkv_t"][XH * XD:2 * XH * XD])), (m.wo_r[:], heads(io["L0_xattn_Wo"])),
            (m.affine[:, 0, :], row("L0_xattn_ln2_w")), (m.affine[:, 1, :], row("L0_xattn_ln2_b")),
            (m.affine[:, 2, :], row("L0_xattn_ln1_w")), (m.affine[:, 3, :], row("L0_xattn_ln1_b")),
            (m.wug[:, 0:FI].rearrange("p (n c) -> p n c", c=C), tiles(io["L0_ffn_w_up"])),
            (m.wug[:, FI:2 * FI].rearrange("p (n c) -> p n c", c=C), tiles(io["L0_ffn_w_gate"])),
            (m.wdn[:], io["L0_ffn_w_down"]), (m.causal[:], io["causal"]), (m.w3[:], io["attn1_wqkv_t"]),
            (m.w3o[:], io["attn1_wout_t"]), (m.bases[:, 1, :], row("L1_attn_b_out")),
            (m.w4q[:], io["L1_xattn_Wq"]), (m.w4kv[:], io["L1_xattn_Wkv"]), (m.w4o[:], io["L1_xattn_Wproj"]),
            (m.bases[:, 2, :], row("L1_xattn_bproj")), (m.gate_w[:], io["moe_gate_t"]),
            (m.gate_b[:], row("L1_ffn_gate_bias")), (m.fresh_e[:], io["fresh_experts"]),
            (m.fresh_g[:], io["fresh_groups"])]
        m.wide_loads = 16 * len(later_loads)

        with nc.Block() as block:
            @block.sync
            def _(sp):
                x_view = m.x[:].rearrange("t (b c) -> t b c", c=C)
                for k in range(x_parts):
                    sp.dma_start(x_view[:, k * per:(k + 1) * per, :],
                                 io["x"][k * per:(k + 1) * per].rearrange("b t c -> t b c"))\
                        .then_inc(m.s.loaded[k], 16)
                for dst, src in first_loads:
                    sp.dma_start(dst, src).then_inc(m.s.weights, 16)
                sp.dma_start(m.ctx[0:L, :].rearrange("t (b c) -> t b c", c=C),
                             io["ctx_1024"].rearrange("b t c -> t b c")).then_inc(m.s.ctx_in, 16)
                for dst, src in later_loads:
                    sp.dma_start(dst, src).then_inc(m.s.wide_in, 16)

                def load_experts(k, u):
                    wait(sp, m.es.split, k - 1)
                    src = io["experts"][k] if isinstance(k, int) else io["experts"][bass.ds(k, 1)].rearrange("a p n c -> p (a n) c")
                    sp.dma_start(m.raw[:, u, :, :], src).then_inc(m.es.raw[u], 16)

                sp.wait_ge(s2.weights_t, 1)
                over_sequences(sp, load_experts)
                load_experts(B, 0)

                def load_context(b, u):
                    wait(sp, s4.transposed, b - 1)
                    src = io["ctx_1024"][b] if isinstance(b, int) else io["ctx_1024"][bass.ds(b, 1)].rearrange("a t c -> t (a c)")
                    sp.dma_start(m.cs[0:L, u, :], src).then_inc(s4.copied[u], 16)

                sp.wait_ge(s3.updated, B)
                over_sequences(sp, load_context)
                with sp.Fori(0, G) as g:
                    sp.wait_ge(s5.updated, GB * g + GB)
                    sp.dma_start(out[bass.ds(g * GB, GB)].rearrange("b t c -> t b c"),
                                 x_view[:, bass.ds(g * GB, GB), :]).then_inc(m.s.stored, 16)
                sp.wait_ge(m.s.stored, 16 * G)

            @block.gpsimd
            def _(pool):
                for t in (m.kx[:].bitcast(F32), m.kx_lo[:].bitcast(F32), m.vx[:], m.p[:], m.cs[:]):
                    nc.gpsimd.memset(t, 0.0).then_inc(m.s.zeros, 1)
                pool.wait_ge(m.s.zeros, 5)
                pool.wait_ge(m.s.weights, m.weights_in)
                for part in m.s.loaded:
                    pool.wait_ge(part, 16)
                attention_pool(pool, nc, m, s0, attn0)
                pool.wait_ge(s0.updated, B)
                for t in (m.kv, m.pw):
                    nc.gpsimd.memset(t[:], 0.0).then_inc(m.s.zeros, 1)
                pool.wait_ge(m.s.zeros, 7)
                pool.wait_ge(m.s.wide_in, m.wide_loads)
                wide_pool(pool, nc, m, s1)
                ffn_pool(pool, nc, m, s2)
                pool.wait_ge(s2.updated, B)
                for t in (m.kx[:].bitcast(F32), m.kx_lo[:].bitcast(F32), m.vx[:]):
                    nc.gpsimd.memset(t, 0.0).then_inc(m.s.zeros, 1)
                pool.wait_ge(m.s.zeros, 10)
                attention_pool(pool, nc, m, s3, attn1)
                split_experts(pool, nc, m, m.es, B, 0)
                pool.wait_ge(s3.updated, B)
                nc.gpsimd.memset(m.p[:], 0.0).then_inc(m.s.zeros, 1)
                attention_pool(pool, nc, m, s4, cross)
                moe_pool(pool, nc, m, s5)

            @block.scalar
            def _(act):
                root_scalar(act, nc, m, m.s, 1)
                act.wait_ge(m.s.zeros, 5)
                attention_scalar(act, nc, m, s0, attn0)
                wide_scalar(act, nc, m, s1)
                root_scalar(act, nc, m, m.s, 5)
                ffn_scalar(act, nc, m, s2)
                root_scalar(act, nc, m, m.s, 6)
                attention_scalar(act, nc, m, s3, attn1)
                root_scalar(act, nc, m, m.s, 7)
                act.wait_ge(m.s.zeros, 11)
                attention_scalar(act, nc, m, s4, cross)
                root_scalar(act, nc, m, m.s, 8)
                moe_scalar(act, nc, m, s5)

            @block.vector
            def _(dve):
                link = Chain(dve, m.s.chain)
                for b in range(B):
                    if b % per == 0:
                        dve.wait_ge(m.s.loaded[b // per], 16)
                    nc.vector.bn_stats(m.stats[:, b, :], tok(m.x, b)).then_inc(m.s.stats, 1)
                dve.wait_ge(m.s.stats, B)
                norm_vector(nc, m, m.s, link, 1, m.stats, m.rstd, m.shift)
                nc.vector.memset(m.cols[:, 6:7], 0.0)
                nc.vector.memset(m.magic[:], MAGIC)
                dve.wait_ge(m.s.weights, m.weights_in)
                dve.wait_ge(m.s.zeros, 5)
                attention_vector(dve, nc, m, s0, attn0)
                dve.wait_ge(m.s.stats, 2 * B)
                norm_vector(nc, m, m.s, link, 2, m.cstats, m.crstd, m.cshift, L)
                norm_vector(nc, m, m.s, link, 3, m.stats, m.rstd, m.shift)
                renorm_vector(nc, m, m.s, link, 4)
                dve.wait_ge(m.s.zeros, 7)
                wide_vector(dve, nc, m, s1)
                norm_vector(nc, m, m.s, link, 5, m.stats, m.rstd, m.shift)
                ffn_vector(dve, nc, m, s2, link)
                norm_vector(nc, m, m.s, link, 6, m.stats, m.rstd, m.shift)
                dve.wait_ge(m.s.zeros, 10)
                attention_vector(dve, nc, m, s3, attn1)
                norm_vector(nc, m, m.s, link, 7, m.stats, m.rstd, m.shift)
                attention_vector(dve, nc, m, s4, cross)
                norm_vector(nc, m, m.s, link, 8, m.stats, m.rstd, m.shift)
                moe_vector(dve, nc, m, s5)

            @block.tensor
            def _(pe):
                pe.wait_ge(m.s.weights, m.weights_in)
                pe.wait_ge(m.s.zeros, 5)
                attention_tensor(pe, nc, m, s0, attn0)
                pe.wait_ge(m.s.wide_in, m.wide_loads)
                wide_tensor(pe, nc, m, s1)
                ffn_tensor(pe, nc, m, s2)
                attention_tensor(pe, nc, m, s3, attn1)
                attention_tensor(pe, nc, m, s4, cross)
                pe.wait_ge(m.es.split, B + 1)
                moe_tensor(pe, nc, m, s5)


def constants():
    eye = np.eye(128, dtype=np.float32)
    at = np.arange(T)
    rel = (at[None, :] - at[:, None]).astype(np.float32)
    slope = 2.0 ** -np.arange(1, H + 1, dtype=np.float32)
    future = rel > 0
    alibi = np.where(future[:, None, :], np.float32(MASKED), rel[:, None, :] * slope[None, :, None])
    causal = np.repeat(np.where(future, np.float32(MASKED), np.float32(0))[:, None, :], HC, 1)
    own = (np.arange(128)[:, None] % 32 // D == np.arange(HC)[None, :]).astype(np.float32)

    def fresh(n):
        return np.tile((np.arange(GB * n) % n != 0).astype(np.float32), (128, 1))

    bf = mybir.dt.np(BF16)
    return {"identity": eye, "identity_b": eye.astype(bf), "alibi": alibi.reshape(T, -1).astype(bf),
            "causal": causal.reshape(T, -1).astype(bf), "own_rows": own,
            "fresh_experts": fresh(E), "fresh_groups": fresh(EG)}


def layouts(w):
    def columns(name):
        return w[name].reshape(-1, 128).T

    def up(a, shared):
        return np.concatenate([a.reshape(E // 2, 128, C), shared[None]]).transpose(0, 2, 1)

    down = np.concatenate([w["L1_ffn_ed_w"].reshape(E // 2, 2, C, 64).transpose(0, 1, 3, 2).reshape(E // 2, 128, C),
                           w["L1_ffn_sd_w"].T[None]])
    expert = 2 * np.arange(NT)[:, None] + np.arange(128)[None, :] // 64
    pick = (np.arange(128)[None, :, None] % E == expert[:, None, :]).astype(np.float32)
    experts = np.stack([up(w["L1_ffn_eg_w"], w["L1_ffn_sg_w"]), up(w["L1_ffn_eu_w"], w["L1_ffn_su_w"]),
                        down, pick], 2)
    out = {"bias_columns": np.concatenate([columns("L0_attn_b_attn"), columns("L1_xattn_bq"),
                                           columns("L1_xattn_bkv")], 1),
           "wide_wq_t": w["L0_xattn_Wq"].T, "wide_wkv_t": w["L0_xattn_Wkv"].T,
           "attn1_wqkv_t": w["L1_attn_w_qkv"].T, "attn1_wout_t": w["L1_attn_w_out"].T,
           "moe_gate_t": w["L1_ffn_gate_w"].T, "experts": experts}
    return {n: np.ascontiguousarray(a) for n, a in out.items()}


USED_AS_GIVEN = ("x", "ctx_1024", "L0_attn_W_attn", "L0_attn_W_proj", "L0_attn_b_proj", "L0_xattn_Wo",
                 "L0_xattn_ln1_w", "L0_xattn_ln1_b", "L0_xattn_ln2_w", "L0_xattn_ln2_b", "L0_ffn_w_up",
                 "L0_ffn_w_gate", "L0_ffn_w_down", "L1_attn_b_out", "L1_xattn_Wq", "L1_xattn_Wkv",
                 "L1_xattn_Wproj", "L1_xattn_bproj", "L1_ffn_gate_bias")


def kernel(**inputs):
    import concourse.bacc as bacc
    from concourse.bass_utils import run_bass_kernel_spmd

    nc = bacc.Bacc("TRN2", target_bir_lowering=False, num_devices=1)
    given = {n: np.ascontiguousarray(a) for n, a in inputs.items()}
    arrays = {n: given[n] for n in USED_AS_GIVEN}
    arrays.update(layouts(given))
    arrays.update(constants())
    arrays = {f"in_{n}": a for n, a in arrays.items()}
    io = {n[3:]: nc.dram_tensor(n, a.shape, mybir.dt.from_np(a.dtype), kind="ExternalInput").ap()
          for n, a in arrays.items()}
    out = nc.dram_tensor("out_dram", (B, T, C), F32, kind="ExternalOutput").ap()
    program(nc, io, out)
    return run_bass_kernel_spmd(nc, [arrays], core_ids=[0]).results[0]["out_dram"]
```
